# Optimizing a Trainium2 kernel written in Bass

```python
import numpy as np
import jax
import jax.numpy as jnp

def _softmax(x, axis=-1):
    return jax.nn.softmax(x, axis=axis)

def _gelu(x):
    return jax.nn.gelu(x, approximate=True)

def _silu(x):
    return jax.nn.silu(x)

def _sigmoid(x):
    return jax.nn.sigmoid(x)

def _layernorm(x, axis=-1, eps=1e-05):
    m = jnp.mean(x, axis=axis, keepdims=True)
    v = jnp.var(x, axis=axis, keepdims=True)
    return (x - m) / jnp.sqrt(v + eps)

def _scatter_add(tgt, idx, src, axis=0):
    return tgt.at[idx].add(src)

def _segment_sum(src, seg, n):
    return jax.ops.segment_sum(src, seg, n)
kernel_name = 'mk_recurrent_d2_jaxref_r4_604eae'

def setup_inputs(seed: int=0):
    np.random.seed(seed)
    _w = jnp.asarray

    def _L0_attn_setup():
        import jax, jax.numpy as jnp
        import numpy as np

        def _mamba_fwd(hidden_states, in_proj_w, conv_w, conv_b, x_proj_w, dt_proj_w, dt_proj_b, A_log, D_param, out_proj_w):
            Bsz, L, _ = hidden_states.shape
            d_inner = conv_w.shape[0]
            n = A_log.shape[1]
            r = dt_proj_w.shape[1]
            xz = jnp.einsum('bld,ed->ble', hidden_states, in_proj_w)
            x, z = (xz[..., :d_inner], xz[..., d_inner:])
            x_bdl = jnp.transpose(x, (0, 2, 1))
            kern = conv_w[:, None, :]
            xc = jax.lax.conv_general_dilated(x_bdl, kern, window_strides=(1,), padding=[(conv_w.shape[1] - 1, 0)], dimension_numbers=('NCH', 'OIH', 'NCH'), feature_group_count=d_inner)
            xc = xc + conv_b[None, :, None]
            xc = xc * jax.nn.sigmoid(xc)
            u = jnp.transpose(xc, (0, 2, 1))
            x_dbl = jnp.einsum('bld,ed->ble', u, x_proj_w)
            dt_lo = x_dbl[..., :r]
            B_ssm = x_dbl[..., r:r + n]
            C_ssm = x_dbl[..., r + n:]
            delta = jax.nn.softplus(jnp.einsum('blr,dr->bld', dt_lo, dt_proj_w) + dt_proj_b)
            A = -jnp.exp(A_log)

            def step(h, inp):
                d_t, u_t, b_t, c_t = inp
                dA = jnp.exp(d_t[..., None] * A)
                h = dA * h + (d_t * u_t)[..., None] * b_t[:, None, :]
                y_t = jnp.einsum('bdn,bn->bd', h, c_t)
                return (h, y_t)
            h0 = jnp.zeros((Bsz, d_inner, n), dtype=u.dtype)
            xs = (jnp.transpose(delta, (1, 0, 2)), jnp.transpose(u, (1, 0, 2)), jnp.transpose(B_ssm, (1, 0, 2)), jnp.transpose(C_ssm, (1, 0, 2)))
            _, ys = jax.lax.scan(step, h0, xs)
            y = jnp.transpose(ys, (1, 0, 2)) + u * D_param
            y = y * (z * jax.nn.sigmoid(z))
            return jnp.einsum('bld,ed->ble', y, out_proj_w)
        key = jax.random.key(seed)
        ks = jax.random.split(key, 10)
        B, L, D_MODEL = (2, 512, 256)
        D_INNER, N, W, R = (512, 16, 4, 64)
        s = 0.02
        return {'hidden_states': jax.random.normal(ks[0], (B, L, D_MODEL), jnp.float32), 'in_proj_w': jax.random.normal(ks[1], (2 * D_INNER, D_MODEL), jnp.float32) * s, 'conv_w': jax.random.normal(ks[2], (D_INNER, W), jnp.float32) * 0.2, 'conv_b': jax.random.normal(ks[3], (D_INNER,), jnp.float32) * 0.02, 'x_proj_w': jax.random.normal(ks[4], (R + 2 * N, D_INNER), jnp.float32) * s, 'dt_proj_w': jax.random.normal(ks[5], (D_INNER, R), jnp.float32) * R ** (-0.5), 'dt_proj_b': jnp.log(jnp.expm1(jnp.exp(jax.random.uniform(ks[6], (D_INNER,), jnp.float32, np.log(0.001), np.log(0.1)))) + 1e-20), 'A_log': jnp.log(jnp.broadcast_to(jnp.arange(1, N + 1, dtype=jnp.float32), (D_INNER, N))), 'D_param': jnp.ones((D_INNER,), jnp.float32), 'out_proj_w': jax.random.normal(ks[7], (D_MODEL, D_INNER), jnp.float32) * s}
    _L0_attn_in = _L0_attn_setup()

    def _L0_ffn_setup():
        import jax, jax.numpy as jnp
        import numpy as np
        DIM = 256
        DEPTH = 2
        HEADS = 8
        DIM_HEAD = 64
        WINDOW = 128
        INNER = HEADS * DIM_HEAD
        HID = int(DIM * 4 * 2 / 3)
        B, N = (2, 2048)
        QK_SCALE = 8.0

        def shift_token(t):
            t1, t2 = jnp.split(t, 2, axis=-1)
            t2 = jnp.pad(t2, ((0, 0), (1, 0), (0, 0)))[:, :-1]
            return jnp.concatenate([t1, t2], axis=-1)

        def l2norm(t):
            return t / jnp.clip(jnp.linalg.norm(t, axis=-1, keepdims=True), 1e-12)

        def rotate_half(x):
            x1, x2 = jnp.split(x, 2, axis=-1)
            return jnp.concatenate([-x2, x1], axis=-1)

        def rotary_xpos(q, k):
            n = q.shape[-2]
            half_idx = jnp.arange(0, DIM_HEAD, 2, dtype=jnp.float32)
            inv_freq = 1.0 / 10000.0 ** (half_idx / DIM_HEAD)
            t = jnp.arange(n, dtype=jnp.float32)
            freqs = t[:, None] * inv_freq[None, :]
            freqs = jnp.concatenate([freqs, freqs], axis=-1)
            base = (half_idx + 0.4 * DIM_HEAD) / (1.4 * DIM_HEAD)
            power = (t - n // 2) / float(WINDOW // 2)
            scale = base[None, :] ** power[:, None]
            scale = jnp.concatenate([scale, scale], axis=-1)
            cos, sin = (jnp.cos(freqs), jnp.sin(freqs))
            q = q * cos * scale + rotate_half(q) * sin * scale
            k = k * cos / scale + rotate_half(k) * sin / scale
            return (q, k)

        def local_attention(q, k, v):
            b, h, n, d = q.shape
            w = n // WINDOW
            bq = q.reshape(b, h, w, WINDOW, d) * QK_SCALE
            bk = k.reshape(b, h, w, WINDOW, d)
            bv = v.reshape(b, h, w, WINDOW, d)

            def look_around(t):
                p = jnp.pad(t, ((0, 0), (0, 0), (1, 0), (0, 0), (0, 0)))
                return jnp.concatenate([p[:, :, :w], p[:, :, 1:]], axis=3)
            bk, bv = (look_around(bk), look_around(bv))
            bt = jnp.arange(n).reshape(w, WINDOW)
            btp = jnp.pad(bt, ((1, 0), (0, 0)), constant_values=-1)
            btk = jnp.concatenate([btp[:w], btp[1:]], axis=1)
            sim = jnp.einsum('bhwid,bhwjd->bhwij', bq, bk)
            i = bt[:, :, None]
            j = btk[:, None, :]
            mask = (i < j) | (i > j + WINDOW) | (j == -1)
            sim = jnp.where(mask, -jnp.finfo(sim.dtype).max, sim)
            attn = jax.nn.softmax(sim, axis=-1)
            out = jnp.einsum('bhwij,bhwjd->bhwid', attn, bv)
            return out.reshape(b, h, n, d)

        def _layer(x, wqkv, qs, ksc, wo, lg, lb, w1, b1, w2, b2):
            b, n, _ = x.shape
            h = shift_token(x)
            qkv = h @ wqkv
            q, k, v = jnp.split(qkv, 3, axis=-1)
            to_heads = lambda t: t.reshape(b, n, HEADS, DIM_HEAD).transpose(0, 2, 1, 3)
            q, k, v = (to_heads(q), to_heads(k), to_heads(v))
            q = l2norm(q) * qs
            k = l2norm(k) * ksc
            q, k = rotary_xpos(q, k)
            o = local_attention(q, k, v)
            o = o.transpose(0, 2, 1, 3).reshape(b, n, INNER)
            x = x + o @ wo
            h = shift_token(x)
            mu = h.mean(-1, keepdims=True)
            var = h.var(-1, keepdims=True)
            h = (h - mu) / jnp.sqrt(var + 1e-05) * lg + lb
            h = h @ w1 + b1
            a, g = jnp.split(h, 2, axis=-1)
            h = a * jax.nn.gelu(g, approximate=False)
            x = x + h @ w2 + b2
            return x
        key = jax.random.key(seed)
        ks = jax.random.split(key, 6)
        return {'x': jax.random.normal(ks[0], (B, N, DIM), jnp.float32), 'wqkv': jax.random.normal(ks[1], (DEPTH, DIM, 3 * INNER), jnp.float32) * 0.02, 'q_scale': jnp.ones((DEPTH, DIM_HEAD), jnp.float32), 'k_scale': jnp.ones((DEPTH, DIM_HEAD), jnp.float32), 'wo': jax.random.normal(ks[2], (DEPTH, INNER, DIM), jnp.float32) * 0.02, 'ln_g': jnp.ones((DEPTH, DIM), jnp.float32), 'ln_b': jnp.zeros((DEPTH, DIM), jnp.float32), 'w1': jax.random.normal(ks[3], (DEPTH, DIM, 2 * HID), jnp.float32) * 0.02, 'b1': jnp.zeros((DEPTH, 2 * HID), jnp.float32), 'w2': jax.random.normal(ks[4], (DEPTH, HID, DIM), jnp.float32) * 0.02, 'b2': jnp.zeros((DEPTH, DIM), jnp.float32)}
    _L0_ffn_in = _L0_ffn_setup()

    def _L1_attn_setup():
        import jax, jax.numpy as jnp
        import numpy as np
        HEADS = 16
        THETA = 10000.0

        def _rope(x):
            b, n, d = x.shape
            half = d // 2
            inv_freq = 1.0 / THETA ** (jnp.arange(0, d, 2, dtype=jnp.float32) / d)
            ang = jnp.arange(n, dtype=jnp.float32)[:, None] * inv_freq
            cos, sin = (jnp.cos(ang), jnp.sin(ang))
            xp = x.reshape(b, n, half, 2)
            x1, x2 = (xp[..., 0], xp[..., 1])
            out = jnp.stack([x1 * cos - x2 * sin, x2 * cos + x1 * sin], axis=-1)
            return out.reshape(b, n, d)
        key = jax.random.key(seed)
        ks = jax.random.split(key, 8)
        B, N, C = (8, 512, 256)
        s = C ** (-0.5)
        return {'x': jax.random.normal(ks[0], (B, N, C), jnp.float32), 'Wq': jax.random.normal(ks[1], (C, C), jnp.float32) * s, 'bq': jax.random.normal(ks[2], (C,), jnp.float32) * 0.01, 'Wk': jax.random.normal(ks[3], (C, C), jnp.float32) * s, 'bk': jax.random.normal(ks[4], (C,), jnp.float32) * 0.01, 'Wv': jax.random.normal(ks[5], (C, C), jnp.float32) * s, 'bv': jax.random.normal(ks[6], (C,), jnp.float32) * 0.01, 'gamma': jnp.ones((C,), jnp.float32), 'beta': jnp.zeros((C,), jnp.float32)}
    _L1_attn_in = _L1_attn_setup()

    def _L1_ffn_setup():
        import jax, jax.numpy as jnp
        import numpy as np
        E = 64
        K = 6
        CAP = 128
        ROUTE_SCALE = 1.0
        key = jax.random.key(seed)
        ks = jax.random.split(key, 9)
        B, S, D, I = (2, 256, 256, 176)
        SI = 2 * I
        s = 0.02
        return {'x': jax.random.normal(ks[0], (B, S, D), jnp.float32), 'gate_w': jax.random.normal(ks[1], (E, D), jnp.float32) * s, 'gate_b': jnp.zeros((E,), jnp.float32), 'w1': jax.random.normal(ks[2], (E, I, D), jnp.float32) * s, 'w2': jax.random.normal(ks[3], (E, D, I), jnp.float32) * s, 'w3': jax.random.normal(ks[4], (E, I, D), jnp.float32) * s, 'ws1': jax.random.normal(ks[5], (SI, D), jnp.float32) * s, 'ws2': jax.random.normal(ks[6], (D, SI), jnp.float32) * s, 'ws3': jax.random.normal(ks[7], (SI, D), jnp.float32) * s}
    _L1_ffn_in = _L1_ffn_setup()
    _d = {'L0_attn_hidden_states': _L0_attn_in['hidden_states'], 'L0_attn_in_proj_w': _L0_attn_in['in_proj_w'], 'L0_attn_conv_w': _L0_attn_in['conv_w'], 'L0_attn_conv_b': _L0_attn_in['conv_b'], 'L0_attn_x_proj_w': _L0_attn_in['x_proj_w'], 'L0_attn_dt_proj_w': _L0_attn_in['dt_proj_w'], 'L0_attn_dt_proj_b': _L0_attn_in['dt_proj_b'], 'L0_attn_A_log': _L0_attn_in['A_log'], 'L0_attn_D_param': _L0_attn_in['D_param'], 'L0_attn_out_proj_w': _L0_attn_in['out_proj_w'], 'L0_ffn_wqkv': _L0_ffn_in['wqkv'], 'L0_ffn_q_scale': _L0_ffn_in['q_scale'], 'L0_ffn_k_scale': _L0_ffn_in['k_scale'], 'L0_ffn_wo': _L0_ffn_in['wo'], 'L0_ffn_ln_g': _L0_ffn_in['ln_g'], 'L0_ffn_ln_b': _L0_ffn_in['ln_b'], 'L0_ffn_w1': _L0_ffn_in['w1'], 'L0_ffn_b1': _L0_ffn_in['b1'], 'L0_ffn_w2': _L0_ffn_in['w2'], 'L0_ffn_b2': _L0_ffn_in['b2'], 'L1_attn_Wq': _L1_attn_in['Wq'], 'L1_attn_bq': _L1_attn_in['bq'], 'L1_attn_Wk': _L1_attn_in['Wk'], 'L1_attn_bk': _L1_attn_in['bk'], 'L1_attn_Wv': _L1_attn_in['Wv'], 'L1_attn_bv': _L1_attn_in['bv'], 'L1_attn_gamma': _L1_attn_in['gamma'], 'L1_attn_beta': _L1_attn_in['beta'], 'L1_ffn_gate_w': _L1_ffn_in['gate_w'], 'L1_ffn_gate_b': _L1_ffn_in['gate_b'], 'L1_ffn_w1': _L1_ffn_in['w1'], 'L1_ffn_w2': _L1_ffn_in['w2'], 'L1_ffn_w3': _L1_ffn_in['w3'], 'L1_ffn_ws1': _L1_ffn_in['ws1'], 'L1_ffn_ws2': _L1_ffn_in['ws2'], 'L1_ffn_ws3': _L1_ffn_in['ws3']}
    _x0 = _d['L0_attn_hidden_states']
    _d['L0_attn_hidden_states'] = jax.random.normal(jax.random.fold_in(jax.random.key(seed), 1), (4, 2048, 256), dtype=_x0.dtype)
    del _x0
    return _d

def reference(L0_attn_hidden_states, L0_attn_in_proj_w, L0_attn_conv_w, L0_attn_conv_b, L0_attn_x_proj_w, L0_attn_dt_proj_w, L0_attn_dt_proj_b, L0_attn_A_log, L0_attn_D_param, L0_attn_out_proj_w, L0_ffn_wqkv, L0_ffn_q_scale, L0_ffn_k_scale, L0_ffn_wo, L0_ffn_ln_g, L0_ffn_ln_b, L0_ffn_w1, L0_ffn_b1, L0_ffn_w2, L0_ffn_b2, L1_attn_Wq, L1_attn_bq, L1_attn_Wk, L1_attn_bk, L1_attn_Wv, L1_attn_bv, L1_attn_gamma, L1_attn_beta, L1_ffn_gate_w, L1_ffn_gate_b, L1_ffn_w1, L1_ffn_w2, L1_ffn_w3, L1_ffn_ws1, L1_ffn_ws2, L1_ffn_ws3):

    def _L0_attn_ref(hidden_states, in_proj_w, conv_w, conv_b, x_proj_w, dt_proj_w, dt_proj_b, A_log, D_param, out_proj_w):
        import jax, jax.numpy as jnp
        import numpy as np

        def _mamba_fwd(hidden_states, in_proj_w, conv_w, conv_b, x_proj_w, dt_proj_w, dt_proj_b, A_log, D_param, out_proj_w):
            Bsz, L, _ = hidden_states.shape
            d_inner = conv_w.shape[0]
            n = A_log.shape[1]
            r = dt_proj_w.shape[1]
            xz = jnp.einsum('bld,ed->ble', hidden_states, in_proj_w)
            x, z = (xz[..., :d_inner], xz[..., d_inner:])
            x_bdl = jnp.transpose(x, (0, 2, 1))
            kern = conv_w[:, None, :]
            xc = jax.lax.conv_general_dilated(x_bdl, kern, window_strides=(1,), padding=[(conv_w.shape[1] - 1, 0)], dimension_numbers=('NCH', 'OIH', 'NCH'), feature_group_count=d_inner)
            xc = xc + conv_b[None, :, None]
            xc = xc * jax.nn.sigmoid(xc)
            u = jnp.transpose(xc, (0, 2, 1))
            x_dbl = jnp.einsum('bld,ed->ble', u, x_proj_w)
            dt_lo = x_dbl[..., :r]
            B_ssm = x_dbl[..., r:r + n]
            C_ssm = x_dbl[..., r + n:]
            delta = jax.nn.softplus(jnp.einsum('blr,dr->bld', dt_lo, dt_proj_w) + dt_proj_b)
            A = -jnp.exp(A_log)

            def step(h, inp):
                d_t, u_t, b_t, c_t = inp
                dA = jnp.exp(d_t[..., None] * A)
                h = dA * h + (d_t * u_t)[..., None] * b_t[:, None, :]
                y_t = jnp.einsum('bdn,bn->bd', h, c_t)
                return (h, y_t)
            h0 = jnp.zeros((Bsz, d_inner, n), dtype=u.dtype)
            xs = (jnp.transpose(delta, (1, 0, 2)), jnp.transpose(u, (1, 0, 2)), jnp.transpose(B_ssm, (1, 0, 2)), jnp.transpose(C_ssm, (1, 0, 2)))
            _, ys = jax.lax.scan(step, h0, xs)
            y = jnp.transpose(ys, (1, 0, 2)) + u * D_param
            y = y * (z * jax.nn.sigmoid(z))
            return jnp.einsum('bld,ed->ble', y, out_proj_w)
        return _mamba_fwd(hidden_states, in_proj_w, conv_w, conv_b, x_proj_w, dt_proj_w, dt_proj_b, A_log, D_param, out_proj_w)

    def _L0_ffn_ref(x, wqkv, q_scale, k_scale, wo, ln_g, ln_b, w1, b1, w2, b2):
        import jax, jax.numpy as jnp
        import numpy as np
        DIM = 256
        DEPTH = 2
        HEADS = 8
        DIM_HEAD = 64
        WINDOW = 128
        INNER = HEADS * DIM_HEAD
        HID = int(DIM * 4 * 2 / 3)
        B, N = (2, 2048)
        QK_SCALE = 8.0

        def shift_token(t):
            t1, t2 = jnp.split(t, 2, axis=-1)
            t2 = jnp.pad(t2, ((0, 0), (1, 0), (0, 0)))[:, :-1]
            return jnp.concatenate([t1, t2], axis=-1)

        def l2norm(t):
            return t / jnp.clip(jnp.linalg.norm(t, axis=-1, keepdims=True), 1e-12)

        def rotate_half(x):
            x1, x2 = jnp.split(x, 2, axis=-1)
            return jnp.concatenate([-x2, x1], axis=-1)

        def rotary_xpos(q, k):
            n = q.shape[-2]
            half_idx = jnp.arange(0, DIM_HEAD, 2, dtype=jnp.float32)
            inv_freq = 1.0 / 10000.0 ** (half_idx / DIM_HEAD)
            t = jnp.arange(n, dtype=jnp.float32)
            freqs = t[:, None] * inv_freq[None, :]
            freqs = jnp.concatenate([freqs, freqs], axis=-1)
            base = (half_idx + 0.4 * DIM_HEAD) / (1.4 * DIM_HEAD)
            power = (t - n // 2) / float(WINDOW // 2)
            scale = base[None, :] ** power[:, None]
            scale = jnp.concatenate([scale, scale], axis=-1)
            cos, sin = (jnp.cos(freqs), jnp.sin(freqs))
            q = q * cos * scale + rotate_half(q) * sin * scale
            k = k * cos / scale + rotate_half(k) * sin / scale
            return (q, k)

        def local_attention(q, k, v):
            b, h, n, d = q.shape
            w = n // WINDOW
            bq = q.reshape(b, h, w, WINDOW, d) * QK_SCALE
            bk = k.reshape(b, h, w, WINDOW, d)
            bv = v.reshape(b, h, w, WINDOW, d)

            def look_around(t):
                p = jnp.pad(t, ((0, 0), (0, 0), (1, 0), (0, 0), (0, 0)))
                return jnp.concatenate([p[:, :, :w], p[:, :, 1:]], axis=3)
            bk, bv = (look_around(bk), look_around(bv))
            bt = jnp.arange(n).reshape(w, WINDOW)
            btp = jnp.pad(bt, ((1, 0), (0, 0)), constant_values=-1)
            btk = jnp.concatenate([btp[:w], btp[1:]], axis=1)
            sim = jnp.einsum('bhwid,bhwjd->bhwij', bq, bk)
            i = bt[:, :, None]
            j = btk[:, None, :]
            mask = (i < j) | (i > j + WINDOW) | (j == -1)
            sim = jnp.where(mask, -jnp.finfo(sim.dtype).max, sim)
            attn = jax.nn.softmax(sim, axis=-1)
            out = jnp.einsum('bhwij,bhwjd->bhwid', attn, bv)
            return out.reshape(b, h, n, d)

        def _layer(x, wqkv, qs, ksc, wo, lg, lb, w1, b1, w2, b2):
            b, n, _ = x.shape
            h = shift_token(x)
            qkv = h @ wqkv
            q, k, v = jnp.split(qkv, 3, axis=-1)
            to_heads = lambda t: t.reshape(b, n, HEADS, DIM_HEAD).transpose(0, 2, 1, 3)
            q, k, v = (to_heads(q), to_heads(k), to_heads(v))
            q = l2norm(q) * qs
            k = l2norm(k) * ksc
            q, k = rotary_xpos(q, k)
            o = local_attention(q, k, v)
            o = o.transpose(0, 2, 1, 3).reshape(b, n, INNER)
            x = x + o @ wo
            h = shift_token(x)
            mu = h.mean(-1, keepdims=True)
            var = h.var(-1, keepdims=True)
            h = (h - mu) / jnp.sqrt(var + 1e-05) * lg + lb
            h = h @ w1 + b1
            a, g = jnp.split(h, 2, axis=-1)
            h = a * jax.nn.gelu(g, approximate=False)
            x = x + h @ w2 + b2
            return x
        for l in range(DEPTH):
            x = _layer(x, wqkv[l], q_scale[l], k_scale[l], wo[l], ln_g[l], ln_b[l], w1[l], b1[l], w2[l], b2[l])
        return x

    def _L1_attn_ref(x, Wq, bq, Wk, bk, Wv, bv, gamma, beta):
        import jax, jax.numpy as jnp
        import numpy as np
        HEADS = 16
        THETA = 10000.0

        def _rope(x):
            b, n, d = x.shape
            half = d // 2
            inv_freq = 1.0 / THETA ** (jnp.arange(0, d, 2, dtype=jnp.float32) / d)
            ang = jnp.arange(n, dtype=jnp.float32)[:, None] * inv_freq
            cos, sin = (jnp.cos(ang), jnp.sin(ang))
            xp = x.reshape(b, n, half, 2)
            x1, x2 = (xp[..., 0], xp[..., 1])
            out = jnp.stack([x1 * cos - x2 * sin, x2 * cos + x1 * sin], axis=-1)
            return out.reshape(b, n, d)
        b, n, c = x.shape
        h = HEADS
        d = c // h
        gelu = lambda t: jax.nn.gelu(t, approximate=False)
        q = gelu(x @ Wq.T + bq) + 0.21
        k = gelu(x @ Wk.T + bk) + 0.21
        v = x @ Wv.T + bv
        q_r = _rope(q)
        k_r = _rope(k)
        split = lambda t: t.reshape(b, n, h, d).transpose(0, 2, 1, 3)
        qh, kh, vh, qrh, krh = (split(q), split(k), split(v), split(q_r), split(k_r))
        z = 1.0 / (jnp.einsum('bhnd,bhd->bhn', qh, kh.mean(axis=2)) + 1e-06)
        scale = n ** (-0.5)
        kv = jnp.einsum('bhnd,bhne->bhde', krh * scale, vh * scale)
        out = jnp.einsum('bhnd,bhde->bhne', qrh, kv) * z[..., None]
        out = out.transpose(0, 2, 1, 3).reshape(b, n, c)
        res = out + x
        mu = res.mean(-1, keepdims=True)
        var = res.var(-1, keepdims=True)
        return (res - mu) / jnp.sqrt(var + 1e-12) * gamma + beta

    def _L1_ffn_ref(x, gate_w, gate_b, w1, w2, w3, ws1, ws2, ws3):
        import jax, jax.numpy as jnp
        import numpy as np
        E = 64
        K = 6
        CAP = 128
        ROUTE_SCALE = 1.0
        shape = x.shape
        D = shape[-1]
        xf = x.reshape(-1, D)
        T = xf.shape[0]
        scores = jax.nn.softmax(xf @ gate_w.T, axis=-1)
        _, idx = jax.lax.top_k(scores + gate_b, K)
        weights = jnp.take_along_axis(scores, idx, axis=1) * ROUTE_SCALE
        flat_e = idx.reshape(-1)
        order = jnp.argsort(flat_e)
        se = flat_e[order]
        counts = jnp.bincount(flat_e, length=E)
        starts = jnp.cumsum(counts) - counts
        pos = jnp.arange(T * K) - starts[se]
        tok = order // K
        xb = jnp.zeros((E, CAP, D), xf.dtype).at[se, pos].set(xf[tok], mode='drop')
        h = jax.nn.silu(jnp.einsum('ecd,eid->eci', xb, w1)) * jnp.einsum('ecd,eid->eci', xb, w3)
        yb = jnp.einsum('eci,edi->ecd', h, w2)
        valid = (pos < CAP).astype(xf.dtype)
        contrib = yb[se, jnp.minimum(pos, CAP - 1)]
        wf = weights.reshape(-1)[order] * valid
        y = jnp.zeros_like(xf).at[tok].add(contrib * wf[:, None])
        z = jax.nn.silu(xf @ ws1.T) * (xf @ ws3.T) @ ws2.T
        return (y + z).reshape(shape)
    x = L0_attn_hidden_states
    xn = _layernorm(x, axis=-1)
    s = _L0_attn_ref(xn, L0_attn_in_proj_w, L0_attn_conv_w, L0_attn_conv_b, L0_attn_x_proj_w, L0_attn_dt_proj_w, L0_attn_dt_proj_b, L0_attn_A_log, L0_attn_D_param, L0_attn_out_proj_w)
    g = _silu(_L0_ffn_ref(xn, L0_ffn_wqkv, L0_ffn_q_scale, L0_ffn_k_scale, L0_ffn_wo, L0_ffn_ln_g, L0_ffn_ln_b, L0_ffn_w1, L0_ffn_b1, L0_ffn_w2, L0_ffn_b2))
    x = x + s * g
    xn = _layernorm(x, axis=-1)
    s = _L1_attn_ref(xn, L1_attn_Wq, L1_attn_bq, L1_attn_Wk, L1_attn_bk, L1_attn_Wv, L1_attn_bv, L1_attn_gamma, L1_attn_beta)
    g = _silu(_L1_ffn_ref(xn, L1_ffn_gate_w, L1_ffn_gate_b, L1_ffn_w1, L1_ffn_w2, L1_ffn_w3, L1_ffn_ws1, L1_ffn_ws2, L1_ffn_ws3))
    x = x + s * g
    return x

_drawn_inputs = setup_inputs


def setup_inputs(seed=0):
    import zlib

    import numpy as np

    out = dict(_drawn_inputs(seed))
    spreads = {'L0_attn_D_param': (1.0, 0.2),
     'L0_ffn_q_scale': (1.0, 0.2),
     'L0_ffn_k_scale': (1.0, 0.2),
     'L0_ffn_ln_g': (1.0, 0.2),
     'L0_ffn_ln_b': (0.0, 0.1),
     'L0_ffn_b1': (0.0, 0.1),
     'L0_ffn_b2': (0.0, 0.1),
     'L1_attn_gamma': (1.0, 0.2),
     'L1_attn_beta': (0.0, 0.1),
     'L1_ffn_gate_b': (0.0, 0.1)}
    factors = {}
    for name, (base, spread) in spreads.items():
        noise = np.random.default_rng([zlib.crc32(name.encode()), seed]).standard_normal(out[name].shape)
        drawn = base * np.exp(spread * noise) if base else spread * noise
        out[name] = jnp.asarray(drawn.astype(out[name].dtype))
    for name, factor in factors.items():
        out[name] = (out[name] * factor).astype(out[name].dtype)
    return out
```

```python
from contextlib import ExitStack

import numpy as np

import concourse.bass as bass
from concourse import mybir
from concourse.alu_op_type import AluOpType as ALU

F32 = mybir.dt.float32
BF16 = mybir.dt.bfloat16
I32 = mybir.dt.int32
ACT = mybir.ActivationFunctionType
AX = mybir.AxisListType

P = 128
B, L, D = 4, 2048, 256
T = B * L
NT = T // P
WPB = L // P
CH = 512
CT = CH // P
NC = T // CH
DH = D // P
NL = 2
H, DK = 8, 64
INNER = H * DK
HID = int(D * 4 * 2 / 3)
NJ = -(-HID // P)
QK_SCALE = 8.0
TRANSPOSED = ("L0_attn_in_proj_w", "L0_attn_x_proj_w", "L0_attn_dt_proj_w", "L0_attn_out_proj_w", "L1_attn_Wq",
              "L1_attn_Wk", "L1_attn_Wv", "L1_ffn_gate_w", "L1_ffn_w1", "L1_ffn_w2", "L1_ffn_w3", "L1_ffn_ws1",
              "L1_ffn_ws2", "L1_ffn_ws3")
NEG = -1.0e30

SLOTS = 80
NS = 5


def tile_slot(t):
    return t + (t + WPB) // WPB + 1


def chunk_slot(c):
    return c * CT + c // (WPB // CT) + 2


class Steps:

    def __init__(self, nc, ctx, book, gate, name, lenient=False, scrap=None):
        self.nc, self.name, self.n, self.lenient = nc, name, 0, lenient
        self.ctx, self.free = ctx, gate["free"]
        self.book = book.setdefault(name, {"order": {}, "per_pass": {}, "soft": set()})
        self.count, self.sems, self.waited = {}, {}, {}
        self.gate = gate
        self.base = {}
        for who, k in self.book["per_pass"].items():
            kind = who if who in self.book["soft"] else who.split("_")[0]
            if self.free.get(kind):
                self.sems[who], self.base[who] = self.free[kind].pop()
            else:
                self.sems[who], self.base[who] = ctx.enter_context(nc.semaphore(f"{name}_{who}")), 0
            if who in self.book["soft"]:
                row = len([w for w in self.sems if w in self.book["soft"]])
                nc.gpsimd.dma_start(scrap[0][row - 1:row, :], scrap[1]).then_inc(self.sems[who], 16)
            else:
                nc.sync.sem_inc(self.sems[who], k)
        if self.sems:
            for eng in (nc.tensor, nc.scalar, nc.vector, nc.gpsimd):
                for who, k in self.book["per_pass"].items():
                    eng.wait_ge(self.sems[who], self.base[who] + (16 if who in self.book["soft"] else k))

    def begin(self, n):
        self.n, self.count, self.waited = n, {}, {}

    def _who(self, eng):
        nc = self.nc
        return {id(nc.tensor): "pe", id(nc.scalar): "act", id(nc.vector): "dve", id(nc.gpsimd): "pool",
                id(nc.sync): "sp"}[id(eng)]

    def step(self, who, ins, name):
        o = self.count[who] = self.count.get(who, 0) + 1
        assert name not in self.book["order"] or self.book["order"][name] == (who, o), name
        self.book["order"][name] = (who, o)
        if who in self.sems:
            ins.then_inc(self.sems[who], 1)

    def load(self, ins, name, soft=False):
        who = "dma_" + name
        if soft:
            self.book["soft"].add(who)
        self.count[who] = self.count.get(who, 0) + 16
        self.book["order"][name] = (who, self.count[who])
        if who in self.sems:
            ins.then_inc(self.sems[who], 16)

    def wait(self, eng, name, back=0, alone=False):
        if not self.sems or (self.lenient and name not in self.book["order"]):
            return
        who, o = self.book["order"][name]
        k = self.book["per_pass"][who]
        at = o - back * k
        key = (self._who(eng), who)
        if self.waited.get(key, -10**9) >= at:
            return
        self.waited[key] = at
        if who in self.book["soft"]:
            assert at in (0, k), name
            eng.wait_ge(self.sems[who], self.n * k + at + 16)
        else:
            eng.wait_ge(self.sems[who], (self.n + 1) * k + (self.base[who] + at))
        if alone or eng is self.nc.gpsimd or eng is self.nc.sync:
            eng.sem_inc(self.gate[self._who(eng)], 1)

    def close(self):
        for who, k in self.count.items():
            assert self.book["per_pass"].get(who, k) == k, (self.name, who)
            self.book["per_pass"][who] = k

    def done(self, passes, engines=None):
        nc = self.nc
        for eng in engines or (nc.tensor, nc.scalar, nc.vector, nc.gpsimd, nc.sync):
            for who, sem in self.sems.items():
                k = self.book["per_pass"][who]
                eng.wait_ge(sem, passes * k + (16 if who in self.book["soft"] else k + self.base[who]))
                if not isinstance(passes, int):
                    eng.sem_inc(self.gate[self._who(eng)], 1)
        if isinstance(passes, int):
            for who, sem in self.sems.items():
                if who not in self.book["soft"]:
                    end = self.base[who] + (passes + 1) * self.book["per_pass"][who]
                    self.free.setdefault(who.split("_")[0], []).append((sem, end))


def program(nc, A, out, book):
    pe, act, dve, pool, sp = nc.tensor, nc.scalar, nc.vector, nc.gpsimd, nc.sync
    top = ExitStack()
    xs = nc.dram_tensor("stream", [NS * SLOTS * P, D], F32).ap()
    tabs = nc.dram_tensor("rotary_tables", [NL * WPB * P, 4 * DK], F32).ap()
    scrap = nc.dram_tensor("scrap", [8, 256], F32).ap()
    out_rows = out.rearrange("b t d -> (b t) d")

    def sb(ctx, name, shape, dt=F32):
        return ctx.enter_context(nc.sbuf_tensor(name, shape, dt))

    def ps(ctx, name, cols):
        return ctx.enter_context(nc.psum_tensor(name, [P, cols], F32))

    def rows(stage, slot, n, shift=0):
        return xs[bass.ds((stage * SLOTS + slot) * P + shift, n), :]

    with top:
        gate = {w: top.enter_context(nc.semaphore("gate_" + w)) for w in ("pe", "act", "dve", "pool", "sp")}
        gate["free"] = {}
        ident = sb(top, "ident", [P, P])
        identb = sb(top, "identb", [P, P], BF16)
        mhalf = sb(top, "mhalf", [P, 2 * H])
        zrow = sb(top, "zrow", [P, D])

        with ExitStack() as ctx:
            S = Steps(nc, top, book, gate, "setup")
            base = sb(ctx, "base_tab", [P, WPB, 4 * DK])
            fac = sb(ctx, "scale_fac", [P, NL, 4 * DK])
            ltab = sb(ctx, "layer_tab", [P, NL, WPB, 4 * DK])
            S.step("pool", pool.memset(ident[:], 0.0), "id0")
            S.step("pool", pool.memset(identb[:], 0.0), "idb0")
            S.step("pool", pool.memset(mhalf[:], -0.5), "mhalf")
            S.step("pool", pool.memset(zrow[:], 0.0), "zrow")
            S.wait(pool, "idb0")
            for m, nm in ((ident, "id1"), (identb, "idb1")):
                S.step("pool", pool.affine_select(out=m[:], in_=m[:], compare_op=ALU.not_equal, fill=1.0, base=0,
                                                  pattern=[[-1, P]], channel_multiplier=1), nm)
            S.load(sp.dma_start(base[:], A["c_rotary"].rearrange("w p c -> p w c")), "base")
            hk = DK // 2
            for l in range(NL):
                for q, nm in enumerate(("L0_ffn_q_scale", "L0_ffn_k_scale")):
                    s = A[nm][l:l + 1, :]
                    o = 2 * q * DK
                    for dst, src in ((o, s), (o + DK, s[:, hk:DK]), (o + DK + hk, s[:, 0:hk])):
                        w = src.shape[1]
                        S.load(sp.dma_start(fac[:, l, dst:dst + w], src.to_broadcast([P, w])), "fac")
            S.wait(dve, "base")
            S.wait(dve, "fac")
            for l in range(NL):
                S.step("dve", dve.tensor_tensor(out=ltab[:, l], in0=base[:],
                                                in1=fac[:, l:l + 1, :].to_broadcast([P, WPB, 4 * DK]), op=ALU.mult),
                       f"ltab{l}")
            S.wait(sp, "zrow")
            for s in range(NS - 1):
                for k in (0, 1, 18, 35, 52, *range(69, SLOTS)):
                    S.load(sp.dma_start(rows(s, k, P), zrow[:]), "zeros")
            S.wait(sp, f"ltab{NL - 1}")
            for l in range(NL):
                S.load(sp.dma_start(tabs[l * L:(l + 1) * L, :].rearrange("(w p) c -> p w c", p=P),
                                   ltab[:, l]), "tabs")
            S.close()
            S.done(1)

        x_in = A["L0_attn_hidden_states"].rearrange("b t d -> (b t) d")
        with ExitStack() as ctx:
            x = [sb(ctx, f"ln_x{u}", [P, CT, D]) for u in range(2)]
            y = [sb(ctx, f"ln_y{u}", [P, CT, D]) for u in range(2)]
            st = [sb(ctx, f"ln_st{u}", [P, CT, 6]) for u in range(2)]
            mv = [sb(ctx, f"ln_mv{u}", [P, CT, 2]) for u in range(2)]
            rs = [sb(ctx, f"ln_rs{u}", [P, CT]) for u in range(2)]
            S = Steps(nc, top, book, gate, "norm")
            with nc.Fori(0, NC // 2) as i:
                S.begin(i)
                for u in range(2):
                    c = i * 2 + u
                    S.wait(sp, f"norm{u}", back=1)
                    S.load(sp.dma_start(x[u][:], x_in[bass.ds(c * CH, CH), :].rearrange("(p j) d -> p j d", j=CT)),
                           f"x{u}")
                for u in range(2):
                    S.wait(dve, f"x{u}")
                    for j in range(CT):
                        S.step("dve", dve.bn_stats(st[u][:, j], x[u][:, j]), f"st{u}{j}")
                    for j in range(CT):
                        S.wait(dve, f"st{u}{j}", alone=True)
                        S.step("dve", dve.bn_aggr(mv[u][:, j], st[u][:, j]), f"mv{u}{j}")
                    S.wait(dve, f"mv{u}{CT - 1}")
                    S.step("dve", dve.tensor_scalar(rs[u][:], mv[u][:, :, 1], 1e-5, None, ALU.add), f"var{u}")
                    S.wait(pool, f"var{u}")
                    S.step("pool", pool.tensor_tensor(out=rs[u][:], in0=rs[u][:], in1=mhalf[:, 0:CT], op=ALU.pow),
                           f"rs{u}")
                for u in range(2):
                    S.wait(dve, f"rs{u}")
                    S.wait(dve, f"y{u}", back=1)
                    for j in range(CT):
                        ins = dve.tensor_scalar(y[u][:, j], x[u][:, j], mv[u][:, j, 0:1], rs[u][:, j:j + 1],
                                                ALU.subtract, ALU.mult)
                    S.step("dve", ins, f"norm{u}")
                for u in range(2):
                    c = i * 2 + u
                    S.wait(sp, f"norm{u}")
                    S.load(sp.dma_start(rows(0, chunk_slot(c), CH).rearrange("(p j) d -> p j d", j=CT), y[u][:]),
                           f"y{u}")
                S.close()
            S.done(NC // 2)


        RING = 4
        SA0 = Steps(nc, top, book, gate, "attn_first", lenient=True)
        SA = Steps(nc, top, book, gate, "attn")
        SA1 = Steps(nc, top, book, gate, "attn_last", lenient=True)
        hk = DK // 2

        def layer_rows(name, l, n):
            return A[name].rearrange("l r n -> (l r) n")[bass.ds(l * n, n), :]

        def attention(l, actx):
            wqkv = sb(actx, "wqkv", [P, DH, 3 * INNER])
            wo = sb(actx, "wo", [P, INNER // P, D])
            hx = [sb(actx, f"hx{k}", [P, D]) for k in range(2)]
            tab = [sb(actx, f"tab{k}", [P, 4, DK]) for k in range(2)]
            msk = [sb(actx, f"msk{k}", [P, 2 * P], BF16) for k in range(2)]
            res = [sb(actx, f"res{k}", [P, D]) for k in range(2)]
            xo = [sb(actx, f"xo{k}", [P, D]) for k in range(2)]
            hT = sb(actx, "hT", [P, DH, P])
            sq = sb(actx, "sq", [P, 2 * INNER])
            n2 = [sb(actx, f"n2{k}", [P, 2 * H]) for k in range(2)]
            rn = [sb(actx, f"rn{k}", [P, 2 * H]) for k in range(2)]
            qsc = [sb(actx, f"qsc{u}", [P, H]) for u in range(RING)]
            rc = sb(actx, "rot_cos", [P, 2 * INNER])
            rsn = sb(actx, "rot_sin", [P, 2 * INNER])
            qkT = [sb(actx, f"qkT{u}", [P, 2 * INNER]) for u in range(RING)]
            vv = [sb(actx, f"v{u}", [P, INNER]) for u in range(RING)]
            prob = sb(actx, "prob", [P, H // 2, 2, P])
            probT = sb(actx, "probT", [P, H // 2, 2, P])
            mx = sb(actx, "mx", [P, H])
            nb = sb(actx, "nb", [P, H])
            den = [sb(actx, f"den{k}", [P, H]) for k in range(2)]
            rden = sb(actx, "rden", [P, H])
            o_sb = sb(actx, "o_sb", [P, INNER])
            oT = sb(actx, "oT", [P, INNER])
            p_qk = ps(actx, "p_qk", 2 * INNER)
            p_v = ps(actx, "p_v", INNER)
            p_s = ps(actx, "p_s", 2 * INNER)
            p_t = ps(actx, "p_t", 2 * INNER)
            p_o = ps(actx, "p_o", INNER)

            def V(S, eng, name, u, d=0):
                v = u - d
                S.wait(eng, f"{name}{v % RING}", back=1 if v < 0 else 0)

            def load_tile(S, u, t, l):
                k = (u + 1) % 2
                slot = tile_slot(t)
                S.load(sp.dma_start(hx[k][:, 0:P], rows(2 * l, slot, P)[:, 0:P]), f"hx{u}")
                S.load(sp.dma_start(hx[k][:, P:D], rows(2 * l, slot, P, -1)[:, P:D]), f"hx{u}")
                S.load(sp.dma_start(tab[k][:].rearrange("p a c -> p (a c)"),
                                    tabs[bass.ds((l * WPB + t % WPB) * P, P), :]), f"tab{u}")

            def load_mask(S, u, t):
                S.load(sp.dma_start(msk[(u + 1) % 2][:],
                                    A["c_mask"].rearrange("w p c -> (w p) c")[bass.ds((t % WPB) * P, P), :]), f"msk{u}")

            def front_tile(S, u, k):
                V(S, pe, "hx", u, 1)
                V(S, pe, "v_ev", u, 1)
                for c in range(DH):
                    ins = pe.transpose(p_v[:, c * P:(c + 1) * P], hx[k][:, c * P:(c + 1) * P], ident[:])
                S.step("pe", ins, f"hT{u}")
                V(S, act, "hT", u)
                V(S, act, "v", u, 1)
                S.step("act", act.activation(hT[:].rearrange("p c t -> p (c t)"), p_v[:, 0:D], ACT.Copy), f"hT_ev{u}")

            def front_qk(S, u):
                V(S, pe, "hT_ev", u)
                V(S, pe, "qkT_ev", u)
                for n in range(2):
                    for c in range(DH):
                        ins = pe.matmul(p_qk[:, n * INNER:(n + 1) * INNER], hT[:, c, :],
                                        wqkv[:, c, n * INNER:(n + 1) * INNER], start=(c == 0), stop=(c == DH - 1))
                S.step("pe", ins, f"qk{u}")

            def front_v(S, u, slot):
                V(S, pe, "hT_ev", u)
                for c in range(DH):
                    ins = pe.matmul(p_v[:], hT[:, c, :], wqkv[:, c, 2 * INNER:3 * INNER], start=(c == 0),
                                    stop=(c == DH - 1))
                S.step("pe", ins, f"v{u}")
                V(S, act, "v", u)
                V(S, act, "pvB", u, 1)
                S.step("act", act.activation(vv[slot][:], p_v[:], ACT.Copy), f"v_ev{u}")

            def front_squares(S, u):
                V(S, act, "qk", u)
                V(S, act, "n2", u, 1)
                S.step("act", act.activation(sq[:], p_qk[:], ACT.Square), f"sq{u}")

            def front_rotate(S, u, k):
                qk4 = p_qk[:].rearrange("p (a h c) -> p a h c", a=2, h=H)
                rc4 = rc[:].rearrange("p (a h c) -> p a h c", a=2, h=H)
                rs4 = rsn[:].rearrange("p (a h c) -> p a h c", a=2, h=H)
                tk = tab[k][:].rearrange("p (a s) c -> p a s c", a=2)

                def per_head(x, n):
                    return x.unsqueeze(2).to_broadcast([P, 2, H, n])
                V(S, dve, "tab", u, 1)
                V(S, dve, "sq", u)
                V(S, dve, "qkT", u)
                S.step("dve", dve.tensor_tensor(out=rc4, in0=qk4, in1=per_head(tk[:, :, 0, :], DK), op=ALU.mult),
                       f"rc{u}")
                V(S, dve, "rot", u, 1)
                S.step("dve", dve.tensor_tensor(out=rs4[:, :, :, 0:hk], in0=qk4[:, :, :, hk:DK],
                                                in1=per_head(tk[:, :, 1, 0:hk], hk), op=ALU.mult), f"rs1{u}")
                S.step("dve", dve.tensor_tensor(out=rs4[:, :, :, hk:DK], in0=qk4[:, :, :, 0:hk],
                                                in1=per_head(tk[:, :, 1, hk:DK], hk), op=ALU.mult), f"rs2{u}")
                V(S, dve, "sq", u)
                V(S, dve, "rn", u, 2)
                S.step("dve", dve.tensor_reduce(n2[k][:], sq[:].rearrange("p (h c) -> p h c", c=DK), AX.X, ALU.add),
                       f"n2{u}")
                V(S, dve, "n2", u)
                S.step("dve", dve.tensor_scalar(n2[k][:], n2[k][:], 1e-24, None, ALU.max), f"n2c{u}")
                V(S, pool, "n2c", u)
                V(S, pool, "expB", u, 2)
                V(S, pool, "nbB", u, 2)
                S.step("pool", pool.tensor_tensor(out=rn[k][:], in0=n2[k][:], in1=mhalf[:], op=ALU.pow), f"rn{u}")
                V(S, pool, "rs2", u)
                S.step("pool", pool.tensor_tensor(out=rc[:], in0=rc[:], in1=rsn[:], op=ALU.add), f"rot{u}")
                V(S, pool, "rn", u)
                S.step("pool", pool.tensor_scalar(qsc[(u + 2) % RING][:], rn[k][:, 0:H], QK_SCALE, None, ALU.mult), f"qsc{u}")
                V(S, pool, "rot", u)
                S.step("pool", pool.tensor_tensor(out=rc4[:, 1], in0=rc4[:, 1],
                                                  in1=rn[k][:, H:2 * H].unsqueeze(2).to_broadcast([P, H, DK]),
                                                  op=ALU.mult), f"kn{u}")

            def front_qkT(S, u, slot):
                V(S, pe, "kn", u, 1)
                V(S, pe, "rs2", u, 1)
                V(S, pe, "sq", u, 1)
                for c in range(2 * INNER // P):
                    ins = pe.transpose(p_qk[:, c * P:(c + 1) * P], rc[:, c * P:(c + 1) * P], ident[:])
                S.step("pe", ins, f"qkT{u}")
                V(S, act, "qkT", u)
                V(S, act, "sB", u, 2)
                S.step("act", act.activation(qkT[slot][:], p_qk[:], ACT.Copy), f"qkT_ev{u}")

            def scores(S, u, half):
                n = "AB"[half]
                if half == 0:
                    V(S, pe, "qkT_ev", u, 1)
                    V(S, pe, "msk", u, 1)
                    V(S, pe, "expB", u, 1)
                else:
                    V(S, pe, "expA", u)
                mk = msk[u % 2][:].unsqueeze(1).to_broadcast([P, 2, 2 * P])
                for g in range(2):
                    pe.matmul(p_s[:, g * INNER:(g + 1) * INNER].rearrange("p (h c) -> p h c", h=2), identb[:], mk,
                              start=True, stop=False, skip_group_check=True)
                for a in range(2):
                    for w, s in enumerate(((u - 1) % RING, u)):
                        for g in range(2):
                            c = (2 * half + a) * P
                            at = ((2 * g + a) * 2 + w) * P
                            ins = pe.matmul(p_s[:, at:at + P], qkT[u][g * DK:(g + 1) * DK, c:c + P],
                                            qkT[s][g * DK:(g + 1) * DK, INNER + c:INNER + c + P],
                                            start=False, stop=(a == 1 and w == 1), skip_group_check=True)
                S.step("pe", ins, f"s{n}{u}")

            def head_at(half, j):
                return 4 * half + 2 * (j % 2) + j // 2

            def by_bank(x):
                return x.rearrange("p (a b) -> p b a", b=2)

            def softmax_max(S, u, half):
                n = "AB"[half]
                hs = slice(4 * half, 4 * half + 4)
                V(S, dve, f"s{n}", u)
                S.step("dve", dve.tensor_reduce(mx[:, hs], p_s[:].rearrange("p (h c) -> p h c", h=4), AX.X, ALU.max),
                       f"mx{n}{u}")
                V(S, dve, f"mx{n}", u)
                V(S, dve, "qsc", u, 2)
                V(S, dve, f"exp{n}", u, 1)
                S.step("dve", dve.scalar_tensor_tensor(out=by_bank(nb[:, hs]),
                                                       in0=mx[:, hs].rearrange("p (b a) -> p b a", b=2), scalar=-1.0,
                                                       in1=by_bank(qsc[u][:, hs]),
                                                       op0=ALU.mult, op1=ALU.mult), f"nb{n}{u}")

            def softmax_exp(S, u, half):
                n = "AB"[half]
                V(S, act, f"nb{n}", u)
                if half == 0:
                    V(S, act, "ptB", u, 1)
                    V(S, act, "rden", u, 1)
                else:
                    V(S, act, "ptA", u)
                for j in range(4):
                    h = head_at(half, j)
                    ins = act.activation(prob[:, j].rearrange("p w c -> p (w c)"), p_s[:, j * 2 * P:(j + 1) * 2 * P],
                                         ACT.Exp, bias=nb[:, h:h + 1], scale=qsc[u][:, h:h + 1],
                                         accum_out=den[u % 2][:, h:h + 1])
                S.step("act", ins, f"exp{n}{u}")

            def transpose_prob(S, u, half):
                n = "AB"[half]
                V(S, pe, f"exp{n}", u)
                if half == 0:
                    V(S, pe, "peB", u, 1)
                    V(S, pe, "paB", u, 1)
                else:
                    V(S, pe, "peA", u)
                    V(S, pe, "paA", u)
                pf = prob[:].rearrange("p j w c -> p (j w c)")
                tf = probT[:].rearrange("p j w c -> p (j w c)")
                for c in range(8):
                    ins = pe.transpose(p_t[:, c * P:(c + 1) * P], pf[:, c * P:(c + 1) * P], ident[:])
                S.step("pe", ins, f"pt{n}{u}")
                for eng, who, m, lo, hi in ((act, "act", "pa", 0, INNER), (dve, "dve", "pe", INNER, 2 * INNER)):
                    V(S, eng, f"pt{n}", u)
                    V(S, eng, "pvA" if half else "pvB", u, 0 if half else 1)
                    if eng is act:
                        ins = act.activation(tf[:, lo:hi], p_t[:, lo:hi], ACT.Copy)
                    else:
                        ins = dve.tensor_copy(tf[:, lo:hi], p_t[:, lo:hi])
                    S.step(who, ins, f"{m}{n}{u}")

            def weighted_values(S, u, half):
                n = "AB"[half]
                V(S, pe, f"pe{n}", u)
                V(S, pe, f"pa{n}", u)
                if half == 0:
                    V(S, pe, "v_ev", u, 2)
                    V(S, pe, "xo", u)
                for j in range(4):
                    h = head_at(half, j)
                    for w, s in enumerate(((u - 1) % RING, u)):
                        ins = pe.matmul(p_o[:, h * DK:(h + 1) * DK], probT[:, j, w, :], vv[s][:, h * DK:(h + 1) * DK],
                                        start=(w == 0), stop=(w == 1), skip_group_check=True)
                S.step("pe", ins, f"pv{n}{u}")

            def divide(S, u, k):
                V(S, dve, "expB", u, 1)
                S.step("dve", dve.reciprocal(rden[:], den[k][:]), f"rden{u}")
                V(S, dve, "pvB", u, 1)
                V(S, dve, "rden", u)
                V(S, dve, "oT", u, 1)
                S.step("dve", dve.tensor_tensor(out=o_sb[:].rearrange("p (h c) -> p h c", h=H),
                                                in0=p_o[:].rearrange("p (h c) -> p h c", h=H),
                                                in1=rden[:].unsqueeze(2).to_broadcast([P, H, DK]), op=ALU.mult), f"o{u}")

            def turn_out(S, u):
                V(S, pe, "o", u)
                for c in range(INNER // P):
                    ins = pe.transpose(p_o[:, c * P:(c + 1) * P], o_sb[:, c * P:(c + 1) * P], ident[:])
                S.step("pe", ins, f"oT{u}")
                V(S, act, "oT", u)
                V(S, act, "wo", u, 1)
                S.step("act", act.activation(oT[:], p_o[:], ACT.Copy), f"oT_ev{u}")

            def project(S, u, k, t):
                V(S, pe, "oT_ev", u)
                for c in range(INNER // P):
                    ins = pe.matmul(p_o[:, 0:D], oT[:, c * P:(c + 1) * P], wo[:, c, :], start=(c == 0),
                                    stop=(c == INNER // P - 1))
                S.step("pe", ins, f"wo{u}")
                V(S, dve, "wo", u)
                V(S, dve, "res", u, 1)
                V(S, dve, "out", u, 2)
                S.step("dve", dve.tensor_tensor(out=xo[k][:], in0=p_o[:, 0:D], in1=res[k][:], op=ALU.add), f"xo{u}")
                V(S, sp, "xo", u)
                S.load(sp.dma_start(rows(2 * l + 1, tile_slot(t), P), xo[k][:]), f"out{u}")

            S = SA0
            S.begin(l)
            S.load(sp.dma_start(wqkv[:], layer_rows("L0_ffn_wqkv", l, D).rearrange("(c p) n -> p c n", p=P)),
                   "weights")
            S.load(sp.dma_start(wo[:], layer_rows("L0_ffn_wo", l, INNER).rearrange("(c p) n -> p c n", p=P)),
                   "weights")
            S.step("dve", dve.memset(qkT[RING - 1][:], 0.0), "k_none")
            S.step("dve", dve.memset(vv[RING - 1][:], 0.0), "v_none")
            S.step("dve", dve.memset(den[1][:], 1.0), "den_none")
            S.step("dve", dve.memset(res[1][:], 0.0), "res_none")
            S.step("dve", dve.memset(p_o[:], 0.0), "o_none")
            load_tile(S, 1, 0, l)
            load_tile(S, 2, 1, l)
            load_mask(S, RING - 1, 0)
            S.wait(pe, "weights")
            front_tile(S, 2, 0)
            front_qk(S, 2)
            front_squares(S, 2)
            front_rotate(S, 2, 0)
            front_v(S, 2, 0)
            S.wait(sp, "hT2")
            S.wait(sp, "rs22")
            load_tile(S, 3, 2, l)
            front_qkT(S, 3, 0)
            front_tile(S, 3, 1)
            front_qk(S, 3)
            front_squares(S, 3)
            front_rotate(S, 3, 1)
            front_v(S, 3, 1)
            S.close()
            S.done(l + 1)
            S = SA
            with nc.Fori(0, NT // RING) as i:
                S.begin(l * (NT // RING) + i)
                for u in range(RING):
                    t = i * RING + u
                    k = u % 2
                    V(S, sp, "hT", u, 1)
                    V(S, sp, "rs2", u, 1)
                    load_tile(S, u, t + 3, l)
                    V(S, sp, "sB", u, 1)
                    load_mask(S, u, t + 1)
                    V(S, sp, "xo", u, 1)
                    S.load(sp.dma_start(res[k][:], rows(2 * l, tile_slot(t), P)), f"res{u}")
                    scores(S, u, 0)
                    divide(S, u, 1 - k)
                    turn_out(S, u)
                    softmax_max(S, u, 0)
                    front_tile(S, u, k)
                    softmax_exp(S, u, 0)
                    project(S, u, 1 - k, t - 1)
                    transpose_prob(S, u, 0)
                    scores(S, u, 1)
                    softmax_max(S, u, 1)
                    front_qkT(S, u, (u + 1) % RING)
                    softmax_exp(S, u, 1)
                    weighted_values(S, u, 0)
                    front_qk(S, u)
                    front_squares(S, u)
                    transpose_prob(S, u, 1)
                    front_v(S, u, (u + 2) % RING)
                    weighted_values(S, u, 1)
                    front_rotate(S, u, k)
                S.close()
            S.done((l + 1) * (NT // RING))
            S = SA1
            S.begin(l)
            divide(S, 0, 1)
            turn_out(S, 0)
            project(S, 0, 1, NT - 1)
            S.close()
            S.done(l + 1)

        DI, NST, WC, R = 512, 16, 4, 64
        Q = DI // P
        CPB = L // CH
        ssm_out = nc.dram_tensor("ssm_out", [CH + T, D], F32).ap()

        NB, LAG = 4, 2

        def mamba(ctx):
            w_in = sb(ctx, "w_in", [P, DH, 2 * DI])
            w_xp = sb(ctx, "w_xp", [P, Q, R + 2 * NST])
            w_bc = sb(ctx, "w_bc", [P, Q, 3, 2 * NST])
            w_dt = sb(ctx, "w_dt", [R, DI])
            w_out = sb(ctx, "w_out", [P, Q, D])
            cw = sb(ctx, "cw", [P, Q, WC])
            cb = sb(ctx, "cb", [P, Q])
            dtb = sb(ctx, "dtb", [P, Q])
            dpar = sb(ctx, "dpar", [P, Q])
            am = sb(ctx, "am", [P, Q, NST])
            sel = sb(ctx, "sel", [96, 2 * NST, P], BF16)
            one = sb(ctx, "one", [P, 1])
            xin = sb(ctx, "xin", [P, CT, D])
            xT = sb(ctx, "mxT", [P, DH, CH])
            xr = sb(ctx, "xr", [P, Q, WC - 1 + CH])
            cv = sb(ctx, "cv", [P, Q, CH])
            xd = sb(ctx, "xd", [R, CH])
            bc = sb(ctx, "bc", [96, CH])
            bcr = sb(ctx, "bcr", [96, CH])
            bct = sb(ctx, "bct", [96, CH], BF16)
            bc3 = [sb(ctx, f"bc3{k}", [96, CH], BF16) for k in range(2)]
            ee = sb(ctx, "ee", [P, Q, CH])
            uu = [sb(ctx, f"uu{k}", [P, Q, CH]) for k in range(2)]
            sz = [sb(ctx, f"sz{k}", [P, Q, CH]) for k in range(2)]
            dl = [sb(ctx, f"dl{k}", [P, Q, CH]) for k in range(2)]
            du = [sb(ctx, f"du{k}", [P, Q, CH]) for k in range(2)]
            da = [sb(ctx, f"da{k}", [P, Q, CH]) for k in range(2)]
            hh = [sb(ctx, f"hh{k}", [P, Q, CH]) for k in range(NB)]
            cs = [sb(ctx, f"cs{k}", [P, CH]) for k in range(NB)]
            hlast = sb(ctx, "hlast", [P, NST, Q])
            so = sb(ctx, "so", [P, CT, D])
            p_acc = ps(ctx, "p_acc", Q * CH)
            p_b = ps(ctx, "p_b", CH)
            p_c = ps(ctx, "p_c", CH)
            p_f = [ps(ctx, f"p_f{k}", CH) for k in range(2)]

            def VM(S, eng, name, u, d=0, alone=False):
                v = u - d
                S.wait(eng, f"{name}_{v % CPB}", back=1 if v < 0 else 0, alone=alone)

            def load_x(S, u, c):
                S.load(sp.dma_start(xin[:], rows(0, chunk_slot(c), CH).rearrange("(j p) d -> p j d", p=P)), f"x_{u}")

            def f_turn(S, u):
                VM(S, pe, "x", u, 1)
                VM(S, pe, "rl3", u, 1)
                for f in range(DH):
                    for j in range(CT):
                        ins = pe.transpose(p_f[f][:, j * P:(j + 1) * P], xin[:, j, f * P:(f + 1) * P], ident[:])
                S.step("pe", ins, f"tr_{u}")
                VM(S, act, "tr", u)
                for f in range(DH):
                    ins = act.activation(xT[:, f], p_f[f][:], ACT.Copy)
                S.step("act", ins, f"xT_{u}")

            def f_in(S, u, q, o, name, prev):
                VM(S, pe, "xT", u)
                VM(S, pe, prev, u)
                for f in range(DH):
                    ins = pe.matmul(p_f[q % 2][:], w_in[:, f, o + q * P:o + (q + 1) * P], xT[:, f], start=(f == 0),
                                    stop=(f == DH - 1))
                S.step("pe", ins, f"{name}_{u}")

            def f_x(S, u, q):
                if q == 0:
                    VM(S, dve, "tap3", u, 1)
                    if u == CPB - 1:
                        ins = dve.memset(xr[:, :, 0:WC - 1], 0.0)
                    else:
                        VM(S, dve, "xr3", u, 1)
                        ins = dve.tensor_copy(xr[:, :, 0:WC - 1], xr[:, :, CH:CH + WC - 1])
                    S.step("dve", ins, f"carry_{u}")
                f_in(S, u, q, 0, f"inx{q}", "xT" if q < 2 else f"xr{q - 2}")
                VM(S, act, f"inx{q}", u)
                VM(S, act, "carry", u)
                S.step("act", act.activation(xr[:, q, WC - 1:], p_f[q % 2][:], ACT.Copy), f"xr{q}_{u}")

            def f_z(S, u, q, k):
                if q < 2:
                    VM(S, pe, "so", u)
                f_in(S, u, q, DI, f"inz{q}", f"xr{q + 2}" if q < 2 else f"zr{q - 2}")
                VM(S, act, f"inz{q}", u)
                VM(S, act, "yz", u)
                S.step("act", act.activation(sz[k][:, q], p_f[q % 2][:], ACT.Copy), f"zr{q}_{u}")

            def f_tap(S, u, w):
                if w == 0:
                    VM(S, dve, "xr3", u)
                    VM(S, dve, "u", u, 1)
                else:
                    VM(S, dve, f"tap{w - 1}", u)
                for q in range(Q):
                    if w == 0:
                        ins = dve.tensor_scalar(cv[:, q], xr[:, q, 0:CH], cw[:, q, 0:1], None, ALU.mult)
                    else:
                        ins = dve.scalar_tensor_tensor(out=cv[:, q], in0=xr[:, q, w:w + CH], scalar=cw[:, q, w:w + 1],
                                                       in1=cv[:, q], op0=ALU.mult, op1=ALU.add)
                S.step("dve", ins, f"tap{w}_{u}")

            def f_u(S, u, k):
                VM(S, act, "zr3", u)
                S.step("act", act.activation(sz[k][:], sz[k][:], ACT.Silu), f"sz_{u}")
                VM(S, act, "tap3", u)
                VM(S, act, "op", u)
                for q in range(Q):
                    ins = act.activation(uu[k][:, q], cv[:, q], ACT.Silu, bias=cb[:, q:q + 1])
                S.step("act", ins, f"u_{u}")

            def f_xp(S, u, k):
                VM(S, pe, "u", u)
                VM(S, pe, "zr3", u)
                for q in range(Q):
                    ins = pe.matmul(p_f[0][0:R, :], w_xp[:, q, 0:R], uu[k][:, q], start=(q == 0), stop=(q == Q - 1))
                S.step("pe", ins, f"xp_{u}")
                for q in range(Q):
                    ins = pe.matmul(p_f[1][0:96, :], w_bc[:, q].rearrange("p r n -> p (r n)"), uu[k][:, q],
                                    start=(q == 0), stop=(q == Q - 1))
                S.step("pe", ins, f"bc_{u}")
                VM(S, act, "xp", u)
                VM(S, act, "dt3", u, 1)
                S.step("act", act.activation(xd[:], p_f[0][0:R, :], ACT.Copy), f"xd_{u}")
                VM(S, act, "bc", u)
                VM(S, act, "b3c", u, 1)
                S.step("act", act.activation(bc[:], p_f[1][0:96, :], ACT.Copy), f"bcs_{u}")

            def f_split(S, u, k):
                VM(S, dve, "bcs", u)
                VM(S, dve, "cn15", u, 1)
                S.step("dve", dve.tensor_copy(bct[:], bc[:]), f"b1_{u}")
                S.step("dve", dve.tensor_copy(bc3[k][0:32, :], bc[0:32, :]), f"b1c_{u}")
                VM(S, dve, "b1", u)
                S.step("dve", dve.tensor_tensor(out=bcr[:], in0=bc[:], in1=bct[:], op=ALU.subtract), f"r1_{u}")
                VM(S, dve, "r1", u)
                S.step("dve", dve.tensor_copy(bct[:], bcr[:]), f"b2_{u}")
                S.step("dve", dve.tensor_copy(bc3[k][32:64, :], bcr[32:64, :]), f"b2c_{u}")
                VM(S, dve, "b2", u)
                S.step("dve", dve.tensor_tensor(out=bcr[64:96, :], in0=bcr[64:96, :], in1=bct[64:96, :],
                                                op=ALU.subtract), f"r2_{u}")
                VM(S, dve, "r2", u)
                S.step("dve", dve.tensor_copy(bc3[k][64:96, :], bcr[64:96, :]), f"b3c_{u}")

            def f_dt(S, u, q, k):
                VM(S, pe, "xd", u)
                VM(S, pe, "bcs", u)
                if q >= 2:
                    VM(S, pe, f"rl{q - 2}", u)
                S.step("pe", pe.matmul(p_f[q % 2][:], w_dt[:, q * P:(q + 1) * P], xd[:], start=True, stop=True),
                       f"dt{q}_{u}")
                VM(S, act, f"dt{q}", u)
                VM(S, act, "sp", u, 1)
                VM(S, act, "ex15", u, 1)
                S.step("act", act.activation(ee[:, q], p_f[q % 2][:], ACT.Abs, bias=dtb[:, q:q + 1]), f"ab{q}_{u}")
                S.step("act", act.activation(dl[k][:, q], p_f[q % 2][:], ACT.Relu, bias=dtb[:, q:q + 1]), f"rl{q}_{u}")

            def f_softplus(S, u, k):
                VM(S, act, "rl3", u)
                S.step("act", act.activation(ee[:], ee[:], ACT.Exp, scale=-1.0), f"ea_{u}")
                VM(S, act, "ea", u)
                S.step("act", act.activation(ee[:], ee[:], ACT.Ln, bias=one[:]), f"ln_{u}")
                VM(S, pool, "ln", u)
                S.step("pool", pool.tensor_tensor(out=dl[k][:], in0=dl[k][:], in1=ee[:], op=ALU.add), f"sp_{u}")

            def f_du(S, u, k):
                VM(S, pool, "sp", u)
                VM(S, pool, "db15", u, 1)
                S.step("pool", pool.tensor_tensor(out=du[k][:], in0=dl[k][:], in1=uu[k][:], op=ALU.mult), f"du_{u}")

            def b_cast(S, u, n, k):
                if n == 0:
                    VM(S, pe, "b3c", u, 1)
                    VM(S, pe, "b2c", u, 1)
                    VM(S, pe, "db15", u, 1)
                    VM(S, pe, "ce15", u, 1)
                else:
                    VM(S, pe, f"db{n - 1}", u)
                    VM(S, pe, f"ce{n - 1}", u)
                S.step("pe", pe.matmul(p_b[:], sel[:, n, :], bc3[k][:], start=True, stop=True), f"bn{n}_{u}")
                S.step("pe", pe.matmul(p_c[:], sel[:, NST + n, :], bc3[k][:], start=True, stop=True), f"cn{n}_{u}")

            def b_in(S, u, n, k):
                a, b = n % 2, n % NB
                if n < 2:
                    VM(S, act, f"sc{n + 14}", u, 1)
                else:
                    VM(S, act, f"sc{n - 2}", u)
                if n == 0:
                    VM(S, act, "sp", u, 1)
                for q in range(Q):
                    ins = act.activation(da[a][:, q], dl[k][:, q], ACT.Exp, scale=am[:, q, n:n + 1])
                S.step("act", ins, f"ex{n}_{u}")
                VM(S, act, f"cn{n}", u)
                before = (n - NB) % NST
                VM(S, act, f"hc{before}", u, int(n < NB))
                S.step("act", act.activation(cs[b][:], p_c[:], ACT.Copy), f"ce{n}_{u}")
                VM(S, dve, f"bn{n}", u)
                VM(S, dve, f"ac{before}", u, int(n < NB and before < NST - LAG))
                if n == 0:
                    VM(S, dve, "du", u, 1)
                S.step("dve", dve.tensor_tensor(out=hh[b][:], in0=du[k][:],
                                                in1=p_b[:].unsqueeze(1).to_broadcast([P, Q, CH]), op=ALU.mult),
                       f"db{n}_{u}")

            def b_scan(S, u, n):
                a, b = n % 2, n % NB
                VM(S, dve, f"ex{n}", u)
                VM(S, dve, f"db{n}", u)
                if u > 0:
                    VM(S, dve, f"hl{n}", u, 1)
                for q in range(Q):
                    ins = dve.tensor_tensor_scan(out=hh[b][:, q], data0=da[a][:, q], data1=hh[b][:, q],
                                                 initial=0.0 if u == 0 else hlast[:, n, q:q + 1],
                                                 op0=ALU.mult, op1=ALU.add)
                S.step("dve", ins, f"sc{n}_{u}")

            def b_out(S, u, n):
                b = n % NB
                VM(S, pool, f"sc{n}", u)
                VM(S, pool, f"ce{n}", u)
                S.step("pool", pool.tensor_copy(hlast[:, n].unsqueeze(2), hh[b][:, :, CH - 1:CH]), f"hl{n}_{u}")
                VM(S, pool, f"hl{n}", u)
                S.step("pool", pool.tensor_tensor(out=hh[b][:], in0=hh[b][:],
                                                  in1=cs[b][:].unsqueeze(1).to_broadcast([P, Q, CH]), op=ALU.mult),
                       f"hc{n}_{u}")

            def b_sum(S, u, n):
                VM(S, pe, f"hc{n}", u, int(n >= NST - LAG))
                if n == 0:
                    VM(S, pe, "yu", u)
                for q in range(Q):
                    ins = pe.matmul(p_acc[:, q * CH:(q + 1) * CH], ident[:], hh[n % NB][:, q], start=(n == 0),
                                    stop=(n == NST - 1), skip_group_check=True)
                S.step("pe", ins, f"ac{n}_{u}")

            def e_gate(S, u, k):
                VM(S, dve, "ac15", u)
                for q in range(Q):
                    ins = dve.scalar_tensor_tensor(out=uu[k][:, q], in0=uu[k][:, q], scalar=dpar[:, q:q + 1],
                                                   in1=p_acc[:, q * CH:(q + 1) * CH], op0=ALU.mult, op1=ALU.add)
                S.step("dve", ins, f"yu_{u}")
                VM(S, pool, "yu", u)
                S.step("pool", pool.tensor_tensor(out=uu[k][:], in0=uu[k][:], in1=sz[k][:], op=ALU.mult), f"yz_{u}")

            def e_out(S, u, k, c):
                VM(S, pe, "yz", u)
                VM(S, pe, "xr3", u)
                for j in range(CT):
                    for q in range(Q):
                        ins = pe.matmul(p_f[j // 2][:, (j % 2) * D:(j % 2 + 1) * D], uu[k][:, q, j * P:(j + 1) * P],
                                        w_out[:, q, :], start=(q == 0), stop=(q == Q - 1))
                S.step("pe", ins, f"op_{u}")
                VM(S, act, "op", u)
                VM(S, act, "st", u, 1)
                for j in range(2):
                    ins = act.activation(so[:, 2 * j:2 * j + 2].rearrange("p j d -> p (j d)"), p_f[j][:], ACT.Copy)
                S.step("act", ins, f"so_{u}")
                VM(S, sp, "so", u)
                S.load(sp.dma_start(ssm_out[bass.ds((c + 1) * CH, CH), :].rearrange("(j p) d -> p j d", p=P), so[:]),
                       f"st_{u}")

            def front_at(S, u, n):
                k = (u + 1) % 2
                if n == 0:
                    f_turn(S, u)
                elif n in (1, 2):
                    f_x(S, u, 2 * n - 2)
                    f_x(S, u, 2 * n - 1)
                elif n in (3, 4):
                    f_tap(S, u, n - 3)
                elif n in (5, 6):
                    f_tap(S, u, n - 3)
                    f_z(S, u, 2 * n - 10, k)
                    f_z(S, u, 2 * n - 9, k)
                elif n == 7:
                    f_u(S, u, k)
                elif n == 8:
                    f_xp(S, u, k)
                elif n == 9:
                    f_split(S, u, k)
                elif n in (10, 11):
                    f_dt(S, u, 2 * n - 20, k)
                    f_dt(S, u, 2 * n - 19, k)
                elif n == 12:
                    f_softplus(S, u, k)
                elif n == 13:
                    f_du(S, u, k)

            S = Steps(nc, top, book, gate, "ssm_first", lenient=True)
            S.begin(0)
            w = "weights"
            S.load(sp.dma_start(w_in[:], A["L0_attn_in_proj_w"].rearrange("(c p) n -> p c n", p=P)), w)
            S.load(sp.dma_start(w_xp[:], A["L0_attn_x_proj_w"].rearrange("(q p) n -> p q n", p=P)), w)
            for r in range(3):
                S.load(sp.dma_start(w_bc[:, :, r, :],
                                    A["L0_attn_x_proj_w"][:, R:].rearrange("(q p) n -> p q n", p=P)), w)
            S.load(sp.dma_start(w_dt[:], A["L0_attn_dt_proj_w"]), w)
            S.load(sp.dma_start(w_out[:], A["L0_attn_out_proj_w"].rearrange("(q p) n -> p q n", p=P)), w)
            S.load(sp.dma_start(cw[:], A["L0_attn_conv_w"].rearrange("(q p) n -> p q n", p=P)), w)
            for dst, nm in ((cb, "L0_attn_conv_b"), (dtb, "L0_attn_dt_proj_b"), (dpar, "L0_attn_D_param")):
                for q in range(Q):
                    S.load(sp.dma_start(dst[:, q:q + 1], A[nm].unsqueeze(1)[q * P:(q + 1) * P, :]), w)
            S.load(sp.dma_start(am[:], A["L0_attn_A_log"].rearrange("(q p) n -> p q n", p=P)), w)
            S.load(sp.dma_start(sel[:], A["c_select"]), w)
            S.step("dve", dve.memset(one[:], 1.0), "one")
            for t in (uu[1], sz[1], hh[NB - 2], hh[NB - 1]):
                ins = dve.memset(t[:], 0.0)
            S.step("dve", ins, "none")
            S.wait(pe, "none")
            for q in range(Q):
                ins = pe.matmul(p_acc[:, q * CH:(q + 1) * CH], ident[:], hh[NB - 1][:, q], start=True, stop=False,
                                skip_group_check=True)
            S.step("pe", ins, "acc0")
            load_x(S, CPB - 2, 0)
            for eng in (pe, act, dve):
                S.wait(eng, w)
            S.wait(act, "one")
            S.step("act", act.activation(am[:], am[:], ACT.Exp), "aexp")
            S.wait(dve, "aexp")
            S.step("dve", dve.tensor_scalar(am[:], am[:], -1.0, None, ALU.mult), "aneg")
            for n in range(NST):
                front_at(S, CPB - 1, n)
            S.wait(sp, f"tr_{CPB - 1}")
            load_x(S, CPB - 1, 1)
            S.close()
            S.done(1)

            S = Steps(nc, top, book, gate, "ssm")
            with nc.Fori(0, B) as i:
                S.begin(i)
                for u in range(CPB):
                    c, k = i * CPB + u, u % 2
                    b_cast(S, u, 0, k)
                    b_in(S, u, 0, k)
                    for n in range(NST):
                        if n + 1 < NST:
                            b_cast(S, u, n + 1, k)
                            b_in(S, u, n + 1, k)
                        b_scan(S, u, n)
                        b_out(S, u, n)
                        b_sum(S, u, (n - LAG) % NST)
                        if n == LAG - 1:
                            e_gate(S, u, 1 - k)
                        if n == 4:
                            e_out(S, u, 1 - k, c - 1)
                        front_at(S, u, n)
                        if n == 1:
                            VM(S, sp, "tr", u)
                            load_x(S, u, c + 2)
                S.close()
            S.done(B)

            S = Steps(nc, top, book, gate, "ssm_last", lenient=True)
            S.begin(0)
            for n in range(NST - LAG, NST):
                b_sum(S, 0, n)
            e_gate(S, 0, 1)
            e_out(S, 0, 1, NC - 1)
            S.close()
            S.done(1)

        with ExitStack() as ctx:
            mamba(ctx)

        SG0 = Steps(nc, top, book, gate, "gated_first", lenient=True)
        SG = Steps(nc, top, book, gate, "gated")
        BJ = -(-HID // NJ)
        BLK = [min(BJ, HID - j * BJ) for j in range(NJ)]

        def V2(S, eng, name, u, d=0, alone=False):
            v = u - d
            S.wait(eng, f"{name}{v % 2}", back=1 if v < 0 else 0, alone=alone)

        def norm_stats(S, u, x, st, mv, rstd, eps, last_use):
            V2(S, dve, last_use, u, 1)
            for j in range(CT):
                ins = dve.bn_stats(st[:, j], x[:, j])
            S.step("dve", ins, f"st{u}")
            V2(S, dve, "st", u, alone=True)
            for j in range(CT):
                ins = dve.bn_aggr(mv[:, j], st[:, j])
            S.step("dve", ins, f"mv{u}")
            V2(S, dve, "mv", u)
            S.step("dve", dve.tensor_scalar(rstd[:], mv[:, :, 1], eps, None, ALU.add), f"var{u}")
            V2(S, pool, "var", u)
            S.step("pool", pool.tensor_tensor(out=rstd[:], in0=rstd[:], in1=mhalf[:, 0:CT], op=ALU.pow), f"rs{u}")

        def gated(l, gctx):
            w1 = sb(gctx, "w1", [P, DH, 2 * HID])
            w2 = sb(gctx, "w2", [BJ, NJ, D])
            b1 = sb(gctx, "b1", [BJ, 2, NJ])
            b2 = sb(gctx, "b2", [P, D])
            lgb = sb(gctx, "lgb", [P, 2, DH])
            h = [sb(gctx, f"gh{k}", [P, CT, D]) for k in range(2)]
            r = [sb(gctx, f"gr{k}", [P, CT, D]) for k in range(2)]
            hn = sb(gctx, "ghn", [P, CT, D])
            hT = sb(gctx, "ghT", [P, DH, CH])
            st = sb(gctx, "gst", [P, CT, 6])
            mv = sb(gctx, "gmv", [P, CT, 2])
            rstd = sb(gctx, "grstd", [P, CT])
            gg = [sb(gctx, f"gg{k}", [BJ, CH]) for k in range(2)]
            hid = sb(gctx, "ghid", [BJ, NJ, CH])
            p_tr = ps(gctx, "p_tr", DH * CH)
            p_a = [ps(gctx, f"p_a{k}", CH) for k in range(2)]
            p_g = [ps(gctx, f"p_g{k}", CH) for k in range(2)]
            p_y = ps(gctx, "p_y", CT * D)

            def load_h(S, u, c):
                slot = chunk_slot(c)
                for src, cols in ((0, slice(0, P)), (-1, slice(P, D))):
                    S.load(sp.dma_start(h[u][:, :, cols],
                                        rows(2 * l + 1, slot, CH, src)[:, cols].rearrange("(j p) d -> p j d", p=P)),
                           f"h{u}")

            def prepare(S, u, k):
                V2(S, dve, "h", u, 1)
                norm_stats(S, u, h[k], st, mv, rstd, 1e-5, "norm")
                V2(S, dve, "rs", u)
                V2(S, dve, "tr", u, 1)
                for j in range(CT):
                    ins = dve.tensor_scalar(hn[:, j], h[k][:, j], mv[:, j, 0:1], rstd[:, j:j + 1], ALU.subtract,
                                            ALU.mult)
                S.step("dve", ins, f"norm{u}")

            def turn(S, u):
                V2(S, pe, "norm", u)
                V2(S, pe, "hT", u, 1)
                for f in range(DH):
                    for j in range(CT):
                        ins = pe.transpose(p_tr[:, f * CH + j * P:f * CH + (j + 1) * P],
                                           hn[:, j, f * P:(f + 1) * P], ident[:])
                S.step("pe", ins, f"tr{u}")
                V2(S, dve, "tr", u)
                V2(S, dve, "w1_5", u)
                for f in range(DH):
                    ins = dve.tensor_scalar(hT[:, f], p_tr[:, f * CH:(f + 1) * CH], lgb[:, 0, f:f + 1],
                                            lgb[:, 1, f:f + 1], ALU.mult, ALU.add)
                S.step("dve", ins, f"hT{u}")

            def up(S, u):
                for j in range(NJ):
                    n, k = BLK[j], j % 2
                    if j == 0:
                        V2(S, pe, "hT", u, 1)
                    if j < 2:
                        V2(S, pe, f"hid_{j + NJ - 2}_", u, 1)
                    else:
                        V2(S, pe, f"hid_{j - 2}_", u)
                    for dst, o in ((p_g[k], HID), (p_a[k], 0)):
                        for f in range(DH):
                            ins = pe.matmul(dst[0:n, :], w1[:, f, o + j * BJ:o + j * BJ + n], hT[:, f, :],
                                            start=(f == 0), stop=(f == DH - 1))
                    S.step("pe", ins, f"w1_{j}{u}")
                    V2(S, act, f"w1_{j}", u)
                    if j < 2:
                        V2(S, act, f"hid_{j + NJ - 2}_", u, 1)
                    else:
                        V2(S, act, f"hid_{j - 2}_", u)
                    S.step("act", act.activation(gg[k][0:n, :], p_g[k][0:n, :], ACT.Gelu, bias=b1[0:n, 1, j:j + 1]),
                           f"gelu_{j}_{u}")
                    V2(S, dve, f"gelu_{j}_", u)
                    if j == 0:
                        V2(S, dve, "w2b", u, 1)
                    S.step("dve", dve.scalar_tensor_tensor(out=hid[0:n, j], in0=p_a[k][0:n, :],
                                                           scalar=b1[0:n, 0, j:j + 1], in1=gg[k][0:n, :],
                                                           op0=ALU.add, op1=ALU.mult), f"hid_{j}_{u}")

            def down(S, u):
                V2(S, pool, "r", u)
                S.step("pool", pool.tensor_tensor(out=r[u][:], in0=r[u][:],
                                                  in1=b2[:].unsqueeze(1).to_broadcast([P, CT, D]), op=ALU.add),
                       f"rb{u}")
                V2(S, pe, f"hid_{NJ - 1}_", u)
                for half, nm in enumerate("ab"):
                    V2(S, pe, "y" + nm, u, 1)
                    for m in range(2):
                        j0 = 2 * half + m
                        for j in range(NJ):
                            n = BLK[j]
                            ins = pe.matmul(p_y[:, j0 * D:(j0 + 1) * D], hid[0:n, j, j0 * P:(j0 + 1) * P],
                                            w2[0:n, j, :], start=(j == 0), stop=(j == NJ - 1))
                    S.step("pe", ins, f"w2{nm}{u}")
                V2(S, dve, "rb", u)
                for half, nm in enumerate("ab"):
                    V2(S, dve, "w2" + nm, u)
                    rr = r[u][:, 2 * half:2 * half + 2].rearrange("p j d -> p (j d)")
                    S.step("dve", dve.tensor_tensor(out=rr, in0=p_y[:, 2 * half * D:(2 * half + 2) * D], in1=rr,
                                                    op=ALU.add), f"y{nm}{u}")

            S = SG0
            S.begin(l)
            S.load(sp.dma_start(w1[:], layer_rows("L0_ffn_w1", l, D).rearrange("(c p) n -> p c n", p=P)), "weights")
            b1f = A["L0_ffn_b1"].rearrange("l n -> (l n)").unsqueeze(1)
            w2f = A["L0_ffn_w2"].rearrange("l r n -> (l r) n")
            for j in range(NJ):
                n = BLK[j]
                S.load(sp.dma_start(w2[0:n, j, :], w2f[bass.ds(l * HID + j * BJ, n), :]), "weights")
                for q in range(2):
                    S.load(sp.dma_start(b1[0:n, q, j:j + 1], b1f[bass.ds(l * 2 * HID + q * HID + j * BJ, n), :]),
                           "weights")
            for q, nm in enumerate(("L0_ffn_ln_g", "L0_ffn_ln_b")):
                v = A[nm].rearrange("l n -> (l n)").unsqueeze(1)
                for f in range(DH):
                    S.load(sp.dma_start(lgb[:, q, f:f + 1], v[bass.ds(l * D + f * P, P), :]), "weights")
            S.load(sp.dma_start(b2[:], A["L0_ffn_b2"][bass.ds(l, 1), :].to_broadcast([P, D])), "weights")
            load_h(S, 0, 0)
            load_h(S, 1, 1)
            S.wait(dve, "weights")
            S.wait(dve, "h0")
            prepare(S, 1, 0)
            turn(S, 1)
            S.close()
            S.done(l + 1)
            S = SG
            with nc.Fori(0, NC // 2) as i:
                S.begin(l * (NC // 2) + i)
                for u in range(2):
                    c = i * 2 + u
                    V2(S, sp, "norm", u, 1)
                    load_h(S, u, c + 2)
                    V2(S, sp, "out", u, 2)
                    S.load(sp.dma_start(r[u][:], rows(2 * l + 1, chunk_slot(c), CH).rearrange("(j p) d -> p j d", p=P)),
                           f"r{u}")
                    up(S, u)
                    prepare(S, u, (u + 1) % 2)
                    turn(S, u)
                    down(S, u)
                    V2(S, sp, "yb", u)
                    S.load(sp.dma_start(rows(2 * l + 2, chunk_slot(c), CH).rearrange("(j p) d -> p j d", p=P), r[u][:]),
                           f"out{u}")
                S.close()
            S.done((l + 1) * (NC // 2))

        with nc.Fori(0, NL) as l:
            with ExitStack() as ctx:
                attention(l, ctx)
            with ExitStack() as ctx:
                gated(l, ctx)

        HA, DA = 16, 16
        NE, TOPK, CAP, EI = 64, 6, 128, 176
        SI = 2 * EI
        NX = NE + 2
        EXT = D + NE + 1
        NJS = 3
        BS = [min(P, SI - j * P) for j in range(NJS)]
        FAR = 16384.0
        KB = 0.21
        x1_d = nc.dram_tensor("x1", [T, D], F32).ap()
        xn1_d = nc.dram_tensor("xn1", [T, D], F32).ap()
        xb_d = nc.dram_tensor("dispatched", [NE * CAP, EXT], F32).ap()
        y_d = nc.dram_tensor("moe_out", [T + 1, D], F32).ap()
        kv_d = nc.dram_tensor("kv", [B * P, 2 * D], F32).ap()

        def VC(S, eng, name, u, d=0, alone=False):
            v = u - d
            S.wait(eng, f"{name}_{v % CPB}", back=1 if v < 0 else 0, alone=alone)

        def tiles(ap):
            return ap.rearrange("(j p) d -> p j d", p=P)

        def rope(S, u, src, cos, sin, t1, t2, free, tag):
            s2, i2, o2 = (x.rearrange("p j (h two) -> p j h two", two=2) for x in (src, sin, t2))
            for nm in free:
                VC(S, dve, nm, u, 1)
            S.step("dve", dve.tensor_tensor(out=t1, in0=src, in1=cos, op=ALU.mult), f"{tag}c_{u}")
            for e in range(2):
                ins = dve.tensor_tensor(out=o2[:, :, :, e], in0=s2[:, :, :, 1 - e], in1=i2[:, :, :, e], op=ALU.mult)
            S.step("dve", ins, f"{tag}s_{u}")
            VC(S, pool, f"{tag}s", u)
            S.step("pool", pool.tensor_tensor(out=t1, in0=t1, in1=t2, op=ALU.add), f"{tag}_{u}")

        def layer_norm(S, u, x, st, mv, rs, eps, out, free, tag):
            VC(S, dve, f"{tag}", u, 1)
            for j in range(CT):
                ins = dve.bn_stats(st[:, j], x[:, j])
            S.step("dve", ins, f"{tag}st_{u}")
            VC(S, dve, f"{tag}st", u, alone=True)
            for j in range(CT):
                ins = dve.bn_aggr(mv[:, j], st[:, j])
            S.step("dve", ins, f"{tag}mv_{u}")
            VC(S, dve, f"{tag}mv", u)
            S.step("dve", dve.tensor_scalar(rs[:], mv[:, :, 1], eps, None, ALU.add), f"{tag}va_{u}")
            VC(S, pool, f"{tag}va", u)
            S.step("pool", pool.tensor_tensor(out=rs[:], in0=rs[:], in1=mhalf[:, 0:CT], op=ALU.pow), f"{tag}rs_{u}")
            VC(S, dve, f"{tag}rs", u)
            for nm, d in free:
                VC(S, dve, nm, u, d)
            for j in range(CT):
                ins = dve.tensor_scalar(out[:, j], x[:, j], mv[:, j, 0:1], rs[:, j:j + 1], ALU.subtract, ALU.mult)
            S.step("dve", ins, f"{tag}_{u}")

        def route(ctx):
            x = sb(ctx, "rx", [P, CT, D])
            s0 = sb(ctx, "rs0", [P, CT, D])
            f0 = sb(ctx, "rf0", [P, CT, D])
            st, mv, rs = sb(ctx, "rst", [P, CT, 6]), sb(ctx, "rmv", [P, CT, 2]), sb(ctx, "rrs", [P, CT])
            xe = [sb(ctx, f"xe{k}", [P, CT, EXT]) for k in range(2)]
            xT = sb(ctx, "rxT", [P, DH, CH])
            w_kv = sb(ctx, "w_kv", [P, DH, 2 * D])
            b_kv = sb(ctx, "b_kv", [1, 2 * D])
            ones = sb(ctx, "ones", [P, P])
            kg = sb(ctx, "kg", [P, CT, D])
            vg = sb(ctx, "vg", [P, CT, D])
            cs = sb(ctx, "rcs", [P, CT, 2, D])
            kr = sb(ctx, "kr", [P, CT, D])
            kt = sb(ctx, "kt", [P, CT, D])
            kvm = sb(ctx, "kvm", [P, P])
            kvs = sb(ctx, "kvs", [P, 2 * D])
            w_g = sb(ctx, "w_g", [P, DH, NE])
            gb = sb(ctx, "gb", [P, NE])
            lmx = sb(ctx, "lmx", [P, CT])
            lsub = sb(ctx, "lsub", [P, CT, NE])
            lex = sb(ctx, "lex", [P, CT, NE])
            lsum = sb(ctx, "lsum", [P, CT])
            lrec = sb(ctx, "lrec", [P, CT])
            sbx = sb(ctx, "sbx", [P, CT, NX])
            m8 = sb(ctx, "m8", [P, CT, 8])
            mr = sb(ctx, "mr", [P, CT, NX])
            mk = sb(ctx, "mk", [P, CT, NE], BF16)
            mkf = sb(ctx, "mkf", [P, CT, NE])
            macc = sb(ctx, "macc", [P, NE])
            msum = sb(ctx, "msum", [P, NE])
            maccb = sb(ctx, "maccb", [P, NE], BF16)
            tri = sb(ctx, "tri", [P, P], BF16)
            onesb = sb(ctx, "onesb", [P, P], BF16)
            eb = sb(ctx, "eb", [P, NE])
            sv = sb(ctx, "sv", [P, CT, NE])
            sl = sb(ctx, "sl", [P, CT, NE])
            s8 = sb(ctx, "s8", [P, CT, 8])
            s8o = sb(ctx, "s8o", [P, CT, 8])
            idx = [sb(ctx, f"idx{k}", [P, CT, 8], I32) for k in range(2)]
            tok = sb(ctx, "tok", [P, CT])
            ws13 = sb(ctx, "ws13", [P, DH, 2, SI])
            ws2 = sb(ctx, "ws2", [P, NJS, D])
            sg = [sb(ctx, f"sg{k}", [P, CH]) for k in range(2)]
            sh = sb(ctx, "sh", [P, NJS, CH])
            zs = sb(ctx, "zs", [P, CT, D])
            p_tr = ps(ctx, "rp_tr", DH * CH)
            p_k = ps(ctx, "rp_k", 2 * D)
            p_kv = ps(ctx, "rp_kv", 512)
            p_ks = ps(ctx, "rp_ks", 512)
            p_l = ps(ctx, "rp_l", 512)
            p_h = [ps(ctx, f"rp_h{k}", CH) for k in range(2)]

            def load_mix(S, u, c):
                S.load(sp.dma_start(x[:], tiles(x_in[bass.ds(c * CH, CH), :])), f"x_{u}")
                S.load(sp.dma_start(s0[:], tiles(ssm_out[bass.ds(c * CH + CH, CH), :])), f"x_{u}")
                S.load(sp.dma_start(f0[:], tiles(rows(4, chunk_slot(c), CH))), f"x_{u}")

            def front(S, u, k, c):
                VC(S, act, "x", u, 1)
                S.step("act", act.activation(f0[:], f0[:], ACT.Silu), f"sf_{u}")
                VC(S, pool, "sf", u)
                S.step("pool", pool.tensor_tensor(out=s0[:], in0=s0[:], in1=f0[:], op=ALU.mult), f"sm_{u}")
                VC(S, dve, "sm", u)
                S.step("dve", dve.tensor_tensor(out=x[:], in0=x[:], in1=s0[:], op=ALU.add), f"x1_{u}")
                VC(S, dve, "x1", u)
                layer_norm(S, u, x, st, mv, rs, 1e-5, xe[k][:, :, 0:D], (("disp", 1), ("sxn", 2), ("tr", 2)), "ln")
                VC(S, sp, "x1", u)
                S.load(sp.dma_start(tiles(x1_d[bass.ds(c * CH, CH), :]), x[:]), f"sx1_{u}")
                VC(S, sp, "ln", u)
                S.load(sp.dma_start(tiles(xn1_d[bass.ds(c * CH, CH), :]), xe[k][:, :, 0:D]), f"sxn_{u}")

            def turn(S, u, k):
                VC(S, pe, "ln", u)
                VC(S, pe, "zs", u, 1)
                for f in range(DH):
                    for j in range(CT):
                        ins = pe.transpose(p_tr[:, f * CH + j * P:f * CH + (j + 1) * P],
                                           xe[k][:, j, f * P:(f + 1) * P], ident[:])
                S.step("pe", ins, f"tr_{u}")
                VC(S, act, "tr", u)
                VC(S, act, f"sp{NJS - 1}", u)
                VC(S, act, "lg", u)
                VC(S, act, "kp3", u)
                S.step("act", act.activation(xT[:].rearrange("p f t -> p (f t)"), p_tr[:], ACT.Copy), f"xT_{u}")

            def keys(S, u):
                VC(S, pe, "xT", u, 1)
                for j in range(CT):
                    if j == 0:
                        VC(S, pe, "vg3", u, 1)
                    else:
                        VC(S, pe, f"vg{j - 1}", u)
                    for f in range(DH):
                        pe.matmul(p_k[:], xT[:, f, j * P:(j + 1) * P], w_kv[:, f, :], start=(f == 0), stop=False)
                    ins = pe.matmul(p_k[:], ones[0:1, :], b_kv[:], start=False, stop=True)
                    S.step("pe", ins, f"kp{j}_{u}")
                    VC(S, act, f"kp{j}", u)
                    VC(S, act, "kvsum", u, 1)
                    VC(S, act, "krs", u, 1)
                    S.step("act", act.activation(kg[:, j], p_k[:, 0:D], ACT.Gelu), f"kg{j}_{u}")
                    S.step("act", act.activation(vg[:, j], p_k[:, D:2 * D], ACT.Copy), f"vg{j}_{u}")
                VC(S, dve, "kg3", u)
                S.step("dve", dve.tensor_scalar(kg[:], kg[:], KB, None, ALU.add), f"ka_{u}")
                VC(S, dve, "cs", u)
                VC(S, dve, "ka", u)
                rope(S, u, kg[:], cs[:, :, 0], cs[:, :, 1], kr[:], kt[:], ("kvsum", "kr"), "kr")

            def key_sums(S, u):
                VC(S, pe, "ka", u)
                if u == 0:
                    VC(S, pe, "kvst", u, 1)
                for j in range(CT):
                    ins = pe.matmul(p_ks[:, 0:D], ones[:], kg[:, j], start=(u == 0 and j == 0),
                                    stop=(u == CPB - 1 and j == CT - 1))
                S.step("pe", ins, f"ksum_{u}")
                VC(S, pe, "kr", u)
                for j in range(CT):
                    for f in range(DH):
                        fs = slice(f * P, (f + 1) * P)
                        ins = pe.matmul(p_kv[:, fs], kr[:, j, fs], vg[:, j, fs], start=(u == 0 and j == 0 and f == 0),
                                        stop=(u == CPB - 1 and j == CT - 1 and f == DH - 1), skip_group_check=True)
                S.step("pe", ins, f"kvsum_{u}")
                if u == CPB - 1:
                    VC(S, dve, "kvsum", u)
                    VC(S, dve, "kvo", u, CPB)
                    S.step("dve", dve.tensor_tensor(out=kvs[:, 0:D].rearrange("p (f c) -> p f c", f=DH),
                                                    in0=p_kv[:, 0:D].rearrange("p (f c) -> p f c", f=DH),
                                                    in1=kvm[:].unsqueeze(1).to_broadcast([P, DH, P]), op=ALU.mult),
                           f"kvm_{u}")
                    S.step("dve", dve.tensor_scalar(kvs[:, D:2 * D], p_ks[:, 0:D], 1.0 / L, None, ALU.mult),
                           f"kvst_{u}")

            def gate_scores(S, u, k):
                VC(S, pe, "xT", u, 1)
                VC(S, pe, "sl", u, 1)
                for j in range(CT):
                    for f in range(DH):
                        ins = pe.matmul(p_l[:, j * NE:(j + 1) * NE], xT[:, f, j * P:(j + 1) * P], w_g[:, f, :],
                                        start=(f == 0), stop=(f == DH - 1))
                S.step("pe", ins, f"lg_{u}")
                lg = p_l[:, 0:CT * NE].rearrange("p (j e) -> p j e", j=CT)

                def each(t):
                    return t[:].unsqueeze(2).to_broadcast([P, CT, NE])
                VC(S, dve, "lg", u)
                S.step("dve", dve.tensor_reduce(lmx[:], lg, AX.X, ALU.max), f"lmx_{u}")
                VC(S, dve, "lmx", u)
                S.step("dve", dve.tensor_tensor(out=lsub[:], in0=lg, in1=each(lmx), op=ALU.subtract), f"lsub_{u}")
                VC(S, act, "lsub", u)
                VC(S, act, "sc", u, 1)
                S.step("act", act.activation(lex[:], lsub[:], ACT.Exp), f"lex_{u}")
                VC(S, dve, "lex", u)
                S.step("dve", dve.tensor_reduce(lsum[:], lex[:], AX.X, ALU.add), f"lsum_{u}")
                VC(S, dve, "lsum", u)
                S.step("dve", dve.reciprocal(lrec[:], lsum[:]), f"lrec_{u}")
                VC(S, dve, "lrec", u)
                S.step("dve", dve.tensor_tensor(out=xe[k][:, :, D:D + NE], in0=lex[:], in1=each(lrec), op=ALU.mult),
                       f"sc_{u}")
                VC(S, dve, "sc", u)
                S.step("dve", dve.tensor_tensor(out=sbx[:, :, 0:NE], in0=xe[k][:, :, D:D + NE],
                                                in1=gb[:].unsqueeze(1).to_broadcast([P, CT, NE]), op=ALU.add),
                       f"sb_{u}")
                VC(S, dve, "sb", u, alone=True)
                for j in range(CT):
                    ins = dve.max(out=m8[:, j], in_=sbx[:, j])
                S.step("dve", ins, f"m8_{u}")
                VC(S, dve, "m8", u)
                S.step("dve", dve.memset(m8[:, :, TOPK:8], NEG), f"m6_{u}")
                VC(S, dve, "m6", u, alone=True)
                for j in range(CT):
                    ins = dve.match_replace(out=mr[:, j], in_to_replace=m8[:, j], in_values=sbx[:, j],
                                            imm_value=-NEG)
                S.step("dve", ins, f"mr_{u}")
                VC(S, dve, "mr", u)
                VC(S, dve, "pos", u, 1)
                S.step("dve", dve.tensor_scalar(mkf[:], mr[:, :, 0:NE], -NEG, None, ALU.is_ge), f"mkf_{u}")
                VC(S, dve, "mkf", u)
                S.step("dve", dve.tensor_copy(mk[:], mkf[:]), f"mk_{u}")

            def positions(S, u, k):
                S.step("dve", dve.tensor_copy(maccb[:], macc[:]), f"mb_{u}")
                VC(S, pe, "mk", u)
                VC(S, pe, "mb", u)
                VC(S, pe, "lsub", u)
                for j in range(CT):
                    o = p_l[:, j * NE:(j + 1) * NE]
                    pe.matmul(o, tri[:], mk[:, j], start=True, stop=False)
                    for i in range(j):
                        pe.matmul(o, onesb[:], mk[:, i], start=False, stop=False)
                    ins = pe.matmul(o, onesb[:], maccb[:], start=False, stop=True)
                S.step("pe", ins, f"pos_{u}")
                VC(S, dve, "mb", u)
                S.step("dve", dve.tensor_reduce(msum[:], mkf[:].rearrange("p j e -> p e j"), AX.X, ALU.add),
                       f"ms_{u}")
                VC(S, dve, "ms", u)
                S.step("dve", dve.tensor_tensor(out=macc[:], in0=macc[:], in1=msum[:], op=ALU.add), f"ma_{u}")
                pos = p_l[:, 0:CT * NE].rearrange("p (j e) -> p j e", j=CT)
                VC(S, dve, "pos", u)
                S.step("dve", dve.scalar_tensor_tensor(out=sv[:], in0=pos, scalar=float(CAP), in1=mkf[:],
                                                       op0=ALU.is_lt, op1=ALU.mult), f"sv_{u}")
                S.step("dve", dve.tensor_tensor(out=sl[:], in0=pos, in1=eb[:].unsqueeze(1).to_broadcast([P, CT, NE]),
                                                op=ALU.add), f"sl_{u}")
                VC(S, dve, "sl", u)
                VC(S, dve, "ma", u)
                S.step("dve", dve.tensor_tensor(out=sl[:], in0=sl[:], in1=sv[:], op=ALU.mult), f"sw_{u}")
                VC(S, dve, "sw", u, alone=True)
                for j in range(CT):
                    ins = dve.max(out=s8[:, j], in_=sl[:, j])
                S.step("dve", ins, f"s8_{u}")
                VC(S, dve, "s8", u)
                S.step("dve", dve.tensor_scalar(s8o[:], s8[:], 0.0, FAR, ALU.is_equal, ALU.mult), f"so_{u}")
                VC(S, dve, "so", u)
                VC(S, dve, "disp", u, 2)
                S.step("dve", dve.scalar_tensor_tensor(out=idx[k][:], in0=s8[:], scalar=-1.0, in1=s8o[:],
                                                       op0=ALU.add, op1=ALU.add), f"idx_{u}")
                VC(S, dve, "tk", u, 1)
                S.step("dve", dve.tensor_copy(xe[k][:, :, D + NE:EXT], tok[:].unsqueeze(2)), f"tw_{u}")
                VC(S, dve, "tw", u)
                S.step("dve", dve.tensor_scalar(tok[:], tok[:], float(CH), None, ALU.add), f"tk_{u}")
                VC(S, pool, "idx", u)
                VC(S, pool, "tw", u)
                for j in range(CT):
                    for m in range(TOPK):
                        S.load(pool.indirect_dma_start(
                            out=xb_d, out_offset=bass.IndirectOffsetOnAxis(ap=idx[k][:, j, m:m + 1], axis=0),
                            in_=xe[k][:, j], in_offset=None, bounds_check=NE * CAP - 1, oob_is_err=False),
                            f"disp_{u}", soft=True)

            def shared(S, u):
                for j in range(NJS):
                    n, o = BS[j], j * P
                    for q in range(2):
                        if q == 0 and j == 0:
                            VC(S, pe, f"sh{NJS - 1}", u, 1)
                        elif q == 0:
                            VC(S, pe, f"sh{j - 1}", u)
                        for f in range(DH):
                            ins = pe.matmul(p_h[q][0:n, :], ws13[:, f, q, o:o + n], xT[:, f, :], start=(f == 0),
                                            stop=(f == DH - 1))
                    S.step("pe", ins, f"sp{j}_{u}")
                    VC(S, act, f"sp{j}", u)
                    if j == 0:
                        VC(S, act, f"sh{NJS - 1}", u, 1)
                    S.step("act", act.activation(sg[0][0:n, :], p_h[0][0:n, :], ACT.Silu), f"sg{j}_{u}")
                    VC(S, dve, f"sg{j}", u)
                    if j == 0:
                        VC(S, dve, "z", u, 1)
                    S.step("dve", dve.tensor_tensor(out=sh[0:n, j], in0=p_h[1][0:n, :], in1=sg[0][0:n, :],
                                                    op=ALU.mult), f"sh{j}_{u}")
                    if j < NJS - 1:
                        VC(S, act, f"sh{j}", u)

            def shared_out(S, u, c):
                VC(S, pe, f"sh{NJS - 1}", u)
                VC(S, pe, "xT", u)
                for j in range(CT):
                    for i in range(NJS):
                        ins = pe.matmul(p_tr[:, j * D:(j + 1) * D], sh[0:BS[i], i, j * P:(j + 1) * P],
                                        ws2[0:BS[i], i, :], start=(i == 0), stop=(i == NJS - 1))
                S.step("pe", ins, f"z_{u}")
                VC(S, act, "z", u)
                VC(S, act, "sz", u, 1)
                S.step("act", act.activation(zs[:].rearrange("p j d -> p (j d)"), p_tr[:], ACT.Copy), f"zs_{u}")
                VC(S, sp, "zs", u)
                S.load(sp.dma_start(tiles(y_d[bass.ds(c * CH + 1, CH), :]), zs[:]), f"sz_{u}")

            S = Steps(nc, top, book, gate, "route_first", lenient=True)
            S.begin(0)
            w = "weights"
            zx = kg[:].rearrange("p j d -> p (j d)")
            S.step("pool", pool.memset(zx, 0.0), "zx")
            S.wait(sp, "zx")
            for n in range(NE * CAP // (3 * P)):
                S.load(sp.dma_start(xb_d[n * 3 * P:(n + 1) * 3 * P, :].rearrange("(p r) e -> p (r e)", r=3),
                                    zx[:, 0:3 * EXT]), "zero")
            n = NE * CAP // (3 * P) * 3 * P
            S.load(sp.dma_start(xb_d[n:NE * CAP, :].rearrange("(p r) e -> p (r e)", p=P),
                                zx[:, 0:(NE * CAP - n) // P * EXT]), "zero")
            S.load(sp.dma_start(y_d[0:1, :], zrow[0:1, :]), "zero")
            for o, a, b in ((0, "L1_attn_Wk", "L1_attn_bk"), (D, "L1_attn_Wv", "L1_attn_bv")):
                S.load(sp.dma_start(w_kv[:, :, o:o + D], A[a].rearrange("(c p) n -> p c n", p=P)), w)
                S.load(sp.dma_start(b_kv[:, o:o + D], A[b].unsqueeze(0)), w)
            S.load(sp.dma_start(w_g[:], A["L1_ffn_gate_w"].rearrange("(c p) n -> p c n", p=P)), w)
            S.load(sp.dma_start(gb[:], A["L1_ffn_gate_b"].unsqueeze(0).to_broadcast([P, NE])), w)
            for q, a in enumerate(("L1_ffn_ws1", "L1_ffn_ws3")):
                S.load(sp.dma_start(ws13[:, :, q, :], A[a].rearrange("(c p) n -> p c n", p=P)), w)
            for j in range(NJS):
                S.load(sp.dma_start(ws2[0:BS[j], j, :], A["L1_ffn_ws2"][j * P:j * P + BS[j], :]), w)
            S.load(sp.dma_start(kvm[:], A["c_blocks"]), w)
            S.step("pool", pool.memset(ones[:], 1.0), "ones")
            S.step("pool", pool.memset(onesb[:], 1.0), "onesb")
            S.step("pool", pool.memset(macc[:], 0.0), "macc")
            S.step("pool", pool.memset(sbx[:], NEG), "sbx")
            S.wait(pool, "onesb")
            S.step("pool", pool.affine_select(out=tri[:], in_=onesb[:], compare_op=ALU.is_gt, fill=0.0, base=0,
                                              pattern=[[1, P]], channel_multiplier=-1), "tri")
            S.step("pool", pool.iota(idx[0][:, :, 0:1], [[P, CT]], base=1, channel_multiplier=1), "toki")
            S.step("pool", pool.iota(idx[1][:].rearrange("p j e -> p (j e)"), [[CAP, 32]], base=1,
                                     channel_multiplier=0), "ebi")
            S.wait(dve, "ebi")
            S.step("dve", dve.tensor_copy(tok[:], idx[0][:, :, 0]), "tok")
            S.step("dve", dve.tensor_copy(eb[:, 0:32], idx[1][:].rearrange("p j e -> p (j e)")), "eb0")
            S.step("dve", dve.tensor_scalar(eb[:, 32:64], idx[1][:].rearrange("p j e -> p (j e)"), float(32 * CAP),
                                            None, ALU.add), "eb1")
            load_mix(S, CPB - 2, 0)
            S.load(sp.dma_start(cs[:], A["c_rope"][0:CH, :].rearrange("(j p) (a d) -> p j a d", p=P, a=2)), "cs0")
            front(S, CPB - 1, 0, 0)
            turn(S, CPB - 1, 0)
            S.wait(sp, f"sx1_{CPB - 1}")
            S.wait(sp, f"ln_{CPB - 1}")
            load_mix(S, CPB - 1, 1)
            S.close()
            S.done(1)

            S = Steps(nc, top, book, gate, "route", scrap=(scrap[0:4, :], zrow[0:1, :]))
            with nc.Fori(0, B) as i:
                S.begin(i)
                for u in range(CPB):
                    c, k = i * CPB + u, u % 2
                    VC(S, sp, "krs", u, 1)
                    S.load(sp.dma_start(cs[:], A["c_rope"][u * CH:(u + 1) * CH, :].rearrange(
                        "(j p) (a d) -> p j a d", p=P, a=2)), f"cs_{u}")
                    gate_scores(S, u, k)
                    keys(S, u)
                    positions(S, u, k)
                    shared(S, u)
                    front(S, u, (u + 1) % 2, (c + 1) % NC)
                    key_sums(S, u)
                    turn(S, u, (u + 1) % 2)
                    shared_out(S, u, c)
                    VC(S, sp, "sx1", u)
                    VC(S, sp, "ln", u)
                    load_mix(S, u, (c + 2) % NC)
                    if u == CPB - 1:
                        VC(S, sp, "kvst", u)
                        S.load(sp.dma_start(kv_d[bass.ds(i * P, P), :], kvs[:]), f"kvo_{u}")
                S.close()
            S.done(B)

        with ExitStack() as ctx:
            route(ctx)

        def experts(ctx):
            EB, U = EI // 2, 2
            xs_ = [sb(ctx, f"ex{k}", [P, EXT]) for k in range(U)]
            wt = [sb(ctx, f"ewt{k}", [P, 1]) for k in range(U)]
            w13 = [sb(ctx, f"ew13{k}", [P, DH, 2, EI]) for k in range(U)]
            w2 = [sb(ctx, f"ew2{k}", [EB, 2, D]) for k in range(U)]
            xT = [sb(ctx, f"exT{k}", [P, DH, P]) for k in range(U)]
            sg = [sb(ctx, f"esg{k}", [EB, 2, P]) for k in range(U)]
            hd = [sb(ctx, f"ehd{k}", [EB, 2, P]) for k in range(U)]
            yb = [sb(ctx, f"eyb{k}", [P, D]) for k in range(U)]
            far = [sb(ctx, f"efar{k}", [P, 1]) for k in range(U)]
            idx = [sb(ctx, f"eidx{k}", [P, 1], I32) for k in range(U)]
            p_t = [ps(ctx, f"ep_t{k}", 512) for k in range(U)]
            p_g = [ps(ctx, f"ep_g{k}", 512) for k in range(U)]
            p_u = [ps(ctx, f"ep_u{k}", 512) for k in range(U)]
            p_y = [ps(ctx, f"ep_y{k}", 512) for k in range(U)]
            S = Steps(nc, top, book, gate, "experts", scrap=(scrap[4:8, :], zrow[0:1, :]))
            w1f, w3f = (A[n].rearrange("e d i -> (e d) i") for n in ("L1_ffn_w1", "L1_ffn_w3"))
            w2f = A["L1_ffn_w2"].rearrange("e i d -> (e i) d")

            def W(eng, name, k, back=0, alone=False):
                S.wait(eng, f"{name}{k}", back=back, alone=alone)
            with nc.Fori(0, NE // U) as i:
                S.begin(i)
                for k in range(U):
                    e = i * U + k
                    W(sp, "xT", k, 1)
                    W(sp, "idx", k, 1)
                    W(sp, "yb", k, 1)
                    S.load(sp.dma_start(xs_[k][:], xb_d[bass.ds(e * CAP, CAP), :]), f"x{k}")
                    S.load(sp.dma_start(w13[k][:, :, 0, :], w1f[bass.ds(e * D, D), :].rearrange("(c p) i -> p c i", p=P)),
                           f"w{k}")
                    S.load(sp.dma_start(w13[k][:, :, 1, :], w3f[bass.ds(e * D, D), :].rearrange("(c p) i -> p c i", p=P)),
                           f"w{k}")
                    S.load(sp.dma_start(w2[k][:], w2f[bass.ds(e * EI, EI), :].rearrange("(c p) d -> p c d", p=EB)),
                           f"w{k}")
                    S.load(sp.dma_start(wt[k][:], xb_d[bass.ds(e * CAP, CAP), bass.ds(e + D, 1)],
                                        allow_slow_non_contiguous=True), f"wt{k}")
                for k in range(U):
                    W(pe, "x", k)
                    W(pe, "xT", k, 1)
                    for f in range(DH):
                        ins = pe.transpose(p_t[k][:, f * P:(f + 1) * P], xs_[k][:, f * P:(f + 1) * P], ident[:])
                    S.step("pe", ins, f"tr{k}")
                    W(act, "tr", k)
                    W(act, "up", k, 1)
                    S.step("act", act.activation(xT[k][:].rearrange("p f t -> p (f t)"), p_t[k][:, 0:D], ACT.Copy),
                           f"xT{k}")
                    W(dve, "x", k)
                    W(dve, "add", k, 1)
                    S.step("dve", dve.tensor_scalar(far[k][:], xs_[k][:, D + NE:EXT], 0.0, FAR, ALU.is_equal, ALU.mult),
                           f"far{k}")
                    W(dve, "far", k)
                    S.step("dve", dve.tensor_tensor(out=idx[k][:], in0=xs_[k][:, D + NE:EXT], in1=far[k][:],
                                                    op=ALU.add), f"idx{k}")
                for k in range(U):
                    W(pe, "xT", k)
                    W(pe, "w", k)
                    W(pe, "hd", k, 1)
                    for q, dst in ((0, p_g[k]), (1, p_u[k])):
                        for b in range(2):
                            for f in range(DH):
                                ins = pe.matmul(dst[0:EB, b * P:(b + 1) * P], w13[k][:, f, q, b * EB:(b + 1) * EB],
                                                xT[k][:, f, :], start=(f == 0), stop=(f == DH - 1))
                    S.step("pe", ins, f"up{k}")
                    W(act, "up", k)
                    W(act, "hd", k, 1)
                    S.step("act", act.activation(sg[k][:].rearrange("p b t -> p (b t)"), p_g[k][0:EB, 0:2 * P],
                                                 ACT.Silu), f"sg{k}")
                    W(dve, "sg", k)
                    W(dve, "dn", k, 1)
                    S.step("dve", dve.tensor_tensor(out=hd[k][:].rearrange("p b t -> p (b t)"),
                                                    in0=p_u[k][0:EB, 0:2 * P],
                                                    in1=sg[k][:].rearrange("p b t -> p (b t)"), op=ALU.mult), f"hd{k}")
                for k in range(U):
                    W(pe, "hd", k)
                    W(pe, "yb", k, 1)
                    for b in range(2):
                        ins = pe.matmul(p_y[k][:, 0:D], hd[k][:, b, :], w2[k][:, b, :], start=(b == 0), stop=(b == 1))
                    S.step("pe", ins, f"dn{k}")
                    W(dve, "dn", k)
                    W(dve, "wt", k)
                    W(dve, "add", k, 1)
                    S.step("dve", dve.tensor_scalar(yb[k][:], p_y[k][:, 0:D], wt[k][:], None, ALU.mult), f"yb{k}")
                    W(pool, "yb", k)
                    W(pool, "idx", k)
                    W(pool, "add", 1 - k, 1 if k == 0 else 0)
                    S.load(pool.indirect_dma_start(out=y_d, out_offset=bass.IndirectOffsetOnAxis(ap=idx[k][:], axis=0),
                                                   in_=yb[k][:], in_offset=None, bounds_check=T, oob_is_err=False,
                                                   compute_op=ALU.add), f"add{k}", soft=True)
                S.close()
            S.done(NE // U)

        with ExitStack() as ctx:
            experts(ctx)

        def final(ctx):
            xn = [sb(ctx, f"fxn{k}", [P, CT, D]) for k in range(2)]
            x1 = [sb(ctx, f"fx1{k}", [P, CT, D]) for k in range(2)]
            ym = [sb(ctx, f"fym{k}", [P, CT, D]) for k in range(2)]
            cs = sb(ctx, "fcs", [P, CT, 2, D])
            kv = sb(ctx, "fkv", [P, 2 * D])
            xT = sb(ctx, "fxT", [P, DH, CH])
            w_q = sb(ctx, "w_q", [P, DH, D])
            b_q = sb(ctx, "b_q", [1, D])
            ones = sb(ctx, "fones", [1, P])
            gam, bet = sb(ctx, "gam", [P, D]), sb(ctx, "bet", [P, D])
            qg = [sb(ctx, f"qg{k}", [P, CT, D]) for k in range(2)]
            qr = [sb(ctx, f"qr{k}", [P, CT, D]) for k in range(2)]
            qt = sb(ctx, "qt", [P, CT, D])
            qrT = sb(ctx, "qrT", [P, DH, CH])
            zt = sb(ctx, "zt", [P, CT, D])
            zz = sb(ctx, "zz", [P, CT * HA])
            rz = sb(ctx, "rz", [P, CT * HA])
            o = sb(ctx, "fo", [P, CT, D])
            s1 = sb(ctx, "fs1", [P, CT, D])
            st, mv, rs = sb(ctx, "fst", [P, CT, 6]), sb(ctx, "fmv", [P, CT, 2]), sb(ctx, "frs", [P, CT])
            p_tr = ps(ctx, "fp_tr", DH * CH)
            p_q = ps(ctx, "fp_q", CT * D)
            p_t2 = ps(ctx, "fp_t2", DH * CH)
            p_o = ps(ctx, "fp_o", CT * D)

            def loads(S, u, c, pos, k):
                cc = bass.ds(c * CH, CH)
                S.load(sp.dma_start(xn[k][:], tiles(xn1_d[cc, :])), f"xn_{u}")
                S.load(sp.dma_start(x1[k][:], tiles(x1_d[cc, :])), f"x1_{u}")
                S.load(sp.dma_start(ym[k][:], tiles(y_d[bass.ds(c * CH + 1, CH), :])), f"ym_{u}")
                VC(S, sp, "qrs", u, 1)
                S.load(sp.dma_start(cs[:], A["c_rope"][pos * CH:(pos + 1) * CH, :].rearrange(
                    "(j p) (a d) -> p j a d", p=P, a=2)), f"cs_{u}")

            def queries(S, u, k):
                VC(S, pe, "xn", u)
                VC(S, pe, "xT", u, 1)
                for f in range(DH):
                    for j in range(CT):
                        ins = pe.transpose(p_tr[:, f * CH + j * P:f * CH + (j + 1) * P],
                                           xn[k][:, j, f * P:(f + 1) * P], ident[:])
                S.step("pe", ins, f"tr_{u}")
                VC(S, act, "tr", u)
                VC(S, act, "qp", u, 1)
                S.step("act", act.activation(xT[:].rearrange("p f t -> p (f t)"), p_tr[:], ACT.Copy), f"xT_{u}")
                VC(S, pe, "xT", u)
                VC(S, pe, "qg", u, 1)
                for j in range(CT):
                    dst = p_q[:, j * D:(j + 1) * D]
                    for f in range(DH):
                        pe.matmul(dst, xT[:, f, j * P:(j + 1) * P], w_q[:, f, :], start=(f == 0), stop=False)
                    ins = pe.matmul(dst, ones[0:1, :], b_q[:], start=False, stop=True)
                S.step("pe", ins, f"qp_{u}")
                VC(S, act, "qp", u)
                VC(S, act, "zt", u, 1)
                S.step("act", act.activation(qg[k][:].rearrange("p j d -> p (j d)"), p_q[:], ACT.Gelu), f"qg_{u}")
                VC(S, dve, "qg", u)
                S.step("dve", dve.tensor_scalar(qg[k][:], qg[k][:], KB, None, ALU.add), f"qa_{u}")
                VC(S, dve, "cs", u)
                VC(S, dve, "qa", u)
                rope(S, u, qg[k][:], cs[:, :, 0], cs[:, :, 1], qr[k][:], qt[:], ("t2", "qr"), "qr")

            def attend(S, u, k, c):
                VC(S, pe, "qr", u, 1)
                VC(S, pe, "qrT", u, 1)
                for f in range(DH):
                    for j in range(CT):
                        ins = pe.transpose(p_t2[:, f * CH + j * P:f * CH + (j + 1) * P],
                                           qr[k][:, j, f * P:(f + 1) * P], ident[:])
                S.step("pe", ins, f"t2_{u}")
                VC(S, act, "t2", u)
                VC(S, act, "o", u, 1)
                S.step("act", act.activation(qrT[:].rearrange("p f t -> p (f t)"), p_t2[:], ACT.Copy), f"qrT_{u}")
                VC(S, pe, "qrT", u)
                if u == 0:
                    VC(S, pe, "kv", u)
                VC(S, pe, "os", u, 1)
                for j in range(CT):
                    for f in range(DH):
                        at = j * D + f * P
                        ins = pe.matmul(p_o[:, at:at + P], qrT[:, f, j * P:(j + 1) * P], kv[:, f * P:(f + 1) * P],
                                        start=True, stop=True)
                S.step("pe", ins, f"o_{u}")
                if u == 0:
                    VC(S, dve, "kv", u)
                VC(S, dve, "qa", u, 1)
                S.step("dve", dve.tensor_tensor(out=zt[:], in0=qg[k][:],
                                                in1=kv[:, D:2 * D].unsqueeze(1).to_broadcast([P, CT, D]),
                                                op=ALU.mult), f"zt_{u}")
                VC(S, dve, "zt", u)
                S.step("dve", dve.tensor_reduce(zz[:], zt[:].rearrange("p j (h c) -> p (j h) c", c=DA), AX.X, ALU.add),
                       f"zz_{u}")
                VC(S, dve, "zz", u)
                S.step("dve", dve.tensor_scalar(zz[:], zz[:], 1e-6, None, ALU.add), f"ze_{u}")
                VC(S, dve, "ze", u)
                S.step("dve", dve.reciprocal(rz[:], zz[:]), f"rz_{u}")
                VC(S, dve, "rz", u)
                VC(S, dve, "o", u)
                VC(S, dve, "fin", u, 1)
                S.step("dve", dve.tensor_tensor(out=o[:].rearrange("p j (h c) -> p (j h) c", c=DA),
                                                in0=p_o[:].rearrange("p (h c) -> p h c", c=DA),
                                                in1=rz[:].unsqueeze(2).to_broadcast([P, CT * HA, DA]), op=ALU.mult),
                       f"os_{u}")
                VC(S, pool, "os", u)
                S.step("pool", pool.tensor_tensor(out=o[:], in0=o[:], in1=xn[k][:], op=ALU.add), f"re_{u}")
                VC(S, act, "ym", u, 1)
                S.step("act", act.activation(ym[k][:], ym[k][:], ACT.Silu), f"sy_{u}")
                VC(S, dve, "re", u)
                layer_norm(S, u, o, st, mv, rs, 1e-12, s1, (("out", 1),), "ln")
                VC(S, pool, "ln", u)
                S.step("pool", pool.tensor_tensor(out=s1[:], in0=s1[:], in1=gam[:].unsqueeze(1).to_broadcast([P, CT, D]),
                                                  op=ALU.mult), f"ga_{u}")
                VC(S, pool, "ga", u)
                S.step("pool", pool.tensor_tensor(out=s1[:], in0=s1[:], in1=bet[:].unsqueeze(1).to_broadcast([P, CT, D]),
                                                  op=ALU.add), f"be_{u}")
                VC(S, dve, "be", u)
                VC(S, dve, "sy", u)
                S.step("dve", dve.tensor_tensor(out=s1[:], in0=s1[:], in1=ym[k][:], op=ALU.mult), f"sy1_{u}")
                VC(S, dve, "sy1", u)
                VC(S, dve, "x1", u, 1)
                S.step("dve", dve.tensor_tensor(out=s1[:], in0=s1[:], in1=x1[k][:], op=ALU.add), f"fin_{u}")
                VC(S, sp, "fin", u)
                S.load(sp.dma_start(tiles(out_rows[bass.ds(c * CH, CH), :]), s1[:]), f"out_{u}")

            S = Steps(nc, top, book, gate, "final_first", lenient=True)
            S.begin(0)
            w = "weights"
            S.load(sp.dma_start(w_q[:], A["L1_attn_Wq"].rearrange("(c p) n -> p c n", p=P)), w)
            S.load(sp.dma_start(b_q[:], A["L1_attn_bq"].unsqueeze(0)), w)
            S.load(sp.dma_start(gam[:], A["L1_attn_gamma"].unsqueeze(0).to_broadcast([P, D])), w)
            S.load(sp.dma_start(bet[:], A["L1_attn_beta"].unsqueeze(0).to_broadcast([P, D])), w)
            S.step("dve", dve.memset(ones[:], 1.0), "ones")
            S.wait(pe, w)
            S.wait(pe, "ones")
            loads(S, CPB - 1, 0, 0, 0)
            queries(S, CPB - 1, 0)
            S.close()
            S.done(1)
            S = Steps(nc, top, book, gate, "final")
            with nc.Fori(0, B) as i:
                S.begin(i)
                for u in range(CPB):
                    c, k = i * CPB + u, u % 2
                    if u == 0:
                        VC(S, sp, "zt", u, 1)
                        VC(S, sp, "o", u, 1)
                        S.load(sp.dma_start(kv[:], kv_d[bass.ds(i * P, P), :]), "kv_0")
                    VC(S, sp, "fin", u, 1)
                    loads(S, u, (c + 1) % NC, (u + 1) % CPB, (u + 1) % 2)
                    queries(S, u, (u + 1) % 2)
                    attend(S, u, k, c)
                S.close()
            S.done(B)

        with ExitStack() as ctx:
            final(ctx)


def _constants():
    half = np.arange(0, DK, 2, dtype=np.float32)
    inv = (1.0 / 10000.0 ** (half / DK)).astype(np.float32)
    t = np.arange(L, dtype=np.float32)
    f = (t[:, None] * inv[None, :]).astype(np.float32)
    f = np.concatenate([f, f], axis=-1)
    base = ((half + np.float32(0.4 * DK)) / np.float32(1.4 * DK)).astype(np.float32)
    scale = base[None, :] ** ((t - L // 2) / np.float32(P // 2)).astype(np.float32)[:, None]
    scale = np.concatenate([scale, scale], axis=-1)
    cos, sin = np.cos(f), np.sin(f)
    sgn = np.concatenate([-np.ones(DK // 2), np.ones(DK // 2)])
    tab = np.concatenate([cos * scale, sgn * sin * scale, cos / scale, sgn * sin / scale], axis=-1)
    a, c = np.arange(P)[:, None], np.arange(P)[None, :]
    mask = np.zeros((WPB, P, 2 * P), np.float32)
    mask[:, :, 0:P] = np.where(c >= a, 0.0, NEG)
    mask[0, :, 0:P] = NEG
    mask[:, :, P:] = np.where(c <= a, 0.0, NEG)
    sel = np.broadcast_to((np.arange(96)[:, None] % 32 == np.arange(32)[None, :])[:, :, None], (96, 32, P))
    inv = (1.0 / 10000.0 ** (np.arange(0, D, 2, dtype=np.float32) / D)).astype(np.float32)
    ang = np.repeat((t[:, None] * inv).astype(np.float32), 2, axis=1)
    rope = np.concatenate([np.cos(ang), np.sin(ang) * np.tile([-1.0, 1.0], D // 2)], axis=1)
    blocks = (np.arange(P)[:, None] // 16 == np.arange(P)[None, :] // 16) / float(L)
    return {"c_rope": rope.astype(np.float32), "c_blocks": blocks.astype(np.float32), "c_select": sel.astype(mybir.dt.np(BF16)),
            "c_rotary": tab.astype(np.float32).reshape(WPB, P, 4 * DK),
            "c_mask": mask.astype(mybir.dt.np(BF16))}


def kernel(**inputs):
    import concourse.bacc as bacc
    from concourse.bass_utils import run_bass_kernel_spmd

    arrays = dict(inputs)
    for name in TRANSPOSED:
        arrays[name] = np.swapaxes(np.asarray(arrays[name]), -1, -2)
    arrays.update(_constants())
    arrays = {k: np.ascontiguousarray(v) for k, v in arrays.items()}

    book = {}
    for _ in range(2):
        nc = bacc.Bacc("TRN2", target_bir_lowering=False, num_devices=1)
        A = {k: nc.dram_tensor(f"in_{k}", v.shape, mybir.dt.from_np(v.dtype), kind="ExternalInput").ap()
             for k, v in arrays.items()}
        out = nc.dram_tensor("out_0", (B, L, D), F32, kind="ExternalOutput").ap()
        program(nc, A, out, book)
    r = run_bass_kernel_spmd(nc, [{f"in_{k}": v for k, v in arrays.items()}], core_ids=[0])
    return r.results[0]["out_0"]
```

```python
from contextlib import ExitStack

import numpy as np

import concourse.bass as bass
from concourse import mybir
from concourse.alu_op_type import AluOpType as ALU

F32 = mybir.dt.float32
BF16 = mybir.dt.bfloat16
I32 = mybir.dt.int32
ACT = mybir.ActivationFunctionType
AX = mybir.AxisListType

P = 128
B, L, D = 4, 2048, 256
T = B * L
NT = T // P
WPB = L // P
CH = 512
CT = CH // P
NC = T // CH
DH = D // P
NL = 2
H, DK = 8, 64
INNER = H * DK
HID = int(D * 4 * 2 / 3)
NJ = -(-HID // P)
QK_SCALE = 8.0
TRANSPOSED = ("L0_attn_in_proj_w", "L0_attn_x_proj_w", "L0_attn_dt_proj_w", "L0_attn_out_proj_w", "L1_attn_Wq",
              "L1_attn_Wk", "L1_attn_Wv", "L1_ffn_gate_w", "L1_ffn_w1", "L1_ffn_w2", "L1_ffn_w3", "L1_ffn_ws1",
              "L1_ffn_ws2", "L1_ffn_ws3")
NEG = -1.0e30

SLOTS = 70
NS = 5


def tile_slot(t):
    return t + (t + WPB) // WPB + 1


def chunk_slot(c):
    return c * CT + c // (WPB // CT) + 2


class Steps:

    def __init__(self, nc, ctx, book, gate, name, lenient=False, scrap=None):
        self.nc, self.name, self.n, self.lenient = nc, name, 0, lenient
        self.ctx, self.free = ctx, gate["free"]
        self.book = book.setdefault(name, {"order": {}, "per_pass": {}, "soft": set()})
        self.count, self.sems, self.waited = {}, {}, {}
        self.gate = gate
        self.base = {}
        for who, k in self.book["per_pass"].items():
            kind = who if who in self.book["soft"] else who.split("_")[0]
            if self.free.get(kind):
                self.sems[who], self.base[who] = self.free[kind].pop()
            else:
                self.sems[who], self.base[who] = ctx.enter_context(nc.semaphore(f"{name}_{who}")), 0
            if who in self.book["soft"]:
                row = len([w for w in self.sems if w in self.book["soft"]])
                nc.gpsimd.dma_start(scrap[0][row - 1:row, :], scrap[1]).then_inc(self.sems[who], 16)
            else:
                nc.sync.sem_inc(self.sems[who], k)
        if self.sems:
            for eng in (nc.tensor, nc.scalar, nc.vector, nc.gpsimd):
                for who, k in self.book["per_pass"].items():
                    eng.wait_ge(self.sems[who], self.base[who] + (16 if who in self.book["soft"] else k))

    def begin(self, n):
        self.n, self.count, self.waited = n, {}, {}

    def _who(self, eng):
        nc = self.nc
        return {id(nc.tensor): "pe", id(nc.scalar): "act", id(nc.vector): "dve", id(nc.gpsimd): "pool",
                id(nc.sync): "sp"}[id(eng)]

    def step(self, who, ins, name):
        o = self.count[who] = self.count.get(who, 0) + 1
        assert name not in self.book["order"] or self.book["order"][name] == (who, o), name
        self.book["order"][name] = (who, o)
        if who in self.sems:
            ins.then_inc(self.sems[who], 1)

    def load(self, ins, name, soft=False):
        who = "dma_" + name
        if soft:
            self.book["soft"].add(who)
        self.count[who] = self.count.get(who, 0) + 16
        self.book["order"][name] = (who, self.count[who])
        if who in self.sems:
            ins.then_inc(self.sems[who], 16)

    def wait(self, eng, name, back=0, alone=False):
        if not self.sems or (self.lenient and name not in self.book["order"]):
            return
        who, o = self.book["order"][name]
        k = self.book["per_pass"][who]
        at = o - back * k
        key = (self._who(eng), who)
        if self.waited.get(key, -10**9) >= at:
            return
        self.waited[key] = at
        if who in self.book["soft"]:
            assert at in (0, k), name
            eng.wait_ge(self.sems[who], self.n * k + at + 16)
        else:
            eng.wait_ge(self.sems[who], (self.n + 1) * k + (self.base[who] + at))
        if alone or eng is self.nc.gpsimd or eng is self.nc.sync:
            eng.sem_inc(self.gate[self._who(eng)], 1)

    def close(self):
        for who, k in self.count.items():
            assert self.book["per_pass"].get(who, k) == k, (self.name, who)
            self.book["per_pass"][who] = k

    def done(self, passes, engines=None):
        nc = self.nc
        for eng in engines or (nc.tensor, nc.scalar, nc.vector, nc.gpsimd, nc.sync):
            for who, sem in self.sems.items():
                k = self.book["per_pass"][who]
                eng.wait_ge(sem, passes * k + (16 if who in self.book["soft"] else k + self.base[who]))
                if not isinstance(passes, int):
                    eng.sem_inc(self.gate[self._who(eng)], 1)
        if isinstance(passes, int):
            for who, sem in self.sems.items():
                if who not in self.book["soft"]:
                    end = self.base[who] + (passes + 1) * self.book["per_pass"][who]
                    self.free.setdefault(who.split("_")[0], []).append((sem, end))


def program(nc, A, out, book):
    pe, act, dve, pool, sp = nc.tensor, nc.scalar, nc.vector, nc.gpsimd, nc.sync
    top = ExitStack()
    xs = nc.dram_tensor("stream", [NS * SLOTS * P, D], F32).ap()
    tabs = nc.dram_tensor("rotary_tables", [NL * WPB * P, 4 * DK], F32).ap()
    scrap = nc.dram_tensor("scrap", [12, 256], F32).ap()
    out_rows = out.rearrange("b t d -> (b t) d")

    def sb(ctx, name, shape, dt=F32):
        return ctx.enter_context(nc.sbuf_tensor(name, shape, dt))

    def ps(ctx, name, cols):
        return ctx.enter_context(nc.psum_tensor(name, [P, cols], F32))

    def rows(stage, slot, n, shift=0):
        return xs[bass.ds((stage * SLOTS + slot) * P + shift, n), :]

    with top:
        gate = {w: top.enter_context(nc.semaphore("gate_" + w)) for w in ("pe", "act", "dve", "pool", "sp")}
        gate["free"] = {}
        ident = sb(top, "ident", [P, P])
        identb = sb(top, "identb", [P, P], BF16)
        mhalf = sb(top, "mhalf", [P, 2 * H])
        zrow = sb(top, "zrow", [P, D])

        with ExitStack() as ctx:
            S = Steps(nc, top, book, gate, "setup")
            base = sb(ctx, "base_tab", [P, WPB, 4 * DK])
            fac = sb(ctx, "scale_fac", [P, NL, 4 * DK])
            ltab = sb(ctx, "layer_tab", [P, NL, WPB, 4 * DK])
            S.step("pool", pool.memset(ident[:], 0.0), "id0")
            S.step("pool", pool.memset(identb[:], 0.0), "idb0")
            S.step("pool", pool.memset(mhalf[:], -0.5), "mhalf")
            S.step("pool", pool.memset(zrow[:], 0.0), "zrow")
            S.wait(pool, "idb0")
            for m, nm in ((ident, "id1"), (identb, "idb1")):
                S.step("pool", pool.affine_select(out=m[:], in_=m[:], compare_op=ALU.not_equal, fill=1.0, base=0,
                                                  pattern=[[-1, P]], channel_multiplier=1), nm)
            S.load(sp.dma_start(base[:], A["c_rotary"].rearrange("w p c -> p w c")), "base")
            hk = DK // 2
            for l in range(NL):
                for q, nm in enumerate(("L0_ffn_q_scale", "L0_ffn_k_scale")):
                    s = A[nm][l:l + 1, :]
                    o = 2 * q * DK
                    for dst, src in ((o, s), (o + DK, s[:, hk:DK]), (o + DK + hk, s[:, 0:hk])):
                        w = src.shape[1]
                        S.load(sp.dma_start(fac[:, l, dst:dst + w], src.to_broadcast([P, w])), "fac")
            S.wait(dve, "base")
            S.wait(dve, "fac")
            for l in range(NL):
                S.step("dve", dve.tensor_tensor(out=ltab[:, l], in0=base[:],
                                                in1=fac[:, l:l + 1, :].to_broadcast([P, WPB, 4 * DK]), op=ALU.mult),
                       f"ltab{l}")
            S.wait(sp, "zrow")
            for s in range(NS - 1):
                for b in range(B):
                    S.load(sp.dma_start(rows(s, tile_slot(b * WPB), 1, -1), zrow[0:1, :]), "zeros")
            S.wait(sp, f"ltab{NL - 1}")
            for l in range(NL):
                S.load(sp.dma_start(tabs[l * L:(l + 1) * L, :].rearrange("(w p) c -> p w c", p=P),
                                   ltab[:, l]), "tabs")
            S.close()
            S.done(1)

        x_in = A["L0_attn_hidden_states"].rearrange("b t d -> (b t) d")

        RING = 4
        SA0 = Steps(nc, top, book, gate, "attn_first", lenient=True)
        SA = Steps(nc, top, book, gate, "attn")
        SA1 = Steps(nc, top, book, gate, "attn_last", lenient=True)
        hk = DK // 2

        def layer_rows(name, l, n):
            return A[name].rearrange("l r n -> (l r) n")[bass.ds(l * n, n), :]

        def attention(l, actx):
            wqkv = sb(actx, "wqkv", [P, DH, 3 * INNER])
            wo = sb(actx, "wo", [P, INNER // P, D])
            hx = [sb(actx, f"hx{k}", [P, D]) for k in range(2)]
            tab = [sb(actx, f"tab{k}", [P, 4, DK]) for k in range(2)]
            msk = [sb(actx, f"msk{k}", [P, 2 * P], BF16) for k in range(2)]
            res = [sb(actx, f"res{k}", [P, D]) for k in range(2)]
            xo = [sb(actx, f"xo{k}", [P, D]) for k in range(2)]
            hT = sb(actx, "hT", [P, DH, P])
            sq = sb(actx, "sq", [P, 2 * INNER])
            n2 = [sb(actx, f"n2{k}", [P, 2 * H]) for k in range(2)]
            rn = [sb(actx, f"rn{k}", [P, 2 * H]) for k in range(2)]
            qsc = [sb(actx, f"qsc{u}", [P, H]) for u in range(RING)]
            rc = sb(actx, "rot_cos", [P, 2 * INNER])
            rsn = sb(actx, "rot_sin", [P, 2 * INNER])
            qkT = [sb(actx, f"qkT{u}", [P, 2 * INNER]) for u in range(RING)]
            vv = [sb(actx, f"v{u}", [P, INNER]) for u in range(RING)]
            prob = sb(actx, "prob", [P, H // 2, 2, P])
            probT = sb(actx, "probT", [P, H // 2, 2, P])
            mx = sb(actx, "mx", [P, H])
            nb = sb(actx, "nb", [P, H])
            den = [sb(actx, f"den{k}", [P, H]) for k in range(2)]
            rden = sb(actx, "rden", [P, H])
            o_sb = sb(actx, "o_sb", [P, INNER])
            oT = sb(actx, "oT", [P, INNER])
            p_qk = ps(actx, "p_qk", 2 * INNER)
            p_v = ps(actx, "p_v", INNER)
            p_s = ps(actx, "p_s", 2 * INNER)
            p_t = ps(actx, "p_t", 2 * INNER)
            p_o = ps(actx, "p_o", INNER)

            def V(S, eng, name, u, d=0):
                v = u - d
                S.wait(eng, f"{name}{v % RING}", back=1 if v < 0 else 0)

            def load_tile(S, u, t, l):
                k = (u + 1) % 2
                slot = tile_slot(t)
                S.load(sp.dma_start(hx[k][:, 0:P], rows(2 * l, slot, P)[:, 0:P]), f"hx{u}")
                S.load(sp.dma_start(hx[k][:, P:D], rows(2 * l, slot, P, -1)[:, P:D]), f"hx{u}")
                S.load(sp.dma_start(tab[k][:].rearrange("p a c -> p (a c)"),
                                    tabs[bass.ds((l * WPB + t % WPB) * P, P), :]), f"tab{u}")

            def load_mask(S, u, t):
                S.load(sp.dma_start(msk[(u + 1) % 2][:],
                                    A["c_mask"].rearrange("w p c -> (w p) c")[bass.ds((t % WPB) * P, P), :]), f"msk{u}")

            def front_tile(S, u, k):
                V(S, pe, "hx", u, 1)
                V(S, pe, "v_ev", u, 1)
                for c in range(DH):
                    ins = pe.transpose(p_v[:, c * P:(c + 1) * P], hx[k][:, c * P:(c + 1) * P], ident[:])
                S.step("pe", ins, f"hT{u}")
                V(S, act, "hT", u)
                V(S, act, "v", u, 1)
                S.step("act", act.activation(hT[:].rearrange("p c t -> p (c t)"), p_v[:, 0:D], ACT.Copy), f"hT_ev{u}")

            def front_qk(S, u):
                V(S, pe, "hT_ev", u)
                V(S, pe, "qkT_ev", u)
                for n in range(2):
                    for c in range(DH):
                        ins = pe.matmul(p_qk[:, n * INNER:(n + 1) * INNER], hT[:, c, :],
                                        wqkv[:, c, n * INNER:(n + 1) * INNER], start=(c == 0), stop=(c == DH - 1))
                S.step("pe", ins, f"qk{u}")

            def front_v(S, u, slot):
                V(S, pe, "hT_ev", u)
                for c in range(DH):
                    ins = pe.matmul(p_v[:], hT[:, c, :], wqkv[:, c, 2 * INNER:3 * INNER], start=(c == 0),
                                    stop=(c == DH - 1))
                S.step("pe", ins, f"v{u}")
                V(S, act, "v", u)
                V(S, act, "pvB", u, 1)
                S.step("act", act.activation(vv[slot][:], p_v[:], ACT.Copy), f"v_ev{u}")

            def front_squares(S, u):
                V(S, act, "qk", u)
                V(S, act, "n2", u, 1)
                S.step("act", act.activation(sq[:], p_qk[:], ACT.Square), f"sq{u}")

            def front_rotate(S, u, k):
                qk4 = p_qk[:].rearrange("p (a h c) -> p a h c", a=2, h=H)
                rc4 = rc[:].rearrange("p (a h c) -> p a h c", a=2, h=H)
                rs4 = rsn[:].rearrange("p (a h c) -> p a h c", a=2, h=H)
                tk = tab[k][:].rearrange("p (a s) c -> p a s c", a=2)

                def per_head(x, n):
                    return x.unsqueeze(2).to_broadcast([P, 2, H, n])
                V(S, dve, "tab", u, 1)
                V(S, dve, "sq", u)
                V(S, dve, "qkT", u)
                S.step("dve", dve.tensor_tensor(out=rc4, in0=qk4, in1=per_head(tk[:, :, 0, :], DK), op=ALU.mult),
                       f"rc{u}")
                V(S, dve, "rot", u, 1)
                S.step("dve", dve.tensor_tensor(out=rs4[:, :, :, 0:hk], in0=qk4[:, :, :, hk:DK],
                                                in1=per_head(tk[:, :, 1, 0:hk], hk), op=ALU.mult), f"rs1{u}")
                S.step("dve", dve.tensor_tensor(out=rs4[:, :, :, hk:DK], in0=qk4[:, :, :, 0:hk],
                                                in1=per_head(tk[:, :, 1, hk:DK], hk), op=ALU.mult), f"rs2{u}")
                V(S, dve, "sq", u)
                V(S, dve, "rn", u, 2)
                S.step("dve", dve.tensor_reduce(n2[k][:], sq[:].rearrange("p (h c) -> p h c", c=DK), AX.X, ALU.add),
                       f"n2{u}")
                V(S, dve, "n2", u)
                S.step("dve", dve.tensor_scalar(n2[k][:], n2[k][:], 1e-24, None, ALU.max), f"n2c{u}")
                V(S, pool, "n2c", u)
                V(S, pool, "expB", u, 2)
                V(S, pool, "nbB", u, 2)
                S.step("pool", pool.tensor_tensor(out=rn[k][:], in0=n2[k][:], in1=mhalf[:], op=ALU.pow), f"rn{u}")
                V(S, pool, "rs2", u)
                S.step("pool", pool.tensor_tensor(out=rc[:], in0=rc[:], in1=rsn[:], op=ALU.add), f"rot{u}")
                V(S, pool, "rn", u)
                S.step("pool", pool.tensor_scalar(qsc[(u + 2) % RING][:], rn[k][:, 0:H], QK_SCALE, None, ALU.mult), f"qsc{u}")
                V(S, pool, "rot", u)
                S.step("pool", pool.tensor_tensor(out=rc4[:, 1], in0=rc4[:, 1],
                                                  in1=rn[k][:, H:2 * H].unsqueeze(2).to_broadcast([P, H, DK]),
                                                  op=ALU.mult), f"kn{u}")

            def front_qkT(S, u, slot):
                V(S, pe, "kn", u, 1)
                V(S, pe, "rs2", u, 1)
                V(S, pe, "sq", u, 1)
                for c in range(2 * INNER // P):
                    ins = pe.transpose(p_qk[:, c * P:(c + 1) * P], rc[:, c * P:(c + 1) * P], ident[:])
                S.step("pe", ins, f"qkT{u}")
                V(S, act, "qkT", u)
                V(S, act, "sB", u, 2)
                S.step("act", act.activation(qkT[slot][:], p_qk[:], ACT.Copy), f"qkT_ev{u}")

            def scores(S, u, half):
                n = "AB"[half]
                if half == 0:
                    V(S, pe, "qkT_ev", u, 1)
                    V(S, pe, "msk", u, 1)
                    V(S, pe, "expB", u, 1)
                else:
                    V(S, pe, "expA", u)
                mk = msk[u % 2][:].unsqueeze(1).to_broadcast([P, 2, 2 * P])
                for g in range(2):
                    pe.matmul(p_s[:, g * INNER:(g + 1) * INNER].rearrange("p (h c) -> p h c", h=2), identb[:], mk,
                              start=True, stop=False, skip_group_check=True)
                for a in range(2):
                    for w, s in enumerate(((u - 1) % RING, u)):
                        for g in range(2):
                            c = (2 * half + a) * P
                            at = ((2 * g + a) * 2 + w) * P
                            ins = pe.matmul(p_s[:, at:at + P], qkT[u][g * DK:(g + 1) * DK, c:c + P],
                                            qkT[s][g * DK:(g + 1) * DK, INNER + c:INNER + c + P],
                                            start=False, stop=(a == 1 and w == 1), skip_group_check=True)
                S.step("pe", ins, f"s{n}{u}")

            def head_at(half, j):
                return 4 * half + 2 * (j % 2) + j // 2

            def by_bank(x):
                return x.rearrange("p (a b) -> p b a", b=2)

            def softmax_max(S, u, half):
                n = "AB"[half]
                hs = slice(4 * half, 4 * half + 4)
                V(S, dve, f"s{n}", u)
                S.step("dve", dve.tensor_reduce(mx[:, hs], p_s[:].rearrange("p (h c) -> p h c", h=4), AX.X, ALU.max),
                       f"mx{n}{u}")
                V(S, dve, f"mx{n}", u)
                V(S, dve, "qsc", u, 2)
                V(S, dve, f"exp{n}", u, 1)
                S.step("dve", dve.scalar_tensor_tensor(out=by_bank(nb[:, hs]),
                                                       in0=mx[:, hs].rearrange("p (b a) -> p b a", b=2), scalar=-1.0,
                                                       in1=by_bank(qsc[u][:, hs]),
                                                       op0=ALU.mult, op1=ALU.mult), f"nb{n}{u}")

            def softmax_exp(S, u, half):
                n = "AB"[half]
                V(S, act, f"nb{n}", u)
                if half == 0:
                    V(S, act, "ptB", u, 1)
                    V(S, act, "rden", u, 1)
                else:
                    V(S, act, "ptA", u)
                for j in range(4):
                    h = head_at(half, j)
                    ins = act.activation(prob[:, j].rearrange("p w c -> p (w c)"), p_s[:, j * 2 * P:(j + 1) * 2 * P],
                                         ACT.Exp, bias=nb[:, h:h + 1], scale=qsc[u][:, h:h + 1],
                                         accum_out=den[u % 2][:, h:h + 1])
                S.step("act", ins, f"exp{n}{u}")

            def transpose_prob(S, u, half):
                n = "AB"[half]
                V(S, pe, f"exp{n}", u)
                if half == 0:
                    V(S, pe, "peB", u, 1)
                    V(S, pe, "paB", u, 1)
                else:
                    V(S, pe, "peA", u)
                    V(S, pe, "paA", u)
                pf = prob[:].rearrange("p j w c -> p (j w c)")
                tf = probT[:].rearrange("p j w c -> p (j w c)")
                for c in range(8):
                    ins = pe.transpose(p_t[:, c * P:(c + 1) * P], pf[:, c * P:(c + 1) * P], ident[:])
                S.step("pe", ins, f"pt{n}{u}")
                for eng, who, m, lo, hi in ((act, "act", "pa", 0, INNER), (dve, "dve", "pe", INNER, 2 * INNER)):
                    V(S, eng, f"pt{n}", u)
                    V(S, eng, "pvA" if half else "pvB", u, 0 if half else 1)
                    if eng is act:
                        ins = act.activation(tf[:, lo:hi], p_t[:, lo:hi], ACT.Copy)
                    else:
                        ins = dve.tensor_copy(tf[:, lo:hi], p_t[:, lo:hi])
                    S.step(who, ins, f"{m}{n}{u}")

            def weighted_values(S, u, half):
                n = "AB"[half]
                V(S, pe, f"pe{n}", u)
                V(S, pe, f"pa{n}", u)
                if half == 0:
                    V(S, pe, "v_ev", u, 2)
                    V(S, pe, "xo", u)
                for j in range(4):
                    h = head_at(half, j)
                    for w, s in enumerate(((u - 1) % RING, u)):
                        ins = pe.matmul(p_o[:, h * DK:(h + 1) * DK], probT[:, j, w, :], vv[s][:, h * DK:(h + 1) * DK],
                                        start=(w == 0), stop=(w == 1), skip_group_check=True)
                S.step("pe", ins, f"pv{n}{u}")

            def divide(S, u, k):
                V(S, dve, "expB", u, 1)
                S.step("dve", dve.reciprocal(rden[:], den[k][:]), f"rden{u}")
                V(S, dve, "pvB", u, 1)
                V(S, dve, "rden", u)
                V(S, dve, "oT", u, 1)
                S.step("dve", dve.tensor_tensor(out=o_sb[:].rearrange("p (h c) -> p h c", h=H),
                                                in0=p_o[:].rearrange("p (h c) -> p h c", h=H),
                                                in1=rden[:].unsqueeze(2).to_broadcast([P, H, DK]), op=ALU.mult), f"o{u}")

            def turn_out(S, u):
                V(S, pe, "o", u)
                for c in range(INNER // P):
                    ins = pe.transpose(p_o[:, c * P:(c + 1) * P], o_sb[:, c * P:(c + 1) * P], ident[:])
                S.step("pe", ins, f"oT{u}")
                V(S, act, "oT", u)
                V(S, act, "wo", u, 1)
                S.step("act", act.activation(oT[:], p_o[:], ACT.Copy), f"oT_ev{u}")

            def project(S, u, k, t):
                V(S, pe, "oT_ev", u)
                for c in range(INNER // P):
                    ins = pe.matmul(p_o[:, 0:D], oT[:, c * P:(c + 1) * P], wo[:, c, :], start=(c == 0),
                                    stop=(c == INNER // P - 1))
                S.step("pe", ins, f"wo{u}")
                V(S, dve, "wo", u)
                V(S, dve, "res", u, 1)
                V(S, dve, "out", u, 2)
                S.step("dve", dve.tensor_tensor(out=xo[k][:], in0=p_o[:, 0:D], in1=res[k][:], op=ALU.add), f"xo{u}")
                V(S, sp, "xo", u)
                S.load(sp.dma_start(rows(2 * l + 1, tile_slot(t), P), xo[k][:]), f"out{u}")

            S = SA0
            S.begin(l)
            S.load(sp.dma_start(wqkv[:], layer_rows("L0_ffn_wqkv", l, D).rearrange("(c p) n -> p c n", p=P)),
                   "weights")
            S.load(sp.dma_start(wo[:], layer_rows("L0_ffn_wo", l, INNER).rearrange("(c p) n -> p c n", p=P)),
                   "weights")
            S.step("dve", dve.memset(qkT[RING - 1][:], 0.0), "k_none")
            S.step("dve", dve.memset(vv[RING - 1][:], 0.0), "v_none")
            S.step("dve", dve.memset(den[1][:], 1.0), "den_none")
            S.step("dve", dve.memset(res[1][:], 0.0), "res_none")
            S.step("dve", dve.memset(p_o[:], 0.0), "o_none")
            load_tile(S, 1, 0, l)
            load_tile(S, 2, 1, l)
            load_mask(S, RING - 1, 0)
            S.wait(pe, "weights")
            front_tile(S, 2, 0)
            front_qk(S, 2)
            front_squares(S, 2)
            front_rotate(S, 2, 0)
            front_v(S, 2, 0)
            S.wait(sp, "hT2")
            S.wait(sp, "rs22")
            load_tile(S, 3, 2, l)
            front_qkT(S, 3, 0)
            front_tile(S, 3, 1)
            front_qk(S, 3)
            front_squares(S, 3)
            front_rotate(S, 3, 1)
            front_v(S, 3, 1)
            S.close()
            S.done(l + 1)
            S = SA
            with nc.Fori(0, NT // RING) as i:
                S.begin(l * (NT // RING) + i)
                for u in range(RING):
                    t = i * RING + u
                    k = u % 2
                    V(S, sp, "hT", u, 1)
                    V(S, sp, "rs2", u, 1)
                    load_tile(S, u, (t + 3) % NT, l)
                    V(S, sp, "sB", u, 1)
                    load_mask(S, u, t + 1)
                    V(S, sp, "xo", u, 1)
                    S.load(sp.dma_start(res[k][:], rows(2 * l, tile_slot(t), P)), f"res{u}")
                    scores(S, u, 0)
                    divide(S, u, 1 - k)
                    turn_out(S, u)
                    softmax_max(S, u, 0)
                    front_tile(S, u, k)
                    softmax_exp(S, u, 0)
                    project(S, u, 1 - k, t - 1)
                    transpose_prob(S, u, 0)
                    scores(S, u, 1)
                    softmax_max(S, u, 1)
                    front_qkT(S, u, (u + 1) % RING)
                    softmax_exp(S, u, 1)
                    weighted_values(S, u, 0)
                    front_qk(S, u)
                    front_squares(S, u)
                    transpose_prob(S, u, 1)
                    front_v(S, u, (u + 2) % RING)
                    weighted_values(S, u, 1)
                    front_rotate(S, u, k)
                S.close()
            S.done((l + 1) * (NT // RING))
            S = SA1
            S.begin(l)
            divide(S, 0, 1)
            turn_out(S, 0)
            project(S, 0, 1, NT - 1)
            S.close()
            S.done(l + 1)

        DI, NST, WC, R = 512, 16, 4, 64
        Q = DI // P
        CPB = L // CH
        ssm_out = nc.dram_tensor("ssm_out", [CH + T, D], F32).ap()

        NB, LAG = 4, 2

        def mamba(ctx):
            w_in = sb(ctx, "w_in", [P, DH, 2 * DI])
            w_xp = sb(ctx, "w_xp", [P, Q, R + 2 * NST])
            w_bc = sb(ctx, "w_bc", [P, Q, 3, 2 * NST])
            w_dt = sb(ctx, "w_dt", [R, DI])
            w_out = sb(ctx, "w_out", [P, Q, D])
            cw = sb(ctx, "cw", [P, Q, WC])
            cb = sb(ctx, "cb", [P, Q])
            dtb = sb(ctx, "dtb", [P, Q])
            dpar = sb(ctx, "dpar", [P, Q])
            am = sb(ctx, "am", [P, Q, NST])
            sel = sb(ctx, "sel", [96, 2 * NST, P], BF16)
            one = sb(ctx, "one", [P, 1])
            xin = sb(ctx, "xin", [P, CT, D])
            nst, nmv, nrs = sb(ctx, "nst", [P, CT, 6]), sb(ctx, "nmv", [P, CT, 2]), sb(ctx, "nrs", [P, CT])
            xT = sb(ctx, "mxT", [P, DH, CH])
            xr = sb(ctx, "xr", [P, Q, WC - 1 + CH])
            cv = sb(ctx, "cv", [P, Q, CH])
            xd = sb(ctx, "xd", [R, CH])
            bc = sb(ctx, "bc", [96, CH])
            bcr = sb(ctx, "bcr", [96, CH])
            bct = sb(ctx, "bct", [96, CH], BF16)
            bc3 = [sb(ctx, f"bc3{k}", [96, CH], BF16) for k in range(2)]
            ee = sb(ctx, "ee", [P, Q, CH])
            uu = [sb(ctx, f"uu{k}", [P, Q, CH]) for k in range(2)]
            sz = [sb(ctx, f"sz{k}", [P, Q, CH]) for k in range(2)]
            dl = [sb(ctx, f"dl{k}", [P, Q, CH]) for k in range(2)]
            du = [sb(ctx, f"du{k}", [P, Q, CH]) for k in range(2)]
            da = [sb(ctx, f"da{k}", [P, Q, CH]) for k in range(2)]
            hh = [sb(ctx, f"hh{k}", [P, Q, CH]) for k in range(NB)]
            cs = [sb(ctx, f"cs{k}", [P, CH]) for k in range(NB)]
            hlast = sb(ctx, "hlast", [P, NST, Q])
            so = sb(ctx, "so", [P, CT, D])
            p_acc = ps(ctx, "p_acc", Q * CH)
            p_b = ps(ctx, "p_b", CH)
            p_c = ps(ctx, "p_c", CH)
            p_f = [ps(ctx, f"p_f{k}", CH) for k in range(2)]

            def VM(S, eng, name, u, d=0, alone=False):
                v = u - d
                S.wait(eng, f"{name}_{v % CPB}", back=1 if v < 0 else 0, alone=alone)

            def load_x(S, u, c):
                VM(S, sp, "sxn", u, 1)
                S.load(sp.dma_start(xin[:], x_in[bass.ds(c * CH, CH), :].rearrange("(j p) d -> p j d", p=P)), f"x_{u}")

            def norm_a(S, u):
                VM(S, dve, "x", u)
                for j in range(CT):
                    ins = dve.bn_stats(nst[:, j], xin[:, j])
                S.step("dve", ins, f"nst_{u}")
                VM(S, dve, "nst", u, alone=True)
                for j in range(CT):
                    ins = dve.bn_aggr(nmv[:, j], nst[:, j])
                S.step("dve", ins, f"nmv_{u}")
                VM(S, dve, "nmv", u)
                S.step("dve", dve.tensor_scalar(nrs[:], nmv[:, :, 1], 1e-5, None, ALU.add), f"nva_{u}")
                VM(S, pool, "nva", u)
                S.step("pool", pool.tensor_tensor(out=nrs[:], in0=nrs[:], in1=mhalf[:, 0:CT], op=ALU.pow), f"nrs_{u}")

            def norm_b(S, u, c):
                VM(S, dve, "nrs", u)
                for j in range(CT):
                    ins = dve.tensor_scalar(xin[:, j], xin[:, j], nmv[:, j, 0:1], nrs[:, j:j + 1], ALU.subtract,
                                            ALU.mult)
                S.step("dve", ins, f"nrm_{u}")
                VM(S, sp, "nrm", u)
                S.load(sp.dma_start(rows(0, chunk_slot(c), CH).rearrange("(j p) d -> p j d", p=P), xin[:]), f"sxn_{u}")

            def f_turn(S, u):
                VM(S, pe, "nrm", u, 1)
                VM(S, pe, "zr3", u, 1)
                for f in range(DH):
                    for j in range(CT):
                        ins = pe.transpose(p_f[f][:, j * P:(j + 1) * P], xin[:, j, f * P:(f + 1) * P], ident[:])
                S.step("pe", ins, f"tr_{u}")
                VM(S, act, "tr", u)
                for f in range(DH):
                    ins = act.activation(xT[:, f], p_f[f][:], ACT.Copy)
                S.step("act", ins, f"xT_{u}")

            def f_in(S, u, q, o, name, prev):
                VM(S, pe, "xT", u)
                VM(S, pe, prev, u)
                for f in range(DH):
                    ins = pe.matmul(p_f[q % 2][:], w_in[:, f, o + q * P:o + (q + 1) * P], xT[:, f], start=(f == 0),
                                    stop=(f == DH - 1))
                S.step("pe", ins, f"{name}_{u}")

            def f_x(S, u, q):
                if q == 0:
                    VM(S, dve, "tap3", u, 1)
                    if u == CPB - 1:
                        ins = dve.memset(xr[:, :, 0:WC - 1], 0.0)
                    else:
                        VM(S, dve, "xr3", u, 1)
                        ins = dve.tensor_copy(xr[:, :, 0:WC - 1], xr[:, :, CH:CH + WC - 1])
                    S.step("dve", ins, f"carry_{u}")
                f_in(S, u, q, 0, f"inx{q}", "xT" if q < 2 else f"xr{q - 2}")
                VM(S, act, f"inx{q}", u)
                VM(S, act, "carry", u)
                S.step("act", act.activation(xr[:, q, WC - 1:], p_f[q % 2][:], ACT.Copy), f"xr{q}_{u}")

            def f_z(S, u, q, k):
                if q < 2:
                    VM(S, pe, f"so{q}", u)
                f_in(S, u, q, DI, f"inz{q}", f"xr{q + 2}" if q < 2 else f"rl{q}")
                VM(S, act, f"inz{q}", u)
                VM(S, act, "yz", u)
                S.step("act", act.activation(sz[k][:, q], p_f[q % 2][:], ACT.Copy), f"zr{q}_{u}")

            def f_tap(S, u, w):
                if w == 0:
                    VM(S, dve, "xr3", u)
                    VM(S, dve, "u", u, 1)
                else:
                    VM(S, dve, f"tap{w - 1}", u)
                for q in range(Q):
                    if w == 0:
                        ins = dve.tensor_scalar(cv[:, q], xr[:, q, 0:CH], cw[:, q, 0:1], None, ALU.mult)
                    else:
                        ins = dve.scalar_tensor_tensor(out=cv[:, q], in0=xr[:, q, w:w + CH], scalar=cw[:, q, w:w + 1],
                                                       in1=cv[:, q], op0=ALU.mult, op1=ALU.add)
                S.step("dve", ins, f"tap{w}_{u}")

            def f_u(S, u, k):
                VM(S, act, "tap3", u)
                VM(S, act, "op1", u)
                for q in range(Q):
                    ins = act.activation(uu[k][:, q], cv[:, q], ACT.Silu, bias=cb[:, q:q + 1])
                S.step("act", ins, f"u_{u}")

            def f_silu_z(S, u, k):
                VM(S, act, "zr3", u)
                S.step("act", act.activation(sz[k][:], sz[k][:], ACT.Silu), f"sz_{u}")

            def f_xp(S, u, k):
                VM(S, pe, "u", u)
                VM(S, pe, "zr1", u)
                for q in range(Q):
                    ins = pe.matmul(p_f[0][0:R, :], w_xp[:, q, 0:R], uu[k][:, q], start=(q == 0), stop=(q == Q - 1))
                S.step("pe", ins, f"xp_{u}")
                VM(S, act, "xp", u)
                VM(S, act, "dt3", u, 1)
                S.step("act", act.activation(xd[:], p_f[0][0:R, :], ACT.Copy), f"xd_{u}")

            def f_bc(S, u, k):
                for q in range(Q):
                    ins = pe.matmul(p_f[1][0:96, :], w_bc[:, q].rearrange("p r n -> p (r n)"), uu[k][:, q],
                                    start=(q == 0), stop=(q == Q - 1))
                S.step("pe", ins, f"bc_{u}")
                VM(S, act, "bc", u)
                VM(S, act, "b3c", u, 1)
                S.step("act", act.activation(bc[:], p_f[1][0:96, :], ACT.Copy), f"bcs_{u}")

            def f_split(S, u, k):
                VM(S, dve, "bcs", u)
                VM(S, dve, "cn15", u, 1)
                S.step("dve", dve.tensor_copy(bct[:], bc[:]), f"b1_{u}")
                S.step("dve", dve.tensor_copy(bc3[k][0:32, :], bc[0:32, :]), f"b1c_{u}")
                VM(S, dve, "b1", u)
                S.step("dve", dve.tensor_tensor(out=bcr[:], in0=bc[:], in1=bct[:], op=ALU.subtract), f"r1_{u}")
                VM(S, dve, "r1", u)
                S.step("dve", dve.tensor_copy(bct[:], bcr[:]), f"b2_{u}")
                S.step("dve", dve.tensor_copy(bc3[k][32:64, :], bcr[32:64, :]), f"b2c_{u}")
                VM(S, dve, "b2", u)
                S.step("dve", dve.tensor_tensor(out=bcr[64:96, :], in0=bcr[64:96, :], in1=bct[64:96, :],
                                                op=ALU.subtract), f"r2_{u}")
                VM(S, dve, "r2", u)
                S.step("dve", dve.tensor_copy(bc3[k][64:96, :], bcr[64:96, :]), f"b3c_{u}")

            def f_dt(S, u, q, k):
                VM(S, pe, "xd", u)
                VM(S, pe, "bcs", u)
                if q >= 2:
                    VM(S, pe, f"rl{q - 2}", u)
                S.step("pe", pe.matmul(p_f[q % 2][:], w_dt[:, q * P:(q + 1) * P], xd[:], start=True, stop=True),
                       f"dt{q}_{u}")
                VM(S, act, f"dt{q}", u)
                VM(S, act, "sp", u, 1)
                VM(S, act, "ex15", u, 1)
                S.step("act", act.activation(ee[:, q], p_f[q % 2][:], ACT.Abs, bias=dtb[:, q:q + 1]), f"ab{q}_{u}")
                S.step("act", act.activation(dl[k][:, q], p_f[q % 2][:], ACT.Relu, bias=dtb[:, q:q + 1]), f"rl{q}_{u}")

            def f_softplus(S, u, k):
                VM(S, act, "rl3", u)
                S.step("act", act.activation(ee[:], ee[:], ACT.Exp, scale=-1.0), f"ea_{u}")
                VM(S, act, "ea", u)
                S.step("act", act.activation(ee[:], ee[:], ACT.Ln, bias=one[:]), f"ln_{u}")
            def f_du(S, u, k):
                VM(S, dve, "ln", u)
                S.step("dve", dve.tensor_tensor(out=dl[k][:], in0=dl[k][:], in1=ee[:], op=ALU.add), f"sp_{u}")
                VM(S, dve, "sp", u)
                VM(S, dve, "db15", u, 1)
                S.step("dve", dve.tensor_tensor(out=du[k][:], in0=dl[k][:], in1=uu[k][:], op=ALU.mult), f"du_{u}")

            def b_cast(S, u, n, k):
                if n == 0:
                    VM(S, pe, "b3c", u, 1)
                    VM(S, pe, "b2c", u, 1)
                    VM(S, pe, "db15", u, 1)
                    VM(S, pe, "ce15", u, 1)
                else:
                    VM(S, pe, f"db{n - 1}", u)
                    VM(S, pe, f"ce{n - 1}", u)
                S.step("pe", pe.matmul(p_b[:], sel[:, n, :], bc3[k][:], start=True, stop=True), f"bn{n}_{u}")
                S.step("pe", pe.matmul(p_c[:], sel[:, NST + n, :], bc3[k][:], start=True, stop=True), f"cn{n}_{u}")

            def b_in(S, u, n, k):
                a, b = n % 2, n % NB
                if n < 2:
                    VM(S, act, f"sc{n + 14}", u, 1)
                else:
                    VM(S, act, f"sc{n - 2}", u)
                if n == 0:
                    VM(S, act, "sp", u, 1)
                for q in range(Q):
                    ins = act.activation(da[a][:, q], dl[k][:, q], ACT.Exp, scale=am[:, q, n:n + 1])
                S.step("act", ins, f"ex{n}_{u}")
                VM(S, act, f"cn{n}", u)
                before = (n - NB) % NST
                VM(S, act, f"hc{before}", u, int(n < NB))
                S.step("act", act.activation(cs[b][:], p_c[:], ACT.Copy), f"ce{n}_{u}")
                VM(S, dve, f"bn{n}", u)
                VM(S, dve, f"ac{before}", u, int(n < NB and before < NST - LAG))
                if n == 0:
                    VM(S, dve, "du", u, 1)
                S.step("dve", dve.tensor_tensor(out=hh[b][:], in0=du[k][:],
                                                in1=p_b[:].unsqueeze(1).to_broadcast([P, Q, CH]), op=ALU.mult),
                       f"db{n}_{u}")

            def b_scan(S, u, n):
                a, b = n % 2, n % NB
                VM(S, dve, f"ex{n}", u)
                VM(S, dve, f"db{n}", u)
                if u > 0:
                    VM(S, dve, f"hl{n}", u, 1)
                for q in range(Q):
                    ins = dve.tensor_tensor_scan(out=hh[b][:, q], data0=da[a][:, q], data1=hh[b][:, q],
                                                 initial=0.0 if u == 0 else hlast[:, n, q:q + 1],
                                                 op0=ALU.mult, op1=ALU.add)
                S.step("dve", ins, f"sc{n}_{u}")

            def b_out(S, u, n):
                b = n % NB
                VM(S, pool, f"sc{n}", u)
                VM(S, pool, f"ce{n}", u)
                S.step("pool", pool.tensor_copy(hlast[:, n].unsqueeze(2), hh[b][:, :, CH - 1:CH]), f"hl{n}_{u}")
                VM(S, pool, f"hl{n}", u)
                S.step("pool", pool.tensor_tensor(out=hh[b][:], in0=hh[b][:],
                                                  in1=cs[b][:].unsqueeze(1).to_broadcast([P, Q, CH]), op=ALU.mult),
                       f"hc{n}_{u}")

            def b_sum(S, u, n):
                VM(S, pe, f"hc{n}", u, int(n >= NST - LAG))
                if n == 0:
                    VM(S, pe, "yu", u)
                for q in range(Q):
                    ins = pe.matmul(p_acc[:, q * CH:(q + 1) * CH], ident[:], hh[n % NB][:, q], start=(n == 0),
                                    stop=(n == NST - 1), skip_group_check=True)
                S.step("pe", ins, f"ac{n}_{u}")

            def e_gate(S, u, k):
                VM(S, dve, "ac15", u)
                for q in range(Q):
                    ins = dve.scalar_tensor_tensor(out=uu[k][:, q], in0=uu[k][:, q], scalar=dpar[:, q:q + 1],
                                                   in1=p_acc[:, q * CH:(q + 1) * CH], op0=ALU.mult, op1=ALU.add)
                S.step("dve", ins, f"yu_{u}")
                VM(S, pool, "yu", u)
                S.step("pool", pool.tensor_tensor(out=uu[k][:], in0=uu[k][:], in1=sz[k][:], op=ALU.mult), f"yz_{u}")

            def e_out(S, u, k, half):
                VM(S, pe, "yz", u)
                VM(S, pe, "xr3", u)
                for j in (2 * half, 2 * half + 1):
                    for q in range(Q):
                        ins = pe.matmul(p_f[j // 2][:, (j % 2) * D:(j % 2 + 1) * D], uu[k][:, q, j * P:(j + 1) * P],
                                        w_out[:, q, :], start=(q == 0), stop=(q == Q - 1))
                S.step("pe", ins, f"op{half}_{u}")
                VM(S, act, f"op{half}", u)
                VM(S, act, "st", u, 1)
                ins = act.activation(so[:, 2 * half:2 * half + 2].rearrange("p j d -> p (j d)"), p_f[half][:], ACT.Copy)
                S.step("act", ins, f"so{half}_{u}")

            def e_store(S, u, c):
                VM(S, sp, "so1", u)
                S.load(sp.dma_start(ssm_out[bass.ds((c + 1) * CH, CH), :].rearrange("(j p) d -> p j d", p=P), so[:]),
                       f"st_{u}")

            def front_at(S, u, n):
                k = (u + 1) % 2
                if n == 0:
                    f_turn(S, u)
                elif n in (1, 2):
                    f_x(S, u, 2 * n - 2)
                    f_x(S, u, 2 * n - 1)
                elif n in (3, 4):
                    f_tap(S, u, n - 3)
                elif n == 5:
                    f_tap(S, u, 2)
                    f_z(S, u, 0, k)
                    f_z(S, u, 1, k)
                elif n == 6:
                    f_tap(S, u, 3)
                elif n == 7:
                    f_u(S, u, k)
                elif n == 8:
                    f_xp(S, u, k)
                elif n == 9:
                    f_bc(S, u, k)
                    f_split(S, u, k)
                elif n in (10, 11):
                    f_dt(S, u, 2 * n - 20, k)
                    f_dt(S, u, 2 * n - 19, k)
                elif n == 12:
                    f_z(S, u, 2, k)
                    f_softplus(S, u, k)
                elif n == 13:
                    f_z(S, u, 3, k)
                    f_du(S, u, k)
                elif n == 14:
                    f_silu_z(S, u, k)

            S = Steps(nc, top, book, gate, "ssm_first", lenient=True)
            S.begin(0)
            w = "weights"
            S.load(sp.dma_start(w_in[:], A["L0_attn_in_proj_w"].rearrange("(c p) n -> p c n", p=P)), w)
            S.load(sp.dma_start(w_xp[:], A["L0_attn_x_proj_w"].rearrange("(q p) n -> p q n", p=P)), w)
            for r in range(3):
                S.load(sp.dma_start(w_bc[:, :, r, :],
                                    A["L0_attn_x_proj_w"][:, R:].rearrange("(q p) n -> p q n", p=P)), w)
            S.load(sp.dma_start(w_dt[:], A["L0_attn_dt_proj_w"]), w)
            S.load(sp.dma_start(w_out[:], A["L0_attn_out_proj_w"].rearrange("(q p) n -> p q n", p=P)), w)
            S.load(sp.dma_start(cw[:], A["L0_attn_conv_w"].rearrange("(q p) n -> p q n", p=P)), w)
            for dst, nm in ((cb, "L0_attn_conv_b"), (dtb, "L0_attn_dt_proj_b"), (dpar, "L0_attn_D_param")):
                for q in range(Q):
                    S.load(sp.dma_start(dst[:, q:q + 1], A[nm].unsqueeze(1)[q * P:(q + 1) * P, :]), w)
            S.load(sp.dma_start(am[:], A["L0_attn_A_log"].rearrange("(q p) n -> p q n", p=P)), w)
            S.load(sp.dma_start(sel[:], A["c_select"]), w)
            S.step("dve", dve.memset(one[:], 1.0), "one")
            for t in (uu[1], sz[1], hh[NB - 2], hh[NB - 1]):
                ins = dve.memset(t[:], 0.0)
            S.step("dve", ins, "none")
            S.wait(pe, "none")
            for q in range(Q):
                ins = pe.matmul(p_acc[:, q * CH:(q + 1) * CH], ident[:], hh[NB - 1][:, q], start=True, stop=False,
                                skip_group_check=True)
            S.step("pe", ins, "acc0")
            load_x(S, CPB - 2, 0)
            for eng in (pe, act, dve):
                S.wait(eng, w)
            S.wait(act, "one")
            S.step("act", act.activation(am[:], am[:], ACT.Exp), "aexp")
            S.wait(dve, "aexp")
            S.step("dve", dve.tensor_scalar(am[:], am[:], -1.0, None, ALU.mult), "aneg")
            norm_a(S, CPB - 2)
            norm_b(S, CPB - 2, 0)
            for n in range(NST):
                if n == 1:
                    S.wait(sp, f"tr_{CPB - 1}")
                    load_x(S, CPB - 1, 1)
                front_at(S, CPB - 1, n)
            norm_a(S, CPB - 1)
            norm_b(S, CPB - 1, 1)
            S.close()
            S.done(1)

            S = Steps(nc, top, book, gate, "ssm")
            with nc.Fori(0, B) as i:
                S.begin(i)
                for u in range(CPB):
                    c, k = i * CPB + u, u % 2
                    b_cast(S, u, 0, k)
                    b_in(S, u, 0, k)
                    for n in range(NST):
                        if n + 1 < NST:
                            b_cast(S, u, n + 1, k)
                            b_in(S, u, n + 1, k)
                        b_scan(S, u, n)
                        b_out(S, u, n)
                        b_sum(S, u, (n - LAG) % NST)
                        if n == LAG - 1:
                            e_gate(S, u, 1 - k)
                        if n in (3, 4):
                            e_out(S, u, 1 - k, n - 3)
                        if n == 4:
                            e_store(S, u, c - 1)
                        front_at(S, u, n)
                        if n == 1:
                            VM(S, sp, "tr", u)
                            load_x(S, u, (c + 2) % NC)
                        if n == 7:
                            norm_a(S, u)
                        if n == 10:
                            norm_b(S, u, (c + 2) % NC)
                S.close()
            S.done(B)

            S = Steps(nc, top, book, gate, "ssm_last", lenient=True)
            S.begin(0)
            for n in range(NST - LAG, NST):
                b_sum(S, 0, n)
            e_gate(S, 0, 1)
            e_out(S, 0, 1, 0)
            e_out(S, 0, 1, 1)
            e_store(S, 0, NC - 1)
            S.close()
            S.done(1)

        with ExitStack() as ctx:
            mamba(ctx)

        SG0 = Steps(nc, top, book, gate, "gated_first", lenient=True)
        SG = Steps(nc, top, book, gate, "gated")
        BJ = -(-HID // NJ)
        BLK = [min(BJ, HID - j * BJ) for j in range(NJ)]

        def V2(S, eng, name, u, d=0, alone=False):
            v = u - d
            S.wait(eng, f"{name}{v % 2}", back=1 if v < 0 else 0, alone=alone)

        def norm_stats(S, u, x, st, mv, rstd, eps, last_use):
            V2(S, dve, last_use, u, 1)
            for j in range(CT):
                ins = dve.bn_stats(st[:, j], x[:, j])
            S.step("dve", ins, f"st{u}")
            V2(S, dve, "st", u, alone=True)
            for j in range(CT):
                ins = dve.bn_aggr(mv[:, j], st[:, j])
            S.step("dve", ins, f"mv{u}")
            V2(S, dve, "mv", u)
            S.step("dve", dve.tensor_scalar(rstd[:], mv[:, :, 1], eps, None, ALU.add), f"var{u}")
            V2(S, pool, "var", u)
            S.step("pool", pool.tensor_tensor(out=rstd[:], in0=rstd[:], in1=mhalf[:, 0:CT], op=ALU.pow), f"rs{u}")

        def gated(l, gctx):
            w1 = sb(gctx, "w1", [P, DH, 2 * HID])
            w2 = sb(gctx, "w2", [BJ, NJ, D])
            b1 = sb(gctx, "b1", [BJ, 2, NJ])
            b2 = sb(gctx, "b2", [P, D])
            lgb = sb(gctx, "lgb", [P, 2, DH])
            h = [sb(gctx, f"gh{k}", [P, CT, D]) for k in range(2)]
            r = [sb(gctx, f"gr{k}", [P, CT, D]) for k in range(2)]
            hn = sb(gctx, "ghn", [P, CT, D])
            hT = sb(gctx, "ghT", [P, DH, CH])
            st = sb(gctx, "gst", [P, CT, 6])
            mv = sb(gctx, "gmv", [P, CT, 2])
            rstd = sb(gctx, "grstd", [P, CT])
            gg = [sb(gctx, f"gg{k}", [BJ, CH]) for k in range(2)]
            hid = sb(gctx, "ghid", [BJ, NJ, CH])
            p_tr = ps(gctx, "p_tr", DH * CH)
            p_a = [ps(gctx, f"p_a{k}", CH) for k in range(2)]
            p_g = [ps(gctx, f"p_g{k}", CH) for k in range(2)]
            p_y = ps(gctx, "p_y", CT * D)

            def load_h(S, u, c):
                slot = chunk_slot(c)
                for src, cols in ((0, slice(0, P)), (-1, slice(P, D))):
                    S.load(sp.dma_start(h[u][:, :, cols],
                                        rows(2 * l + 1, slot, CH, src)[:, cols].rearrange("(j p) d -> p j d", p=P)),
                           f"h{u}")

            def prepare(S, u, k):
                V2(S, dve, "h", u, 1)
                norm_stats(S, u, h[k], st, mv, rstd, 1e-5, "norm")
                V2(S, dve, "rs", u)
                V2(S, dve, "tr", u, 1)
                for j in range(CT):
                    ins = dve.tensor_scalar(hn[:, j], h[k][:, j], mv[:, j, 0:1], rstd[:, j:j + 1], ALU.subtract,
                                            ALU.mult)
                S.step("dve", ins, f"norm{u}")

            def turn(S, u):
                V2(S, pe, "norm", u)
                V2(S, pe, "hT", u, 1)
                for f in range(DH):
                    for j in range(CT):
                        ins = pe.transpose(p_tr[:, f * CH + j * P:f * CH + (j + 1) * P],
                                           hn[:, j, f * P:(f + 1) * P], ident[:])
                S.step("pe", ins, f"tr{u}")
                V2(S, dve, "tr", u)
                V2(S, dve, "w1_5", u)
                for f in range(DH):
                    ins = dve.tensor_scalar(hT[:, f], p_tr[:, f * CH:(f + 1) * CH], lgb[:, 0, f:f + 1],
                                            lgb[:, 1, f:f + 1], ALU.mult, ALU.add)
                S.step("dve", ins, f"hT{u}")

            def up(S, u, blocks):
                for j in blocks:
                    n, k = BLK[j], j % 2
                    if j == 0:
                        V2(S, pe, "hT", u, 1)
                    if j < 2:
                        V2(S, pe, f"hid_{j + NJ - 2}_", u, 1)
                    else:
                        V2(S, pe, f"hid_{j - 2}_", u)
                    for dst, o in ((p_g[k], HID), (p_a[k], 0)):
                        for f in range(DH):
                            ins = pe.matmul(dst[0:n, :], w1[:, f, o + j * BJ:o + j * BJ + n], hT[:, f, :],
                                            start=(f == 0), stop=(f == DH - 1))
                    S.step("pe", ins, f"w1_{j}{u}")
                    V2(S, act, f"w1_{j}", u)
                    if j < 2:
                        V2(S, act, f"hid_{j + NJ - 2}_", u, 1)
                    else:
                        V2(S, act, f"hid_{j - 2}_", u)
                    S.step("act", act.activation(gg[k][0:n, :], p_g[k][0:n, :], ACT.Gelu, bias=b1[0:n, 1, j:j + 1]),
                           f"gelu_{j}_{u}")
                    V2(S, dve, f"gelu_{j}_", u)
                    if j == 0:
                        V2(S, dve, "w2b", u, 1)
                    S.step("dve", dve.scalar_tensor_tensor(out=hid[0:n, j], in0=p_a[k][0:n, :],
                                                           scalar=b1[0:n, 0, j:j + 1], in1=gg[k][0:n, :],
                                                           op0=ALU.add, op1=ALU.mult), f"hid_{j}_{u}")

            def down(S, u):
                V2(S, pool, "r", u)
                S.step("pool", pool.tensor_tensor(out=r[u][:], in0=r[u][:],
                                                  in1=b2[:].unsqueeze(1).to_broadcast([P, CT, D]), op=ALU.add),
                       f"rb{u}")
                V2(S, pe, f"hid_{NJ - 1}_", u)
                for half, nm in enumerate("ab"):
                    V2(S, pe, "y" + nm, u, 1)
                    for m in range(2):
                        j0 = 2 * half + m
                        for j in range(NJ):
                            n = BLK[j]
                            ins = pe.matmul(p_y[:, j0 * D:(j0 + 1) * D], hid[0:n, j, j0 * P:(j0 + 1) * P],
                                            w2[0:n, j, :], start=(j == 0), stop=(j == NJ - 1))
                    S.step("pe", ins, f"w2{nm}{u}")
                V2(S, dve, "rb", u)
                for half, nm in enumerate("ab"):
                    V2(S, dve, "w2" + nm, u)
                    rr = r[u][:, 2 * half:2 * half + 2].rearrange("p j d -> p (j d)")
                    S.step("dve", dve.tensor_tensor(out=rr, in0=p_y[:, 2 * half * D:(2 * half + 2) * D], in1=rr,
                                                    op=ALU.add), f"y{nm}{u}")

            S = SG0
            S.begin(l)
            S.load(sp.dma_start(w1[:], layer_rows("L0_ffn_w1", l, D).rearrange("(c p) n -> p c n", p=P)), "weights")
            b1f = A["L0_ffn_b1"].rearrange("l n -> (l n)").unsqueeze(1)
            w2f = A["L0_ffn_w2"].rearrange("l r n -> (l r) n")
            for j in range(NJ):
                n = BLK[j]
                S.load(sp.dma_start(w2[0:n, j, :], w2f[bass.ds(l * HID + j * BJ, n), :]), "weights")
                for q in range(2):
                    S.load(sp.dma_start(b1[0:n, q, j:j + 1], b1f[bass.ds(l * 2 * HID + q * HID + j * BJ, n), :]),
                           "weights")
            for q, nm in enumerate(("L0_ffn_ln_g", "L0_ffn_ln_b")):
                v = A[nm].rearrange("l n -> (l n)").unsqueeze(1)
                for f in range(DH):
                    S.load(sp.dma_start(lgb[:, q, f:f + 1], v[bass.ds(l * D + f * P, P), :]), "weights")
            S.load(sp.dma_start(b2[:], A["L0_ffn_b2"][bass.ds(l, 1), :].to_broadcast([P, D])), "weights")
            load_h(S, 0, 0)
            load_h(S, 1, 1)
            S.wait(dve, "weights")
            S.wait(dve, "h0")
            prepare(S, 1, 0)
            turn(S, 1)
            S.close()
            S.done(l + 1)
            S = SG
            with nc.Fori(0, NC // 2) as i:
                S.begin(l * (NC // 2) + i)
                for u in range(2):
                    c = i * 2 + u
                    V2(S, sp, "norm", u, 1)
                    load_h(S, u, (c + 2) % NC)
                    V2(S, sp, "out", u, 2)
                    S.load(sp.dma_start(r[u][:], rows(2 * l + 1, chunk_slot(c), CH).rearrange("(j p) d -> p j d", p=P)),
                           f"r{u}")
                    up(S, u, range(0, 3))
                    prepare(S, u, (u + 1) % 2)
                    up(S, u, range(3, NJ))
                    turn(S, u)
                    down(S, u)
                    V2(S, sp, "yb", u)
                    S.load(sp.dma_start(rows(2 * l + 2, chunk_slot(c), CH).rearrange("(j p) d -> p j d", p=P), r[u][:]),
                           f"out{u}")
                S.close()
            S.done((l + 1) * (NC // 2))

        NE, CAP = 64, 128
        EXT = D + NE + 1
        ZR = 4
        xb_d = nc.dram_tensor("dispatched", [NE * CAP, EXT], F32).ap()
        zctx = ExitStack()
        slot_zeros = sb(zctx, "slot_zeros", [P, ZR * EXT])
        zeros_there, slots_zeroed = (top.enter_context(nc.semaphore(n)) for n in ("zeros_there", "slots_zeroed"))
        pool.memset(slot_zeros[:], 0.0).then_inc(zeros_there, 1)
        act.wait_ge(zeros_there, 1)
        NZ = NE * CAP // (ZR * P)
        for n in range(NZ):
            act.dma_start(xb_d[n * ZR * P:(n + 1) * ZR * P, :].rearrange("(p r) e -> p (r e)", r=ZR),
                          slot_zeros[:]).then_inc(slots_zeroed, 16)
        with nc.Fori(0, NL) as l:
            with ExitStack() as ctx:
                attention(l, ctx)
            with ExitStack() as ctx:
                gated(l, ctx)
        for eng in (pe, act, dve, pool, sp):
            eng.wait_ge(slots_zeroed, 16 * NZ)
        zctx.close()

        HA, DA = 16, 16
        TOPK, EI = 6, 176
        SI = 2 * EI
        NX = NE + 2
        NJS = 3
        BS = [min(P, SI - j * P) for j in range(NJS)]
        FAR = 16384.0
        KB = 0.21
        x1_d = nc.dram_tensor("x1", [T, D], F32).ap()
        xn1_d = nc.dram_tensor("xn1", [T, D], F32).ap()
        y_d = nc.dram_tensor("moe_out", [T + 1, D], F32).ap()
        kv_d = nc.dram_tensor("kv", [B * P, 2 * D], F32).ap()

        def VC(S, eng, name, u, d=0, alone=False):
            v = u - d
            S.wait(eng, f"{name}_{v % CPB}", back=1 if v < 0 else 0, alone=alone)

        def tiles(ap):
            return ap.rearrange("(j p) d -> p j d", p=P)

        def rope(S, u, src, cos, sin, t1, t2, free, tag):
            s2, i2, o2 = (x.rearrange("p j (h two) -> p j h two", two=2) for x in (src, sin, t2))
            for nm in free:
                VC(S, dve, nm, u, 1)
            S.step("dve", dve.tensor_tensor(out=t1, in0=src, in1=cos, op=ALU.mult), f"{tag}c_{u}")
            for e in range(2):
                ins = dve.tensor_tensor(out=o2[:, :, :, e], in0=s2[:, :, :, 1 - e], in1=i2[:, :, :, e], op=ALU.mult)
            S.step("dve", ins, f"{tag}s_{u}")
            VC(S, pool, f"{tag}s", u)
            S.step("pool", pool.tensor_tensor(out=t1, in0=t1, in1=t2, op=ALU.add), f"{tag}_{u}")

        def layer_norm(S, u, x, st, mv, rs, eps, out, free, tag):
            VC(S, dve, f"{tag}", u, 1)
            for j in range(CT):
                ins = dve.bn_stats(st[:, j], x[:, j])
            S.step("dve", ins, f"{tag}st_{u}")
            VC(S, dve, f"{tag}st", u, alone=True)
            for j in range(CT):
                ins = dve.bn_aggr(mv[:, j], st[:, j])
            S.step("dve", ins, f"{tag}mv_{u}")
            VC(S, dve, f"{tag}mv", u)
            S.step("dve", dve.tensor_scalar(rs[:], mv[:, :, 1], eps, None, ALU.add), f"{tag}va_{u}")
            VC(S, pool, f"{tag}va", u)
            S.step("pool", pool.tensor_tensor(out=rs[:], in0=rs[:], in1=mhalf[:, 0:CT], op=ALU.pow), f"{tag}rs_{u}")
            VC(S, dve, f"{tag}rs", u)
            for nm, d in free:
                VC(S, dve, nm, u, d)
            for j in range(CT):
                ins = dve.tensor_scalar(out[:, j], x[:, j], mv[:, j, 0:1], rs[:, j:j + 1], ALU.subtract, ALU.mult)
            S.step("dve", ins, f"{tag}_{u}")

        def route(ctx):
            x = sb(ctx, "rx", [P, CT, D])
            s0 = sb(ctx, "rs0", [P, CT, D])
            f0 = sb(ctx, "rf0", [P, CT, D])
            st, mv, rs = sb(ctx, "rst", [P, CT, 6]), sb(ctx, "rmv", [P, CT, 2]), sb(ctx, "rrs", [P, CT])
            xe = [sb(ctx, f"xe{k}", [P, CT, EXT]) for k in range(2)]
            xT = sb(ctx, "rxT", [P, DH, CH])
            w_kv = sb(ctx, "w_kv", [P, DH, 2 * D])
            b_kv = sb(ctx, "b_kv", [1, 2 * D])
            ones = sb(ctx, "ones", [P, P])
            kg = sb(ctx, "kg", [P, CT, D])
            vg = sb(ctx, "vg", [P, CT, D])
            cs = sb(ctx, "rcs", [P, CT, 2, D])
            kr = sb(ctx, "kr", [P, CT, D])
            kt = sb(ctx, "kt", [P, CT, D])
            kvm = sb(ctx, "kvm", [P, P])
            kvs = sb(ctx, "kvs", [P, 2 * D])
            w_g = sb(ctx, "w_g", [P, DH, NE])
            gb = sb(ctx, "gb", [P, NE])
            lmx = sb(ctx, "lmx", [P, CT])
            lsub = sb(ctx, "lsub", [P, CT, NE])
            lex = sb(ctx, "lex", [P, CT, NE])
            lsum = sb(ctx, "lsum", [P, CT])
            lrec = sb(ctx, "lrec", [P, CT])
            sbx = sb(ctx, "sbx", [P, CT, NX])
            m8 = sb(ctx, "m8", [P, CT, 8])
            mr = sb(ctx, "mr", [P, CT, NX])
            mk = sb(ctx, "mk", [P, CT, NE], BF16)
            mkf = sb(ctx, "mkf", [P, CT, NE])
            macc = sb(ctx, "macc", [P, NE])
            msum = sb(ctx, "msum", [P, NE])
            maccb = sb(ctx, "maccb", [P, NE], BF16)
            tri = sb(ctx, "tri", [P, P], BF16)
            onesb = sb(ctx, "onesb", [P, P], BF16)
            eb = sb(ctx, "eb", [P, NE])
            sv = sb(ctx, "sv", [P, CT, NE])
            sl = sb(ctx, "sl", [P, CT, NE])
            s8 = sb(ctx, "s8", [P, CT, 8])
            s8o = sb(ctx, "s8o", [P, CT, 8])
            idx = [sb(ctx, f"idx{k}", [P, CT, 8], I32) for k in range(2)]
            tok = sb(ctx, "tok", [P, CT])
            ws13 = sb(ctx, "ws13", [P, DH, 2, SI])
            ws2 = sb(ctx, "ws2", [P, NJS, D])
            sg = [sb(ctx, f"sg{k}", [P, CH]) for k in range(2)]
            sh = sb(ctx, "sh", [P, NJS, CH])
            zs = sb(ctx, "zs", [P, CT, D])
            p_tr = ps(ctx, "rp_tr", DH * CH)
            p_k = [ps(ctx, f"rp_k{k}", 2 * D) for k in range(2)]
            p_kv = ps(ctx, "rp_kv", 512)
            p_ks = p_kv[:, D:2 * D]
            p_l = ps(ctx, "rp_l", 512)
            p_h = [ps(ctx, f"rp_h{k}", CH) for k in range(2)]

            def load_mix(S, u, c):
                S.load(sp.dma_start(x[:], tiles(x_in[bass.ds(c * CH, CH), :])), f"x_{u}")
                S.load(sp.dma_start(s0[:], tiles(ssm_out[bass.ds(c * CH + CH, CH), :])), f"x_{u}")
                S.load(sp.dma_start(f0[:], tiles(rows(4, chunk_slot(c), CH))), f"x_{u}")

            def front(S, u, k, c):
                VC(S, act, "x", u, 1)
                S.step("act", act.activation(f0[:], f0[:], ACT.Silu), f"sf_{u}")
                VC(S, dve, "sf", u)
                S.step("dve", dve.tensor_tensor(out=s0[:], in0=s0[:], in1=f0[:], op=ALU.mult), f"sm_{u}")
                VC(S, dve, "sm", u)
                S.step("dve", dve.tensor_tensor(out=x[:], in0=x[:], in1=s0[:], op=ALU.add), f"x1_{u}")
                VC(S, dve, "x1", u)
                layer_norm(S, u, x, st, mv, rs, 1e-5, xe[k][:, :, 0:D], (("disp", 1), ("sxn", 2), ("tr", 2)), "ln")
                VC(S, sp, "x1", u)
                S.load(sp.dma_start(tiles(x1_d[bass.ds(c * CH, CH), :]), x[:]), f"sx1_{u}")
                VC(S, sp, "ln", u)
                S.load(sp.dma_start(tiles(xn1_d[bass.ds(c * CH, CH), :]), xe[k][:, :, 0:D]), f"sxn_{u}")

            def turn(S, u, k):
                VC(S, pe, "ln", u)
                VC(S, pe, "zs", u, 1)
                for f in range(DH):
                    for j in range(CT):
                        ins = pe.transpose(p_tr[:, f * CH + j * P:f * CH + (j + 1) * P],
                                           xe[k][:, j, f * P:(f + 1) * P], ident[:])
                S.step("pe", ins, f"tr_{u}")
                VC(S, act, "tr", u)
                VC(S, act, f"sp{NJS - 1}", u)
                VC(S, act, "lg", u)
                VC(S, act, "kp3", u)
                S.step("act", act.activation(xT[:].rearrange("p f t -> p (f t)"), p_tr[:], ACT.Copy), f"xT_{u}")

            def keys(S, u):
                VC(S, pe, "xT", u, 1)
                for j in range(CT):
                    if j < 2:
                        VC(S, pe, f"vg{j + 2}", u, 1)
                    else:
                        VC(S, pe, f"vg{j - 2}", u)
                    for f in range(DH):
                        pe.matmul(p_k[j % 2][:], xT[:, f, j * P:(j + 1) * P], w_kv[:, f, :], start=(f == 0), stop=False)
                    ins = pe.matmul(p_k[j % 2][:], ones[0:1, :], b_kv[:], start=False, stop=True)
                    S.step("pe", ins, f"kp{j}_{u}")
                    VC(S, act, f"kp{j}", u)
                    VC(S, act, "kvsum", u, 1)
                    VC(S, act, "krs", u, 1)
                    S.step("act", act.activation(kg[:, j], p_k[j % 2][:, 0:D], ACT.Gelu), f"kg{j}_{u}")
                    S.step("act", act.activation(vg[:, j], p_k[j % 2][:, D:2 * D], ACT.Copy), f"vg{j}_{u}")
                VC(S, dve, "kg3", u)
                S.step("dve", dve.tensor_scalar(kg[:], kg[:], KB, None, ALU.add), f"ka_{u}")
                VC(S, dve, "cs", u)
                VC(S, dve, "ka", u)
                rope(S, u, kg[:], cs[:, :, 0], cs[:, :, 1], kr[:], kt[:], ("kvsum", "kr"), "kr")

            def key_sums(S, u):
                VC(S, pe, "ka", u)
                if u == 0:
                    VC(S, pe, "kvst", u, 1)
                for j in range(CT):
                    ins = pe.matmul(p_ks, ones[:], kg[:, j], start=(u == 0 and j == 0), stop=False,
                                    skip_group_check=True)
                S.step("pe", ins, f"ksum_{u}")
                VC(S, pe, "kr", u)
                for j in range(CT):
                    for f in range(DH):
                        fs = slice(f * P, (f + 1) * P)
                        ins = pe.matmul(p_kv[:, fs], kr[:, j, fs], vg[:, j, fs], start=False,
                                        stop=(u == CPB - 1 and j == CT - 1 and f == DH - 1), skip_group_check=True)
                S.step("pe", ins, f"kvsum_{u}")
                if u == CPB - 1:
                    VC(S, dve, "kvsum", u)
                    VC(S, dve, "kvo", u, CPB)
                    S.step("dve", dve.tensor_tensor(out=kvs[:, 0:D].rearrange("p (f c) -> p f c", f=DH),
                                                    in0=p_kv[:, 0:D].rearrange("p (f c) -> p f c", f=DH),
                                                    in1=kvm[:].unsqueeze(1).to_broadcast([P, DH, P]), op=ALU.mult),
                           f"kvm_{u}")
                    S.step("dve", dve.tensor_scalar(kvs[:, D:2 * D], p_ks, 1.0 / L, None, ALU.mult),
                           f"kvst_{u}")

            def gate_scores(S, u, k):
                VC(S, pe, "xT", u, 1)
                VC(S, pe, "sl", u, 1)
                for j in range(CT):
                    for f in range(DH):
                        ins = pe.matmul(p_l[:, j * NE:(j + 1) * NE], xT[:, f, j * P:(j + 1) * P], w_g[:, f, :],
                                        start=(f == 0), stop=(f == DH - 1))
                S.step("pe", ins, f"lg_{u}")
                lg = p_l[:, 0:CT * NE].rearrange("p (j e) -> p j e", j=CT)

                def each(t):
                    return t[:].unsqueeze(2).to_broadcast([P, CT, NE])
                VC(S, dve, "lg", u)
                S.step("dve", dve.tensor_reduce(lmx[:], lg, AX.X, ALU.max), f"lmx_{u}")
                VC(S, dve, "lmx", u)
                S.step("dve", dve.tensor_tensor(out=lsub[:], in0=lg, in1=each(lmx), op=ALU.subtract), f"lsub_{u}")
                VC(S, act, "lsub", u)
                VC(S, act, "sc", u, 1)
                S.step("act", act.activation(lex[:], lsub[:], ACT.Exp), f"lex_{u}")

            def choose(S, u, k):
                def each(t):
                    return t[:].unsqueeze(2).to_broadcast([P, CT, NE])
                VC(S, dve, "lex", u)
                S.step("dve", dve.tensor_reduce(lsum[:], lex[:], AX.X, ALU.add), f"lsum_{u}")
                VC(S, dve, "lsum", u)
                S.step("dve", dve.reciprocal(lrec[:], lsum[:]), f"lrec_{u}")
                VC(S, dve, "lrec", u)
                S.step("dve", dve.tensor_tensor(out=xe[k][:, :, D:D + NE], in0=lex[:], in1=each(lrec), op=ALU.mult),
                       f"sc_{u}")
                VC(S, dve, "sc", u)
                S.step("dve", dve.tensor_tensor(out=sbx[:, :, 0:NE], in0=xe[k][:, :, D:D + NE],
                                                in1=gb[:].unsqueeze(1).to_broadcast([P, CT, NE]), op=ALU.add),
                       f"sb_{u}")
                VC(S, dve, "sb", u, alone=True)
                for j in range(CT):
                    ins = dve.max(out=m8[:, j], in_=sbx[:, j])
                S.step("dve", ins, f"m8_{u}")
                VC(S, dve, "m8", u)
                S.step("dve", dve.memset(m8[:, :, TOPK:8], NEG), f"m6_{u}")
                VC(S, dve, "m6", u, alone=True)
                for j in range(CT):
                    ins = dve.match_replace(out=mr[:, j], in_to_replace=m8[:, j], in_values=sbx[:, j],
                                            imm_value=-NEG)
                S.step("dve", ins, f"mr_{u}")
                VC(S, dve, "mr", u)
                VC(S, dve, "pos", u, 1)
                S.step("dve", dve.tensor_scalar(mkf[:], mr[:, :, 0:NE], -NEG, None, ALU.is_ge), f"mkf_{u}")
                VC(S, dve, "mkf", u)
                S.step("dve", dve.tensor_copy(mk[:], mkf[:]), f"mk_{u}")

            def positions(S, u, k):
                S.step("dve", dve.tensor_copy(maccb[:], macc[:]), f"mb_{u}")
                VC(S, pe, "mk", u)
                VC(S, pe, "mb", u)
                VC(S, pe, "lsub", u)
                for j in range(CT):
                    o = p_l[:, j * NE:(j + 1) * NE]
                    pe.matmul(o, tri[:], mk[:, j], start=True, stop=False)
                    for i in range(j):
                        pe.matmul(o, onesb[:], mk[:, i], start=False, stop=False)
                    ins = pe.matmul(o, onesb[:], maccb[:], start=False, stop=True)
                S.step("pe", ins, f"pos_{u}")
                VC(S, dve, "mb", u)
                S.step("dve", dve.tensor_reduce(msum[:], mkf[:].rearrange("p j e -> p e j"), AX.X, ALU.add),
                       f"ms_{u}")
                VC(S, dve, "ms", u)
                S.step("dve", dve.tensor_tensor(out=macc[:], in0=macc[:], in1=msum[:], op=ALU.add), f"ma_{u}")
                pos = p_l[:, 0:CT * NE].rearrange("p (j e) -> p j e", j=CT)
                VC(S, dve, "pos", u)
                S.step("dve", dve.scalar_tensor_tensor(out=sv[:], in0=pos, scalar=float(CAP), in1=mkf[:],
                                                       op0=ALU.is_lt, op1=ALU.mult), f"sv_{u}")
                S.step("dve", dve.tensor_tensor(out=sl[:], in0=pos, in1=eb[:].unsqueeze(1).to_broadcast([P, CT, NE]),
                                                op=ALU.add), f"sl_{u}")
                VC(S, dve, "sl", u)
                VC(S, dve, "ma", u)
                S.step("dve", dve.tensor_tensor(out=sl[:], in0=sl[:], in1=sv[:], op=ALU.mult), f"sw_{u}")
                VC(S, dve, "sw", u, alone=True)
                for j in range(CT):
                    ins = dve.max(out=s8[:, j], in_=sl[:, j])
                S.step("dve", ins, f"s8_{u}")
                VC(S, dve, "s8", u)
                S.step("dve", dve.tensor_scalar(s8o[:], s8[:], 0.0, FAR, ALU.is_equal, ALU.mult), f"so_{u}")
                VC(S, dve, "so", u)
                VC(S, dve, "disp", u, 2)
                S.step("dve", dve.scalar_tensor_tensor(out=idx[k][:], in0=s8[:], scalar=-1.0, in1=s8o[:],
                                                       op0=ALU.add, op1=ALU.add), f"idx_{u}")
                VC(S, dve, "tk", u, 1)
                S.step("dve", dve.tensor_copy(xe[k][:, :, D + NE:EXT], tok[:].unsqueeze(2)), f"tw_{u}")
                VC(S, dve, "tw", u)
                S.step("dve", dve.tensor_scalar(tok[:], tok[:], float(CH), None, ALU.add), f"tk_{u}")
                VC(S, pool, "idx", u)
                VC(S, pool, "tw", u)
                for j in range(CT):
                    for m in range(TOPK):
                        S.load(pool.indirect_dma_start(
                            out=xb_d, out_offset=bass.IndirectOffsetOnAxis(ap=idx[k][:, j, m:m + 1], axis=0),
                            in_=xe[k][:, j], in_offset=None, bounds_check=NE * CAP - 1, oob_is_err=False),
                            f"disp_{u}", soft=True)

            def shared(S, u, j):
                n, o = BS[j], j * P
                for q in range(2):
                    if q == 0 and j == 0:
                        VC(S, pe, f"sh{NJS - 1}", u, 1)
                    elif q == 0:
                        VC(S, pe, f"sh{j - 1}", u)
                    for f in range(DH):
                        ins = pe.matmul(p_h[q][0:n, :], ws13[:, f, q, o:o + n], xT[:, f, :], start=(f == 0),
                                        stop=(f == DH - 1))
                S.step("pe", ins, f"sp{j}_{u}")
                VC(S, act, f"sp{j}", u)
                if j == 0:
                    VC(S, act, f"sh{NJS - 1}", u, 1)
                else:
                    VC(S, act, f"sh{j - 1}", u)
                S.step("act", act.activation(sg[0][0:n, :], p_h[0][0:n, :], ACT.Silu), f"sg{j}_{u}")
                VC(S, dve, f"sg{j}", u)
                if j == 0:
                    VC(S, dve, "z", u, 1)
                S.step("dve", dve.tensor_tensor(out=sh[0:n, j], in0=p_h[1][0:n, :], in1=sg[0][0:n, :],
                                                op=ALU.mult), f"sh{j}_{u}")

            def shared_out(S, u, c):
                VC(S, pe, f"sh{NJS - 1}", u)
                VC(S, pe, "xT", u)
                for j in range(CT):
                    for i in range(NJS):
                        ins = pe.matmul(p_tr[:, j * D:(j + 1) * D], sh[0:BS[i], i, j * P:(j + 1) * P],
                                        ws2[0:BS[i], i, :], start=(i == 0), stop=(i == NJS - 1))
                S.step("pe", ins, f"z_{u}")
                VC(S, act, "z", u)
                VC(S, act, "sz", u, 1)
                S.step("act", act.activation(zs[:].rearrange("p j d -> p (j d)"), p_tr[:], ACT.Copy), f"zs_{u}")
                VC(S, sp, "zs", u)
                S.load(sp.dma_start(tiles(y_d[bass.ds(c * CH + 1, CH), :]), zs[:]), f"sz_{u}")

            S = Steps(nc, top, book, gate, "route_first", lenient=True)
            S.begin(0)
            w = "weights"
            S.load(sp.dma_start(y_d[0:1, :], zrow[0:1, :]), "zero")
            for o, a, b in ((0, "L1_attn_Wk", "L1_attn_bk"), (D, "L1_attn_Wv", "L1_attn_bv")):
                S.load(sp.dma_start(w_kv[:, :, o:o + D], A[a].rearrange("(c p) n -> p c n", p=P)), w)
                S.load(sp.dma_start(b_kv[:, o:o + D], A[b].unsqueeze(0)), w)
            S.load(sp.dma_start(w_g[:], A["L1_ffn_gate_w"].rearrange("(c p) n -> p c n", p=P)), w)
            S.load(sp.dma_start(gb[:], A["L1_ffn_gate_b"].unsqueeze(0).to_broadcast([P, NE])), w)
            for q, a in enumerate(("L1_ffn_ws1", "L1_ffn_ws3")):
                S.load(sp.dma_start(ws13[:, :, q, :], A[a].rearrange("(c p) n -> p c n", p=P)), w)
            for j in range(NJS):
                S.load(sp.dma_start(ws2[0:BS[j], j, :], A["L1_ffn_ws2"][j * P:j * P + BS[j], :]), w)
            S.load(sp.dma_start(kvm[:], A["c_blocks"]), w)
            S.step("pool", pool.memset(ones[:], 1.0), "ones")
            S.step("pool", pool.memset(onesb[:], 1.0), "onesb")
            S.step("pool", pool.memset(macc[:], 0.0), "macc")
            S.step("pool", pool.memset(sbx[:], NEG), "sbx")
            S.wait(pool, "onesb")
            S.step("pool", pool.affine_select(out=tri[:], in_=onesb[:], compare_op=ALU.is_gt, fill=0.0, base=0,
                                              pattern=[[1, P]], channel_multiplier=-1), "tri")
            S.step("pool", pool.iota(idx[0][:, :, 0:1], [[P, CT]], base=1, channel_multiplier=1), "toki")
            S.step("pool", pool.iota(idx[1][:].rearrange("p j e -> p (j e)"), [[CAP, 32]], base=1,
                                     channel_multiplier=0), "ebi")
            S.wait(dve, "ebi")
            S.step("dve", dve.tensor_copy(tok[:], idx[0][:, :, 0]), "tok")
            S.step("dve", dve.tensor_copy(eb[:, 0:32], idx[1][:].rearrange("p j e -> p (j e)")), "eb0")
            S.step("dve", dve.tensor_scalar(eb[:, 32:64], idx[1][:].rearrange("p j e -> p (j e)"), float(32 * CAP),
                                            None, ALU.add), "eb1")
            load_mix(S, CPB - 2, 0)
            S.load(sp.dma_start(cs[:], A["c_rope"][0:CH, :].rearrange("(j p) (a d) -> p j a d", p=P, a=2)), "cs0")
            front(S, CPB - 1, 0, 0)
            turn(S, CPB - 1, 0)
            S.wait(sp, f"sx1_{CPB - 1}")
            S.wait(sp, f"ln_{CPB - 1}")
            load_mix(S, CPB - 1, 1)
            S.close()
            S.done(1)

            S = Steps(nc, top, book, gate, "route", scrap=(scrap[0:4, :], zrow[0:1, :]))
            with nc.Fori(0, B) as i:
                S.begin(i)
                for u in range(CPB):
                    c, k = i * CPB + u, u % 2
                    VC(S, sp, "krs", u, 1)
                    S.load(sp.dma_start(cs[:], A["c_rope"][u * CH:(u + 1) * CH, :].rearrange(
                        "(j p) (a d) -> p j a d", p=P, a=2)), f"cs_{u}")
                    gate_scores(S, u, k)
                    choose(S, u, k)
                    front(S, u, (u + 1) % 2, (c + 1) % NC)
                    VC(S, sp, "sx1", u)
                    VC(S, sp, "ln", u)
                    load_mix(S, u, (c + 2) % NC)
                    keys(S, u)
                    shared(S, u, 0)
                    positions(S, u, k)
                    shared(S, u, 1)
                    key_sums(S, u)
                    shared(S, u, 2)
                    turn(S, u, (u + 1) % 2)
                    shared_out(S, u, c)
                    if u == CPB - 1:
                        VC(S, sp, "kvst", u)
                        S.load(sp.dma_start(kv_d[bass.ds(i * P, P), :], kvs[:]), f"kvo_{u}")
                S.close()
            S.done(B)

        with ExitStack() as ctx:
            route(ctx)

        def experts(ctx):
            EB, U, AHEAD = EI // 2, 8, 4
            xs_ = [sb(ctx, f"ex{k}", [P, EXT]) for k in range(U)]
            wt = [sb(ctx, f"ewt{k}", [P, 1]) for k in range(U)]
            w13 = [sb(ctx, f"ew13{k}", [P, DH, 2, EI]) for k in range(U)]
            w2 = [sb(ctx, f"ew2{k}", [EB, 2, D]) for k in range(U)]
            xT = [sb(ctx, f"exT{k}", [P, DH, P]) for k in range(2)]
            sg = [sb(ctx, f"esg{k}", [EB, 2, P]) for k in range(2)]
            hd = [sb(ctx, f"ehd{k}", [EB, 2, P]) for k in range(2)]
            yb = [sb(ctx, f"eyb{k}", [P, D]) for k in range(U)]
            far = [sb(ctx, f"efar{k}", [P, 1]) for k in range(U)]
            idx = [sb(ctx, f"eidx{k}", [P, 1], I32) for k in range(U)]
            p_t = [ps(ctx, f"ep_t{k}", 512) for k in range(2)]
            p_g = [ps(ctx, f"ep_g{k}", 512) for k in range(2)]
            p_u = [ps(ctx, f"ep_u{k}", 512) for k in range(2)]
            p_y = [ps(ctx, f"ep_y{k}", 512) for k in range(2)]

            def W(eng, name, k, ago=0, alone=False):
                v = k - ago
                S.wait(eng, f"{name}{v % U}", back=1 if v < 0 else 0, alone=alone)

            def loaded(k):
                return U if k < AHEAD else 0

            def load(S, e, k, ago):
                W(sp, "yb", k, ago)
                W(sp, "idx", k, ago)
                S.load(sp.dma_start(xs_[k][:], xb_d[bass.ds(e * CAP, CAP), :]), f"x{k}")
                S.load(sp.dma_start(w13[k][:, :, 0, :], w1f[bass.ds(e * D, D), :].rearrange("(c p) i -> p c i", p=P)),
                       f"w{k}")
                S.load(sp.dma_start(w13[k][:, :, 1, :], w3f[bass.ds(e * D, D), :].rearrange("(c p) i -> p c i", p=P)),
                       f"w{k}")
                S.load(sp.dma_start(w2[k][:], w2f[bass.ds(e * EI, EI), :].rearrange("(c p) d -> p c d", p=EB)),
                       f"w{k}")
                S.load(sp.dma_start(wt[k][:], xb_d[bass.ds(e * CAP, CAP), bass.ds(e + D, 1)],
                                    allow_slow_non_contiguous=True), f"wt{k}")

            w1f, w3f = (A[n].rearrange("e d i -> (e d) i") for n in ("L1_ffn_w1", "L1_ffn_w3"))
            w2f = A["L1_ffn_w2"].rearrange("e i d -> (e i) d")

            S = Steps(nc, top, book, gate, "experts_first", lenient=True)
            S.begin(0)
            for k in range(AHEAD):
                load(S, k, k, 0)
            S.close()
            S.done(1)

            S = Steps(nc, top, book, gate, "experts", scrap=(scrap[4:12, :], zrow[0:1, :]))
            with nc.Fori(0, NE // U) as i:
                S.begin(i)
                for m in range(0, U, 2):
                    for k in (m, m + 1):
                        load(S, (i * U + k + AHEAD) % NE, (k + AHEAD) % U, U if k + AHEAD < U else 0)
                    for k in (m, m + 1):
                        W(pe, "x", k, loaded(k))
                        W(pe, "xT", k, 2)
                        for f in range(DH):
                            ins = pe.transpose(p_t[k % 2][:, f * P:(f + 1) * P], xs_[k][:, f * P:(f + 1) * P], ident[:])
                        S.step("pe", ins, f"tr{k}")
                        W(act, "tr", k)
                        W(act, "up", k, 2)
                        S.step("act", act.activation(xT[k % 2][:].rearrange("p f t -> p (f t)"), p_t[k % 2][:, 0:D], ACT.Copy),
                               f"xT{k}")
                        W(dve, "x", k, loaded(k))
                        W(dve, "add", k, U)
                        S.step("dve", dve.tensor_scalar(far[k][:], xs_[k][:, D + NE:EXT], 0.0, FAR, ALU.is_equal, ALU.mult),
                               f"far{k}")
                        W(dve, "far", k)
                        S.step("dve", dve.tensor_tensor(out=idx[k][:], in0=xs_[k][:, D + NE:EXT], in1=far[k][:],
                                                        op=ALU.add), f"idx{k}")
                    for k in (m, m + 1):
                        W(pe, "xT", k)
                        W(pe, "w", k, loaded(k))
                        W(pe, "hd", k, 2)
                        for q, dst in ((0, p_g[k % 2]), (1, p_u[k % 2])):
                            for b in range(2):
                                for f in range(DH):
                                    ins = pe.matmul(dst[0:EB, b * P:(b + 1) * P], w13[k][:, f, q, b * EB:(b + 1) * EB],
                                                    xT[k % 2][:, f, :], start=(f == 0), stop=(f == DH - 1))
                        S.step("pe", ins, f"up{k}")
                        W(act, "up", k)
                        W(act, "hd", k, 2)
                        S.step("act", act.activation(sg[k % 2][:].rearrange("p b t -> p (b t)"), p_g[k % 2][0:EB, 0:2 * P],
                                                     ACT.Silu), f"sg{k}")
                        W(dve, "sg", k)
                        W(dve, "dn", k, 2)
                        S.step("dve", dve.tensor_tensor(out=hd[k % 2][:].rearrange("p b t -> p (b t)"),
                                                        in0=p_u[k % 2][0:EB, 0:2 * P],
                                                        in1=sg[k % 2][:].rearrange("p b t -> p (b t)"), op=ALU.mult), f"hd{k}")
                    for k in (m, m + 1):
                        W(pe, "hd", k)
                        W(pe, "yb", k, 2)
                        for b in range(2):
                            ins = pe.matmul(p_y[k % 2][:, 0:D], hd[k % 2][:, b, :], w2[k][:, b, :], start=(b == 0), stop=(b == 1))
                        S.step("pe", ins, f"dn{k}")
                        W(dve, "dn", k)
                        W(dve, "wt", k, loaded(k))
                        W(dve, "add", k, U)
                        S.step("dve", dve.tensor_scalar(yb[k][:], p_y[k % 2][:, 0:D], wt[k][:], None, ALU.mult), f"yb{k}")
                        W(pool, "yb", k)
                        W(pool, "idx", k)
                        W(pool, "add", k, 1)
                        S.load(pool.indirect_dma_start(out=y_d, out_offset=bass.IndirectOffsetOnAxis(ap=idx[k][:], axis=0),
                                                       in_=yb[k][:], in_offset=None, bounds_check=T, oob_is_err=False,
                                                       compute_op=ALU.add), f"add{k}", soft=True)
                S.close()
            S.done(NE // U)

        with ExitStack() as ctx:
            experts(ctx)

        def final(ctx):
            xn = [sb(ctx, f"fxn{k}", [P, CT, D]) for k in range(CPB)]
            x1 = [sb(ctx, f"fx1{k}", [P, CT, D]) for k in range(CPB)]
            ym = [sb(ctx, f"fym{k}", [P, CT, D]) for k in range(CPB)]
            cs = [sb(ctx, f"fcs{k}", [P, CT, 2, D]) for k in range(2)]
            kv = sb(ctx, "fkv", [P, 2 * D])
            xT = sb(ctx, "fxT", [P, DH, CH])
            w_q = sb(ctx, "w_q", [P, DH, D])
            b_q = sb(ctx, "b_q", [1, D])
            ones = sb(ctx, "fones", [1, P])
            gam, bet = sb(ctx, "gam", [P, D]), sb(ctx, "bet", [P, D])
            qg = [sb(ctx, f"qg{k}", [P, CT, D]) for k in range(2)]
            qr = [sb(ctx, f"qr{k}", [P, CT, D]) for k in range(2)]
            qt = sb(ctx, "qt", [P, CT, D])
            qrT = sb(ctx, "qrT", [P, DH, CH])
            zt = sb(ctx, "zt", [P, CT, D])
            zz = sb(ctx, "zz", [P, CT * HA])
            rz = sb(ctx, "rz", [P, CT * HA])
            o = sb(ctx, "fo", [P, CT, D])
            s1_ = [sb(ctx, f"fs1{k}", [P, CT, D]) for k in range(2)]
            st, mv, rs = sb(ctx, "fst", [P, CT, 6]), sb(ctx, "fmv", [P, CT, 2]), sb(ctx, "frs", [P, CT])
            p_tr = ps(ctx, "fp_tr", DH * CH)
            p_q = ps(ctx, "fp_q", CT * D)
            p_t2 = ps(ctx, "fp_t2", DH * CH)
            p_o = ps(ctx, "fp_o", CT * D)

            def loads(S, u, c):
                k, cc = (u + 2) % CPB, bass.ds(c * CH, CH)
                VC(S, sp, "fin", u, 2)
                S.load(sp.dma_start(xn[k][:], tiles(xn1_d[cc, :])), f"xn_{u}")
                VC(S, sp, "qrs", u, 1)
                S.load(sp.dma_start(cs[u % 2][:], A["c_rope"][k * CH:(k + 1) * CH, :].rearrange(
                    "(j p) (a d) -> p j a d", p=P, a=2)), f"cs_{u}")
                S.load(sp.dma_start(x1[k][:], tiles(x1_d[cc, :])), f"x1_{u}")
                S.load(sp.dma_start(ym[k][:], tiles(y_d[bass.ds(c * CH + 1, CH), :])), f"ym_{u}")

            def queries(S, u, k):
                b = (u + 1) % CPB
                VC(S, pe, "xn", u, 1)
                VC(S, pe, "xT", u, 1)
                for f in range(DH):
                    for j in range(CT):
                        ins = pe.transpose(p_tr[:, f * CH + j * P:f * CH + (j + 1) * P],
                                           xn[b][:, j, f * P:(f + 1) * P], ident[:])
                S.step("pe", ins, f"tr_{u}")
                VC(S, act, "tr", u)
                VC(S, act, "qp", u, 1)
                S.step("act", act.activation(xT[:].rearrange("p f t -> p (f t)"), p_tr[:], ACT.Copy), f"xT_{u}")
                VC(S, pe, "xT", u)
                VC(S, pe, "qg", u, 1)
                for j in range(CT):
                    dst = p_q[:, j * D:(j + 1) * D]
                    for f in range(DH):
                        pe.matmul(dst, xT[:, f, j * P:(j + 1) * P], w_q[:, f, :], start=(f == 0), stop=False)
                    ins = pe.matmul(dst, ones[0:1, :], b_q[:], start=False, stop=True)
                S.step("pe", ins, f"qp_{u}")
                VC(S, act, "qp", u)
                VC(S, act, "zt", u, 1)
                S.step("act", act.activation(qg[k][:].rearrange("p j d -> p (j d)"), p_q[:], ACT.Gelu), f"qg_{u}")
                VC(S, dve, "qg", u)
                S.step("dve", dve.tensor_scalar(qg[k][:], qg[k][:], KB, None, ALU.add), f"qa_{u}")
                VC(S, dve, "cs", u, 1)
                VC(S, dve, "qa", u)
                rope(S, u, qg[k][:], cs[k][:, :, 0], cs[k][:, :, 1], qr[k][:], qt[:], ("t2", "qr"), "qr")

            def attend(S, u, k, c):
                s1 = s1_[k]
                VC(S, pe, "qr", u, 1)
                VC(S, pe, "qrT", u, 1)
                for f in range(DH):
                    for j in range(CT):
                        ins = pe.transpose(p_t2[:, f * CH + j * P:f * CH + (j + 1) * P],
                                           qr[k][:, j, f * P:(f + 1) * P], ident[:])
                S.step("pe", ins, f"t2_{u}")
                VC(S, act, "t2", u)
                VC(S, act, "o", u, 1)
                S.step("act", act.activation(qrT[:].rearrange("p f t -> p (f t)"), p_t2[:], ACT.Copy), f"qrT_{u}")
                VC(S, pe, "qrT", u)
                if u == 0:
                    VC(S, pe, "kv", u)
                VC(S, pe, "os", u, 1)
                for j in range(CT):
                    for f in range(DH):
                        at = j * D + f * P
                        ins = pe.matmul(p_o[:, at:at + P], qrT[:, f, j * P:(j + 1) * P], kv[:, f * P:(f + 1) * P],
                                        start=True, stop=True)
                S.step("pe", ins, f"o_{u}")
                if u == 0:
                    VC(S, pool, "kv", u)
                VC(S, pool, "qa", u, 1)
                VC(S, pool, "zz", u, 1)
                S.step("pool", pool.tensor_tensor(out=zt[:], in0=qg[k][:],
                                                in1=kv[:, D:2 * D].unsqueeze(1).to_broadcast([P, CT, D]),
                                                op=ALU.mult), f"zt_{u}")
                VC(S, dve, "zt", u)
                S.step("dve", dve.tensor_reduce(zz[:], zt[:].rearrange("p j (h c) -> p (j h) c", c=DA), AX.X, ALU.add),
                       f"zz_{u}")
                VC(S, dve, "zz", u)
                S.step("dve", dve.tensor_scalar(zz[:], zz[:], 1e-6, None, ALU.add), f"ze_{u}")
                VC(S, dve, "ze", u)
                S.step("dve", dve.reciprocal(rz[:], zz[:]), f"rz_{u}")
                VC(S, dve, "rz", u)
                VC(S, dve, "o", u)
                S.step("dve", dve.tensor_tensor(out=o[:].rearrange("p j (h c) -> p (j h) c", c=DA),
                                                in0=p_o[:].rearrange("p (h c) -> p h c", c=DA),
                                                in1=rz[:].unsqueeze(2).to_broadcast([P, CT * HA, DA]), op=ALU.mult),
                       f"os_{u}")
                VC(S, dve, "os", u)
                VC(S, dve, "xn", u, 2)
                S.step("dve", dve.tensor_tensor(out=o[:], in0=o[:], in1=xn[u][:], op=ALU.add), f"re_{u}")
                VC(S, act, "ym", u, 2)
                S.step("act", act.activation(ym[u][:], ym[u][:], ACT.Silu), f"sy_{u}")
                VC(S, dve, "re", u)
                layer_norm(S, u, o, st, mv, rs, 1e-12, s1, (("out", 2),), "ln")
                VC(S, dve, "ln", u)
                S.step("dve", dve.tensor_tensor(out=s1[:], in0=s1[:], in1=gam[:].unsqueeze(1).to_broadcast([P, CT, D]),
                                                  op=ALU.mult), f"ga_{u}")
                VC(S, dve, "ga", u)
                S.step("dve", dve.tensor_tensor(out=s1[:], in0=s1[:], in1=bet[:].unsqueeze(1).to_broadcast([P, CT, D]),
                                                  op=ALU.add), f"be_{u}")
                VC(S, dve, "be", u)
                VC(S, dve, "sy", u)
                S.step("dve", dve.tensor_tensor(out=s1[:], in0=s1[:], in1=ym[u][:], op=ALU.mult), f"sy1_{u}")
                VC(S, pool, "sy1", u)
                VC(S, pool, "x1", u, 2)
                S.step("pool", pool.tensor_tensor(out=s1[:], in0=s1[:], in1=x1[u][:], op=ALU.add), f"fin_{u}")
                VC(S, sp, "fin", u)
                S.load(sp.dma_start(tiles(out_rows[bass.ds(c * CH, CH), :]), s1[:]), f"out_{u}")

            S = Steps(nc, top, book, gate, "final_first", lenient=True)
            S.begin(0)
            w = "weights"
            S.load(sp.dma_start(w_q[:], A["L1_attn_Wq"].rearrange("(c p) n -> p c n", p=P)), w)
            S.load(sp.dma_start(b_q[:], A["L1_attn_bq"].unsqueeze(0)), w)
            S.load(sp.dma_start(gam[:], A["L1_attn_gamma"].unsqueeze(0).to_broadcast([P, D])), w)
            S.load(sp.dma_start(bet[:], A["L1_attn_beta"].unsqueeze(0).to_broadcast([P, D])), w)
            S.step("dve", dve.memset(ones[:], 1.0), "ones")
            S.wait(pe, w)
            S.wait(pe, "ones")
            loads(S, CPB - 2, 0)
            loads(S, CPB - 1, 1)
            queries(S, CPB - 1, 0)
            S.close()
            S.done(1)
            S = Steps(nc, top, book, gate, "final")
            with nc.Fori(0, B) as i:
                S.begin(i)
                for u in range(CPB):
                    c, k = i * CPB + u, u % 2
                    if u == 0:
                        VC(S, sp, "zt", u, 1)
                        VC(S, sp, "o", u, 1)
                        S.load(sp.dma_start(kv[:], kv_d[bass.ds(i * P, P), :]), "kv_0")
                    loads(S, u, (c + 2) % NC)
                    queries(S, u, (u + 1) % 2)
                    attend(S, u, k, c)
                S.close()
            S.done(B)

        with ExitStack() as ctx:
            final(ctx)


def _constants():
    half = np.arange(0, DK, 2, dtype=np.float32)
    inv = (1.0 / 10000.0 ** (half / DK)).astype(np.float32)
    t = np.arange(L, dtype=np.float32)
    f = (t[:, None] * inv[None, :]).astype(np.float32)
    f = np.concatenate([f, f], axis=-1)
    base = ((half + np.float32(0.4 * DK)) / np.float32(1.4 * DK)).astype(np.float32)
    scale = base[None, :] ** ((t - L // 2) / np.float32(P // 2)).astype(np.float32)[:, None]
    scale = np.concatenate([scale, scale], axis=-1)
    cos, sin = np.cos(f), np.sin(f)
    sgn = np.concatenate([-np.ones(DK // 2), np.ones(DK // 2)])
    tab = np.concatenate([cos * scale, sgn * sin * scale, cos / scale, sgn * sin / scale], axis=-1)
    a, c = np.arange(P)[:, None], np.arange(P)[None, :]
    mask = np.zeros((WPB, P, 2 * P), np.float32)
    mask[:, :, 0:P] = np.where(c >= a, 0.0, NEG)
    mask[0, :, 0:P] = NEG
    mask[:, :, P:] = np.where(c <= a, 0.0, NEG)
    sel = np.broadcast_to((np.arange(96)[:, None] % 32 == np.arange(32)[None, :])[:, :, None], (96, 32, P))
    inv = (1.0 / 10000.0 ** (np.arange(0, D, 2, dtype=np.float32) / D)).astype(np.float32)
    ang = np.repeat((t[:, None] * inv).astype(np.float32), 2, axis=1)
    rope = np.concatenate([np.cos(ang), np.sin(ang) * np.tile([-1.0, 1.0], D // 2)], axis=1)
    blocks = (np.arange(P)[:, None] // 16 == np.arange(P)[None, :] // 16) / float(L)
    return {"c_rope": rope.astype(np.float32), "c_blocks": blocks.astype(np.float32), "c_select": sel.astype(mybir.dt.np(BF16)),
            "c_rotary": tab.astype(np.float32).reshape(WPB, P, 4 * DK),
            "c_mask": mask.astype(mybir.dt.np(BF16))}


def kernel(**inputs):
    import concourse.bacc as bacc
    from concourse.bass_utils import run_bass_kernel_spmd

    arrays = dict(inputs)
    for name in TRANSPOSED:
        arrays[name] = np.swapaxes(np.asarray(arrays[name]), -1, -2)
    arrays.update(_constants())
    arrays = {k: np.ascontiguousarray(v) for k, v in arrays.items()}

    book = {}
    for _ in range(2):
        nc = bacc.Bacc("TRN2", target_bir_lowering=False, num_devices=1)
        A = {k: nc.dram_tensor(f"in_{k}", v.shape, mybir.dt.from_np(v.dtype), kind="ExternalInput").ap()
             for k, v in arrays.items()}
        out = nc.dram_tensor("out_0", (B, L, D), F32, kind="ExternalOutput").ap()
        program(nc, A, out, book)
    r = run_bass_kernel_spmd(nc, [{f"in_{k}": v for k, v in arrays.items()}], core_ids=[0])
    return r.results[0]["out_0"]
```
